# Optimizing a Trainium2 kernel written in Bass

```python
import numpy as np
import jax
import jax.numpy as jnp

def _softmax(x, axis=-1):
    return jax.nn.softmax(x, axis=axis)

def _gelu(x):
    return jax.nn.gelu(x, approximate=True)

def _silu(x):
    return jax.nn.silu(x)

def _sigmoid(x):
    return jax.nn.sigmoid(x)

def _layernorm(x, axis=-1, eps=1e-05):
    m = jnp.mean(x, axis=axis, keepdims=True)
    v = jnp.var(x, axis=axis, keepdims=True)
    return (x - m) / jnp.sqrt(v + eps)

def _scatter_add(tgt, idx, src, axis=0):
    return tgt.at[idx].add(src)

def _segment_sum(src, seg, n):
    return jax.ops.segment_sum(src, seg, n)
kernel_name = 'mk_seq_preln_d1_jaxref_r8_e8cc2a'

def setup_inputs(seed: int=0):
    np.random.seed(seed)
    _w = jnp.asarray

    def _L0_attn_setup():
        import jax, jax.numpy as jnp
        import numpy as np
        EPS = 1.1920929e-07

        def _rms(x):
            return x * jax.lax.rsqrt(jnp.mean(x * x, axis=-1, keepdims=True) + EPS)
        key = jax.random.key(seed)
        k0, k1, k2, k3 = jax.random.split(key, 4)
        B, S, D, DFF = (4, 256, 256, 1024)
        x = jax.random.normal(k0, (B, S, D), dtype=jnp.float32)
        w_qkv = jax.random.normal(k1, (3 * D, D), dtype=jnp.float32) * 0.02
        w_swiglu = jax.random.normal(k2, (2 * DFF, D), dtype=jnp.float32) * 0.02
        w_out = jax.random.normal(k3, (D, DFF), dtype=jnp.float32) * 0.02
        return {'x': x, 'w_qkv': w_qkv, 'w_swiglu': w_swiglu, 'w_out': w_out}
    _L0_attn_in = _L0_attn_setup()

    def _L0_ffn_setup():
        import jax, jax.numpy as jnp
        import numpy as np
        B, S, H = (4, 128, 256)
        E, K, I, SI = (16, 4, 176, 704)

        def _silu_mul(gu, inter):
            return jax.nn.silu(gu[:, :inter]) * gu[:, inter:]
        key = jax.random.key(seed)
        ks = jax.random.split(key, 7)
        s = 0.02
        return {'hidden_states': jax.random.normal(ks[0], (B, S, H), jnp.float32), 'gate_w': jax.random.normal(ks[1], (E, H), jnp.float32) * s, 'expert_gate_up': jax.random.normal(ks[2], (E, 2 * I, H), jnp.float32) * s, 'expert_down': jax.random.normal(ks[3], (E, H, I), jnp.float32) * s, 'shared_gate_up': jax.random.normal(ks[4], (2 * SI, H), jnp.float32) * s, 'shared_down': jax.random.normal(ks[5], (H, SI), jnp.float32) * s, 'shared_gate_vec': jax.random.normal(ks[6], (1, H), jnp.float32) * s}
    _L0_ffn_in = _L0_ffn_setup()
    _d = {'L0_attn_x': _L0_attn_in['x'], 'L0_attn_w_qkv': _L0_attn_in['w_qkv'], 'L0_attn_w_swiglu': _L0_attn_in['w_swiglu'], 'L0_attn_w_out': _L0_attn_in['w_out'], 'L0_ffn_gate_w': _L0_ffn_in['gate_w'], 'L0_ffn_expert_gate_up': _L0_ffn_in['expert_gate_up'], 'L0_ffn_expert_down': _L0_ffn_in['expert_down'], 'L0_ffn_shared_gate_up': _L0_ffn_in['shared_gate_up'], 'L0_ffn_shared_down': _L0_ffn_in['shared_down'], 'L0_ffn_shared_gate_vec': _L0_ffn_in['shared_gate_vec']}
    _x0 = _d['L0_attn_x']
    _d['L0_attn_x'] = jax.random.normal(jax.random.fold_in(jax.random.key(seed), 1), (2, 2048, 256), dtype=_x0.dtype)
    del _x0
    return _d

def reference(L0_attn_x, L0_attn_w_qkv, L0_attn_w_swiglu, L0_attn_w_out, L0_ffn_gate_w, L0_ffn_expert_gate_up, L0_ffn_expert_down, L0_ffn_shared_gate_up, L0_ffn_shared_down, L0_ffn_shared_gate_vec):

    def _L0_attn_ref(x, w_qkv, w_swiglu, w_out):
        import jax, jax.numpy as jnp
        import numpy as np
        EPS = 1.1920929e-07

        def _rms(x):
            return x * jax.lax.rsqrt(jnp.mean(x * x, axis=-1, keepdims=True) + EPS)
        qkv = _rms(x) @ w_qkv.T
        q, k, v = jnp.split(qkv, 3, axis=-1)
        q = _rms(q)
        k = _rms(k)
        w = jnp.exp(k)
        kv_cum = jnp.cumsum(w * v, axis=1)
        w_cum = jnp.cumsum(w, axis=1)
        y = jax.nn.sigmoid(q) * (kv_cum / (w_cum + 1e-06))
        uv = y @ w_swiglu.T
        u, g = jnp.split(uv, 2, axis=-1)
        return x + u * jax.nn.silu(g) @ w_out.T

    def _L0_ffn_ref(hidden_states, gate_w, expert_gate_up, expert_down, shared_gate_up, shared_down, shared_gate_vec):
        import jax, jax.numpy as jnp
        import numpy as np
        B, S, H = (4, 128, 256)
        E, K, I, SI = (16, 4, 176, 704)

        def _silu_mul(gu, inter):
            return jax.nn.silu(gu[:, :inter]) * gu[:, inter:]
        orig_shape = hidden_states.shape
        x = hidden_states.reshape(-1, H)
        router_logits = x @ gate_w.T
        routing_probs = jax.nn.softmax(router_logits.astype(jnp.float32), axis=-1)
        topk_w, topk_idx = jax.lax.top_k(routing_probs, K)
        topk_w = topk_w / topk_w.sum(axis=-1, keepdims=True)
        topk_w = topk_w.astype(x.dtype)
        combine = (jax.nn.one_hot(topk_idx, E, dtype=x.dtype) * topk_w[..., None]).sum(1)
        shared = _silu_mul(x @ shared_gate_up.T, SI) @ shared_down.T
        shared = shared * jax.nn.sigmoid(x @ shared_gate_vec.T)

        def step(acc, ew):
            w_gu, w_d, cw = ew
            h = _silu_mul(x @ w_gu.T, I)
            return (acc + h @ w_d.T * cw[:, None], None)
        acc0 = jnp.zeros_like(x)
        sparse, _ = jax.lax.scan(step, acc0, (expert_gate_up, expert_down, combine.T))
        return (shared + sparse).reshape(orig_shape)
    x = L0_attn_x
    x = x + _L0_attn_ref(_layernorm(x, axis=-1), L0_attn_w_qkv, L0_attn_w_swiglu, L0_attn_w_out)
    x = x + _L0_ffn_ref(_layernorm(x, axis=-1), L0_ffn_gate_w, L0_ffn_expert_gate_up, L0_ffn_expert_down, L0_ffn_shared_gate_up, L0_ffn_shared_down, L0_ffn_shared_gate_vec)
    return x

_drawn_inputs = setup_inputs


def setup_inputs(seed=0):
    import zlib

    import numpy as np

    out = dict(_drawn_inputs(seed))
    spreads = {}
    factors = {'L0_attn_w_qkv': 8.0,
     'L0_attn_w_swiglu': 8.0,
     'L0_attn_w_out': 8.0,
     'L0_ffn_gate_w': 8.0,
     'L0_ffn_expert_gate_up': 8.0,
     'L0_ffn_expert_down': 8.0,
     'L0_ffn_shared_gate_up': 7.98,
     'L0_ffn_shared_down': 7.956,
     'L0_ffn_shared_gate_vec': 8.0}
    for name, (base, spread) in spreads.items():
        noise = np.random.default_rng([zlib.crc32(name.encode()), seed]).standard_normal(out[name].shape)
        drawn = base * np.exp(spread * noise) if base else spread * noise
        out[name] = jnp.asarray(drawn.astype(out[name].dtype))
    for name, factor in factors.items():
        out[name] = (out[name] * factor).astype(out[name].dtype)
    return out
```

```python
from contextlib import ExitStack

import concourse.bass as bass
from concourse import mybir

F32 = mybir.dt.float32
F32R = mybir.dt.float32r
BF16 = mybir.dt.bfloat16
U32 = mybir.dt.uint32
ALU = mybir.AluOpType
ACT = mybir.ActivationFunctionType
AX_X = mybir.AxisListType.X

P = 128
D = 256
KD = D // P
BATCH, SEQ = 2, 2048
TOKENS = BATCH * SEQ
CHUNK = 512
CHUNKS = TOKENS // CHUNK
TT = CHUNK // P
RUN = CHUNK // BATCH
FF = 1024
FT = FF // P
SI = 704
ST = -(-SI // P)
SIP = ST * P
E = 16
TOPK = 4
EI = 176
EH = EI // 2
EHP = 96
RW = 32
LN_EPS = 1e-5
RMS_EPS = 1.1920929e-07
DEN_EPS = 1e-6

QKV0 = 0
RT0 = QKV0 + KD * 3 * D
SW0 = RT0 + KD * RW
WO0 = SW0 + KD * 2 * FF
SG0 = WO0 + FT * D
SD0 = SG0 + KD * 2 * SIP
WCOLS = SD0 + ST * D
PIECES = [(QKV0, SW0), (SW0, SW0 + FF * 2), (SW0 + FF * 2, WO0), (WO0, SG0),
          (SG0, SG0 + SIP * 2), (SG0 + SIP * 2, SD0), (SD0, WCOLS)]
STAGE = 2048
STAGES = 4

ROWS = TOKENS // P
LISTS = TOKENS * TOPK // P + E
PICKED = TOKENS * TOPK
UNROLL = 4
LEAD = 3
WSTAGES = 3
assert LISTS % UNROLL == 0
KINDS = ["pre", "first", "steady", "tail", "last"]
STEADY = CHUNKS - 2


class Turn:

    def __init__(self, kind, t=0):
        self.kind, self.t = kind, t
        self.front = kind in ("first", "steady", "tail")
        self.shared = kind in ("steady", "tail", "last")
        self.next = kind in ("pre", "first", "steady")


class Signal:

    def __init__(self, sem, front=(), shared=(), nxt=(), order=None):
        self.sem = sem
        every = order or [*front, *shared, *nxt]
        self.events = {}
        for kind in KINDS:
            turn = Turn(kind)
            on = [*(front if turn.front else ()), *(shared if turn.shared else ()), *(nxt if turn.next else ())]
            self.events[kind] = [e for e in every if e in on]
        self.raised = {kind: 0 for kind in KINDS}

    def start(self, turn):
        n = {kind: len(self.events[kind]) for kind in KINDS}
        before = KINDS[:KINDS.index(turn.kind)]
        at = sum(n[k] * (STEADY if k == "steady" else 1) for k in before)
        return turn.t * n["steady"] + at if turn.kind == "steady" else at

    def did(self, turn, event):
        assert self.events[turn.kind][self.raised[turn.kind]] == event, (turn.kind, event, self.events[turn.kind])
        self.raised[turn.kind] += 1
        return self.sem, 1

    def at(self, turn, event):
        return self.sem, self.start(turn) + (self.events[turn.kind].index(event) + 1)

    def before(self, turn, event):
        was = {"first": ["pre"], "steady": ["first", "steady"], "tail": ["steady"], "last": ["tail"]}[turn.kind]
        after = {len(self.events[k]) - self.events[k].index(event) - 1 for k in was}
        assert len(after) == 1
        return self.sem, self.start(turn) - after.pop()

    def check(self):
        for kind in KINDS:
            assert self.raised[kind] == len(self.events[kind]), (kind, self.raised, self.events)


FILLS = (["k", "q", "v"], [f"G{f}" for f in range(ST)] + ["D0", "D1"], [f"S{f}" for f in range(FT)] + ["W0", "W1"])


def build(nc, x, w1, w_up, w_down, out, xn2_rows, acc, ids, picked):
    ctx = ExitStack()
    with ctx:
        def sb(name, shape, dt, where=ctx):
            return where.enter_context(nc.sbuf_tensor(name, shape, dt))

        def sem(name):
            return ctx.enter_context(nc.semaphore(name))

        ident = sb("ident", [P, P], F32)
        ones_r = sb("ones_r", [P, P], F32R)
        ones_b = sb("ones_b", [P, P], BF16)
        earlier = sb("earlier", [P, P], BF16)
        ones_row = sb("ones_row", [P, RUN], F32)
        notfirst = sb("notfirst", [P, TT * E], F32)
        power = sb("power", [P, TT], F32)
        eps_c = sb("eps_c", [P, 1], F32)
        logits_all = sb("logits_all", [P, CHUNKS, TT, E], F32)
        rank_all = sb("rank_all", [P, CHUNKS, TT, E], F32)
        filled = sb("filled", [P, E], F32)
        first_slot = sb("first_slot", [P, E], F32)
        list_start = sb("list_start", [P, ROWS], F32)
        quarter = sb("quarter", [P, 4], F32)
        in_quarter = sb("in_quarter", [P, 1], F32)
        list_no = sb("list_no", [P, LISTS], F32)
        spare = sb("spare", [P, LISTS], F32)
        share = sb("share", [P, TOKENS // P, TOPK], F32)

        dense = ExitStack()
        whi = sb("whi", [P, WCOLS], F32R, dense)
        wlo = sb("wlo", [P, WCOLS], F32R, dense)
        with ExitStack() as early:
            stage = sb("stage", [P, STAGES, STAGE], F32, early)
        hid_hi = sb("hid_hi", [P, FT, CHUNK], F32R, dense)
        hid_lo = sb("hid_lo", [P, FT, CHUNK], F32R, dense)
        feat_hi = sb("feat_hi", [P, KD, CHUNK], F32R, dense)
        feat_lo = sb("feat_lo", [P, KD, CHUNK], F32R, dense)
        y_hi = sb("y_hi", [P, KD, CHUNK], F32R, dense)
        y_lo = sb("y_lo", [P, KD, CHUNK], F32R, dense)
        xin = sb("xin", [P, TT, D], F32, dense)
        bnorm = sb("bnorm", [P, TT, D], F32, dense)
        rms = bnorm[:, :, :].rearrange("p t d -> p (t d)").rearrange("p (k n) -> p k n", k=KD)
        res = sb("res", [P, TT, D], F32, dense)
        x1 = sb("x1", [P, TT, D], F32, dense)
        xn2 = sb("xn2", [P, TT, D], F32, dense)
        ksb = sb("ksb", [P, KD, CHUNK], F32, dense)
        qsb = sb("qsb", [P, KD, CHUNK], F32, dense)
        vsb = sb("vsb", [P, KD, CHUNK], F32, dense)
        kvsum = sb("kvsum", [P, KD, CHUNK], F32, dense)
        wsum = sb("wsum", [P, KD, CHUNK], F32, dense)
        kvend = sb("kvend", [P, KD, BATCH], F32, dense)
        wend = sb("wend", [P, KD, BATCH], F32, dense)
        gate = sb("gate", [P, 2, CHUNK], F32, dense)
        hid = sb("hid", [P, 2, CHUNK], F32, dense)
        st1 = sb("st1", [P, TT, 6], F32, dense)
        mv1 = sb("mv1", [P, TT, 2], F32, dense)
        sc1 = sb("sc1", [P, 8, TT], F32, dense)
        st2 = sb("st2", [P, TT, 6], F32, dense)
        mv2 = sb("mv2", [P, TT, 2], F32, dense)
        sc2 = sb("sc2", [P, 4, TT], F32, dense)
        lgt = sb("lgt", [RW, CHUNK], F32, dense)
        lg = sb("lg", [P, TT, RW], F32, dense)
        top8 = sb("top8", [P, TT, 8], F32, dense)
        rt = sb("rt", [P, 12, TT * E], F32, dense)
        rsm = sb("rsm", [P, 4, TT], F32, dense)
        selb = sb("selb", [P, TT * E], BF16, dense)
        slot_f = sb("slot_f", [P, TT, TOPK], F32, dense)
        slot_u = sb("slot_u", [P, TT * TOPK], U32, dense)
        idval = sb("idval", [P, TT * TOPK], F32, dense)
        sig = sb("sig", [P, TT], F32, dense)
        dense.close()

        moe = ExitStack()
        up_hi = sb("up_hi", [P, E * KD * 2 * EI], F32R, moe)
        up_lo = sb("up_lo", [P, E * KD * 2 * EI], F32R, moe)
        dn_hi = sb("dn_hi", [EHP, E * 2 * D], F32R, moe)
        dn_lo = sb("dn_lo", [EHP, E * 2 * D], F32R, moe)
        wst = sb("wst", [P, WSTAGES, KD * 2 * EI + 2 * D], F32, moe)
        xg = sb("xg", [P, UNROLL, D], F32, moe)
        xt_hi = sb("xt_hi", [P, 2, D], F32R, moe)
        xt_lo = sb("xt_lo", [P, 2, D], F32R, moe)
        eg = sb("eg", [P, 2, EI], F32, moe)
        eh = sb("eh", [P, 2, EI], F32, moe)
        ht_hi = sb("ht_hi", [EHP, 2, D], F32R, moe)
        ht_lo = sb("ht_lo", [EHP, 2, D], F32R, moe)
        ysb = sb("ysb", [P, UNROLL, D], F32, moe)
        take_now = sb("take_now", [P, UNROLL], U32, moe)
        put_now = sb("put_now", [P, UNROLL], U32, moe)
        take = sb("take", [P, LISTS + UNROLL], U32, moe)
        put = sb("put", [P, LISTS], U32, moe)
        whose = sb("whose", [1, LISTS], mybir.dt.int32, moe)
        tab = sb("tab", [P, E * ROWS // P, P], F32, moe)
        pick = sb("pick", [P, E * ROWS // P, LISTS], F32, moe)
        ix = sb("ix", [P, 4, LISTS], F32, moe)
        em = sb("em", [P, 8, E], F32, moe)
        moe.close()
        TILES = TOKENS // P
        join = ExitStack()
        zin = sb("zin", [P, UNROLL, TOPK * D], F32, join)
        ain = sb("ain", [P, UNROLL, D], F32, join)
        sums = sb("sums", [P, UNROLL, D], F32, join)
        wk = sb("wk", [P, 2, TILES * E], F32, join)
        wm = sb("wm", [P, 3, TILES], F32, join)
        join.close()

        ring = ctx.enter_context(nc.psum_tensor("ring", [P, 3, 2, CHUNK], F32))
        scr = ctx.enter_context(nc.psum_tensor("scr", [P, 2, CHUNK], F32))

        front, shared = (FILLS[0] + FILLS[2]), FILLS[1]
        order = FILLS[0] + FILLS[1] + FILLS[2]
        pair_full = Signal(sem("pair_full"), front, shared, order=order)
        scr_full = Signal(sem("scr_full"), ["stat"], ["x", "logit", "logit_t", "count"], ["b"],
                          order=["x", "logit", "logit_t", "count", "stat", "b"])
        pair_done = Signal(sem("pair_done"), front, shared, order=order)
        feat_split = Signal(sem("feat_split"), (), ["x"], ["b"])
        norm1 = Signal(sem("norm1"), (), (), ["stats", "aggr", "ve", "u0", "u1", "ue", "scale", "b"])
        norm2 = Signal(sem("norm2"), ["stats", "aggr", "ve", "xn2"])
        mid = Signal(sem("mid"), ["ksum", "klo", "qsum", "qlo", "kr", "qr", "wv", "wsum", "wend", "kvsum", "kvend", "d",
                                  "rec", "y", "ylo"])
        routed = Signal(sem("routed"), (), ["lg", "keep", "top", "gt", "eq", "cgt", "need", "ceq", "ok", "tie", "sel", "selb",
                                            "rank", "rsel", "rkeep", "off0", "off1", "off2", "off3", "off4", "slot",
                                            *[f"{a}{k}" for k in range(TOPK) for a in ("m", "s")], "slotu", "id"])
        sig_done = Signal(sem("sig_done"), (), ["half"])
        hid_lo_v = Signal(sem("hid_lo_v"), (), [f"G{f}" for f in range(ST)])
        squares = Signal(sem("squares"), ["k", "q"])
        sq_hi = Signal(sem("sq_hi"), ["k", "q"])
        feat_top = Signal(sem("feat_top"), (), ["x"], ["b"])
        logit_out = Signal(sem("logit_out"), (), ["logit", "tanh"])
        rms_done = Signal(sem("rms_done"), ["lnk", "lnq", "k", "q", "w", "eq", "yhi"])
        hids = [f"G{f}" for f in range(ST)]
        hidf = [f"S{f}" for f in range(FT)]
        silu = Signal(sem("silu"), hidf, hids, order=hids + hidf)
        hid_top = Signal(sem("hid_top"), hidf, hids, order=hids + hidf)
        pows = Signal(sem("pows"), ["n2"], (), ["n1a", "n1b"], order=["n1a", "n1b", "n2"])
        resid = Signal(sem("resid"), (), (), ["rp", "nm", "res"])
        hid_lo_p = Signal(sem("hid_lo_p"), hidf)
        x_in = sem("x_in")
        xn2_out = sem("xn2_out")
        acc_out = sem("acc_out")
        id_out = sem("id_out")
        stage_in = [sem(f"stage_in{i}") for i in range(STAGES)]
        table_clear = sem("table_clear")
        whi_done = sem("whi_done")
        wlo_done = sem("wlo_done")
        consts = sem("consts")
        table_in = sem("table_in")
        lists = sem("lists")
        smalls = sem("smalls")
        lists_t = sem("lists_t")
        w_in = [sem(f"w_in{i}") for i in range(WSTAGES)]
        w_hi = sem("w_hi")
        w_lo = sem("w_lo")
        pad_rows = sem("pad_rows")
        got = [sem(f"got{i}") for i in range(UNROLL)]
        sent = [sem(f"sent{i}") for i in range(UNROLL)]
        take_set = sem("take_set")
        put_set = sem("put_set")
        xt_full = sem("xt_full")
        up_full = sem("up_full")
        ht_full = sem("ht_full")
        y_full = sem("y_full")
        xt_hi_done = sem("xt_hi_done")
        xt_lo_done = sem("xt_lo_done")
        silu_done = sem("silu_done")
        h_done = sem("h_done")
        ht_hi_done = sem("ht_hi_done")
        ht_lo_done = sem("ht_lo_done")
        y_done = sem("y_done")
        z_in = [sem(f"z_in{i}") for i in range(UNROLL)]
        o_out = [sem(f"o_out{i}") for i in range(UNROLL)]
        weights = sem("weights")
        expd = sem("expd")
        summed = sem("summed")
        dense_done = sem("dense_done")
        vconsts = sem("vconsts")

        def whi_c(c0, n):
            return whi[:, c0:c0 + n]

        def wlo_c(c0, n):
            return wlo[:, c0:c0 + n]

        def slot_of(turn, event):
            return ((2 if turn.kind == "first" else 0) + pair_full.events[turn.kind].index(event)) % 3

        def apart(eng, *waits):
            for _, n in waits:
                if not isinstance(n, int):
                    eng.compute_val(n)
            eng.wait_ge(consts, 1)
            for s, n in waits:
                eng.wait_ge(s, n)

        def expert_steps(eng, fn):
            for s in range(UNROLL):
                fn(s, s)
            with eng.Fori(0, LISTS // UNROLL - 1) as t:
                for u in range(UNROLL):
                    fn((t, u), u)
            for s in range(LISTS, LISTS + LEAD):
                fn(s, s % UNROLL)

        def num(s, c=0):
            return s + c if isinstance(s, int) else s[0] * UNROLL + (UNROLL + s[1] + c)

        def lap(s, u, back=0):
            if isinstance(s, int):
                return (s - back) // UNROLL + 1
            return s[0] + ((UNROLL + s[1] - back) // UNROLL + 1)

        def live(s, back):
            return 0 <= s - back < LISTS if isinstance(s, int) else True

        def steps(eng, fn, pre=True):
            if pre:
                fn(Turn("pre"))
            fn(Turn("first"))
            with eng.Fori(0, STEADY) as t:
                fn(Turn("steady", t))
            fn(Turn("tail"))
            fn(Turn("last"))

        block = ctx.enter_context(nc.Block())

        @block.sync
        def _(sp):
            sp.dma_start(xin[:, :, :], x[0:CHUNK, :].rearrange("(t p) d -> p t d", p=P)).then_inc(x_in, 16)
            for n, (a, b) in enumerate(PIECES):
                if n >= STAGES:
                    sp.wait_ge(whi_done, n - STAGES + 1)
                    sp.wait_ge(wlo_done, n - STAGES + 1)
                sp.dma_start(stage[:, n % STAGES, 0:b - a], w1[:, a:b]).then_inc(stage_in[n % STAGES], 16)

            def turn_(turn):
                c = {"first": 0, "steady": turn.t + 1, "tail": CHUNKS - 1, "last": CHUNKS}.get(turn.kind)
                if turn.front and turn.next:
                    sp.wait_ge(*resid.before(turn, "res"))
                    sp.dma_start(xin[:, :, :], x[bass.ds((c + 1) * CHUNK, CHUNK), :].rearrange("(t p) d -> p t d", p=P)
                                 ).then_inc(x_in, 16)
                if turn.shared:
                    sp.wait_ge(*pair_done.at(turn, "D1"))
                    sp.dma_start(acc[bass.ds((c - 1) * CHUNK, CHUNK), :].rearrange("(t p) d -> p t d", p=P),
                                 x1[:, :, :]).then_inc(acc_out, 16)
                if turn.front:
                    sp.wait_ge(*norm2.at(turn, "xn2"))
                    sp.dma_start(xn2_rows[bass.ds(c * CHUNK, CHUNK), :].rearrange("(t p) d -> p t d", p=P),
                                 xn2[:, :, :]).then_inc(xn2_out, 16)
            steps(sp, turn_)
            sp.wait_ge(acc_out, 16 * CHUNKS)
            sp.wait_ge(xn2_out, 16 * CHUNKS)
            sp.wait_ge(dense_done, 3)
            sp.wait_ge(id_out, CHUNKS * 16 * TT * TOPK)
            sp.dma_start(tab[:, :, :], ids.rearrange("(g p n) o -> p g (n o)", p=P, n=P)).then_inc(table_in, 16)
            nu = KD * 2 * EI
            for e in range(E):
                if e >= WSTAGES:
                    sp.wait_ge(w_lo, e - WSTAGES + 1)
                sp.dma_start(wst[:, e % WSTAGES, 0:nu], w_up[e, :, :]).then_inc(w_in[e % WSTAGES], 16)
                sp.dma_start(wst[0:EHP, e % WSTAGES, nu:nu + 2 * D], w_down[e, :, :]).then_inc(w_in[e % WSTAGES], 16)
            for i in range(UNROLL):
                sp.wait_ge(sent[i], 16 * (LISTS // UNROLL))

            def load(i, u):
                sp.dma_start(zin[:, u, :], picked[bass.ds(i * (P * TOPK), P * TOPK), :].rearrange("(p k) d -> p (k d)", k=TOPK)
                             ).then_inc(z_in[u], 16)
                sp.dma_start(ain[:, u, :], acc[bass.ds(i * P, P), :]).then_inc(z_in[u], 16)

            def store(i, u):
                sp.wait_ge(summed, i * TOPK + TOPK)
                sp.dma_start(out[bass.ds(i * P, P), :], sums[:, u, :]).then_inc(o_out[u], 16)
            for u in range(UNROLL):
                load(u, u)
            with sp.Fori(0, TILES // UNROLL - 1) as t:
                for u in range(UNROLL):
                    store(t * UNROLL + u, u)
                    load(t * UNROLL + (u + UNROLL), u)
            for u in range(UNROLL):
                store(TILES - UNROLL + u, u)
            for u in range(UNROLL):
                sp.wait_ge(o_out[u], 16 * (TILES // UNROLL))

        @block.tensor
        def _(pe):
            def three(out, lhs, rhs, first, last):
                pairs = [(0, 0), (0, 1), (1, 0)]
                for n, (a, b) in enumerate(pairs):
                    mm = pe.matmul(out, lhs[a], rhs[b], start=first and n == 0, stop=last and n == 2)
                return mm

            def bank_pair(turn, event):
                if turn.kind != "first" or pair_full.events["first"].index(event) >= 3:
                    s, v = pair_done.at(turn, event)
                    pe.wait_ge(s, v - 3)
                return slot_of(turn, event)

            def proj(turn, event, cols, width, rhi, rlo):
                s = bank_pair(turn, event)
                for h, c in enumerate(cols):
                    for k in range(KD):
                        mm = three(ring[:, s, h, :], (whi_c(c + k * width, P), wlo_c(c + k * width, P)),
                                   (rhi[:, k, :], rlo[:, k, :]), k == 0, k == KD - 1)
                mm.then_inc(*pair_full.did(turn, event))

            def down(turn, event, tiles, w0, n):
                s = bank_pair(turn, event)
                for h, t in enumerate(tiles):
                    for f in range(n):
                        mm = three(ring[:, s, h, 0:D], (hid_hi[:, f, t * P:(t + 1) * P], hid_lo[:, f, t * P:(t + 1) * P]),
                                   (whi_c(w0 + f * D, D), wlo_c(w0 + f * D, D)), f == 0, f == n - 1)
                mm.then_inc(*pair_full.did(turn, event))

            def turn_columns(turn, event, rows):
                for k in range(KD):
                    for t in range(TT):
                        mm = pe.transpose(scr[:, k, t * P:(t + 1) * P], rows[:, t, k * P:(k + 1) * P], ident[:, :])
                mm.then_inc(*scr_full.did(turn, event))

            pe.wait_ge(consts, 1)
            pe.wait_ge(vconsts, 1)

            def turn_(turn):
                def shared_up(f):
                    if f == 0:
                        pe.wait_ge(*feat_split.at(turn, "x"))
                    proj(turn, f"G{f}", (SG0 + SIP + f * P, SG0 + f * P), 2 * SIP, feat_hi, feat_lo)

                if turn.kind == "first":
                    pe.wait_ge(wlo_done, 1)
                if turn.front:
                    pe.wait_ge(*feat_split.before(turn, "b"))
                    for n, part in ((1, "k"), (0, "q"), (2, "v")):
                        proj(turn, part, (QKV0 + n * D, QKV0 + n * D + P), 3 * D, feat_hi, feat_lo)
                if turn.shared:
                    pe.wait_ge(*norm2.before(turn, "xn2"))
                    turn_columns(turn, "x", xn2)
                    pe.wait_ge(*feat_split.at(turn, "x"))
                    for k in range(KD):
                        mm = three(scr[0:RW, 0, :], (whi_c(RT0 + k * RW, RW), wlo_c(RT0 + k * RW, RW)),
                                   (feat_hi[:, k, :], feat_lo[:, k, :]), k == 0, k == KD - 1)
                    mm.then_inc(*scr_full.did(turn, "logit"))
                    shared_up(0)
                    apart(pe, logit_out.at(turn, "logit"))
                    for t in range(TT):
                        mm = pe.transpose(scr[:, 1, t * RW:(t + 1) * RW], lgt[:, t * P:(t + 1) * P], ident[0:RW, 0:RW])
                    mm.then_inc(*scr_full.did(turn, "logit_t"))
                    shared_up(1)
                    pe.wait_ge(*routed.at(turn, "selb"))
                    pe.matmul(scr[:, 1, 128:192], earlier[:, :], selb[:, :], start=True, stop=True)
                    pe.matmul(scr[:, 1, 192:256], ones_b[:, :], selb[:, :], start=True, stop=True
                              ).then_inc(*scr_full.did(turn, "count"))
                    shared_up(2)
                if turn.front:
                    if turn.shared:
                        pe.wait_ge(*routed.at(turn, "slot"))
                    pe.wait_ge(*mid.at(turn, "qlo"))
                    for h in range(2):
                        pe.matmul(scr[:, h, :], ones_r[:, :], y_hi[:, h, :], start=True, stop=False)
                        mm = pe.matmul(scr[:, h, :], ones_r[:, :], y_lo[:, h, :], start=False, stop=True)
                    mm.then_inc(*scr_full.did(turn, "stat"))
                if turn.shared:
                    for f in range(3, ST):
                        shared_up(f)
                    pe.wait_ge(*hid_lo_v.at(turn, f"G{ST - 1}"))
                    down(turn, "D0", (0, 1), SD0, ST)
                    down(turn, "D1", (2, 3), SD0, ST)
                if turn.front:
                    if turn.kind == "first":
                        pe.wait_ge(wlo_done, len(PIECES))
                    pe.wait_ge(*mid.at(turn, "ylo"))
                    for f in range(FT):
                        proj(turn, f"S{f}", (SW0 + f * P, SW0 + FF + f * P), 2 * FF, y_hi, y_lo)
                if turn.next:
                    pe.wait_ge(*norm1.at(turn, "b"))
                    if turn.front:
                        pe.wait_ge(*rms_done.at(turn, "lnq"))
                    turn_columns(turn, "b", bnorm)
                if turn.front:
                    pe.wait_ge(*hid_lo_p.at(turn, f"S{FT - 1}"))
                    down(turn, "W0", (0, 1), WO0, FT)
                    down(turn, "W1", (2, 3), WO0, FT)
            steps(pe, turn_)

            pe.wait_ge(table_in, 16)
            pe.wait_ge(lists, 8)
            groups = E * ROWS // P
            for g in range(groups):
                mm = pe.matmul(scr[:, 0, 0:LISTS], tab[:, g, :], pick[:, g, :], start=g == 0, stop=g == groups - 1)
            mm.then_inc(lists_t, 1)
            pe.wait_ge(lists, 14)
            pe.wait_ge(w_lo, E)
            pe.wait_ge(pad_rows, 2)

            def step(s, u):
                if live(s, 0):
                    b = u % 2
                    pe.wait_ge(got[u], lap(s, u) * 16)
                    if not isinstance(s, int) or s >= 2:
                        pe.wait_ge(xt_lo_done, num(s, -1))
                    for k in range(KD):
                        mm = pe.transpose(ring[:, 0, b, k * P:(k + 1) * P], xg[:, u, k * P:(k + 1) * P], ident[:, :])
                    mm.then_inc(xt_full, 1)
                if live(s, 1):
                    b = (u - 1) % 2
                    pe.wait_ge(consts, 1)
                    pe.wait_ge(xt_lo_done, num(s, 0))
                    if not isinstance(s, int) or s >= 3:
                        pe.wait_ge(h_done, num(s, -2))
                    e = pe.value_load(whose[0:1, bass.ds(num(s, -1), 1)], min_val=0, max_val=E - 1)
                    for k in range(KD):
                        lhs = (xt_hi[:, b, k * P:(k + 1) * P], xt_lo[:, b, k * P:(k + 1) * P])
                        at = e * (KD * 2 * EI) + k * 2 * EI
                        mm = three(ring[:, 1, b, 0:2 * EI], lhs, (up_hi[:, bass.ds(at, 2 * EI)], up_lo[:, bass.ds(at, 2 * EI)]),
                                   k == 0, k == KD - 1)
                    mm.then_inc(up_full, 1)
                if live(s, 2):
                    b = (u - 2) % 2
                    pe.wait_ge(h_done, num(s, -1))
                    if not isinstance(s, int) or s >= 4:
                        pe.wait_ge(ht_lo_done, num(s, -3))
                    for k in range(2):
                        mm = pe.transpose(ring[0:EH, 2, b, k * P:(k + 1) * P], eh[:, b, k * EH:(k + 1) * EH], ident[:, :])
                    mm.then_inc(ht_full, 1)
                if live(s, 3):
                    b = (u - 3) % 2
                    pe.wait_ge(consts, 1)
                    pe.wait_ge(ht_lo_done, num(s, -2))
                    if not isinstance(s, int) or s >= 5:
                        pe.wait_ge(y_done, num(s, -4))
                    e = pe.value_load(whose[0:1, bass.ds(num(s, -3), 1)], min_val=0, max_val=E - 1)
                    for k in range(2):
                        lhs = (ht_hi[:, b, k * P:(k + 1) * P], ht_lo[:, b, k * P:(k + 1) * P])
                        at = e * (2 * D) + k * D
                        mm = three(scr[:, b, 0:D], lhs, (dn_hi[:, bass.ds(at, D)], dn_lo[:, bass.ds(at, D)]), k == 0, k == 1)
                    mm.then_inc(y_full, 1)
            expert_steps(pe, step)

        @block.scalar
        def _(act):
            for n, (a, b) in enumerate(PIECES):
                act.wait_ge(stage_in[n % STAGES], 16 * (n // STAGES + 1))
                nc.scalar.copy(whi[:, a:b], stage[:, n % STAGES, 0:b - a]).then_inc(whi_done, 1)

            def hidden(turn, events):
                every = silu.events[turn.kind]

                def top(event):
                    f = int(event[1:])
                    act.wait_ge(*pair_done.at(turn, event))
                    nc.scalar.copy(hid_hi[:, f, :], hid[:, every.index(event) % 2, :]).then_inc(*hid_top.did(turn, event))
                for n, event in enumerate(events):
                    act.wait_ge(*pair_full.at(turn, event))
                    i = every.index(event)
                    if i >= 2:
                        act.wait_ge(*pair_done.at(turn, every[i - 2]))
                    nc.scalar.activation(gate[:, i % 2, :], ring[:, slot_of(turn, event), 1, :], ACT.Silu
                                         ).then_inc(*silu.did(turn, event))
                    if n:
                        top(events[n - 1])
                top(events[-1])

            act.wait_ge(vconsts, 1)

            def turn_(turn):
                if turn.front:
                    for part, to in (("k", kvsum), ("q", wsum)):
                        act.wait_ge(*pair_full.at(turn, part))
                        if part == "k" and turn.kind != "first":
                            act.wait_ge(*mid.before(turn, "ylo"))
                        nc.scalar.activation(to[:, :, :], ring[:, slot_of(turn, part), :, :], ACT.Square
                                             ).then_inc(*squares.did(turn, part))
                    for h, (part, to) in enumerate((("k", kvsum), ("q", wsum))):
                        act.wait_ge(*mid.at(turn, part + "sum"))
                        nc.scalar.copy(y_hi[:, h, :], to[:, 0, :]).then_inc(*sq_hi.did(turn, part))
                if turn.shared:
                    act.wait_ge(*scr_full.at(turn, "x"))
                    nc.scalar.copy(feat_hi[:, :, :], scr[:, :, :]).then_inc(*feat_top.did(turn, "x"))
                    act.wait_ge(*scr_full.at(turn, "logit"))
                    nc.scalar.copy(lgt[:, :], scr[0:RW, 0, :]).then_inc(*logit_out.did(turn, "logit"))
                    hidden(turn, hids[0:2])
                    act.wait_ge(*routed.at(turn, "lg"))
                    nc.scalar.activation(sig[:, :], lg[:, :, E], ACT.Tanh, scale=0.5).then_inc(*logit_out.did(turn, "tanh"))
                    hidden(turn, hids[2:3])
                if turn.front:
                    act.wait_ge(*scr_full.at(turn, "stat"))
                    nc.scalar.activation(rms[:, 0, :], scr[:, 0, :], ACT.Ln, bias=eps_c[:, 0:1], scale=1.0 / D
                                         ).then_inc(*rms_done.did(turn, "lnk"))
                    nc.scalar.activation(rms[:, 1, :], scr[:, 1, :], ACT.Ln, bias=eps_c[:, 0:1], scale=1.0 / D
                                         ).then_inc(*rms_done.did(turn, "lnq"))
                    for h, part in enumerate("kq"):
                        act.wait_ge(*rms_done.at(turn, "ln" + part))
                        nc.scalar.activation(rms[:, h, :], rms[:, h, :], ACT.Exp, scale=-0.5).then_inc(*rms_done.did(turn, part))
                    act.wait_ge(*mid.at(turn, "kr"))
                    nc.scalar.activation(ksb[:, :, :], ksb[:, :, :], ACT.Exp).then_inc(*rms_done.did(turn, "w"))
                    act.wait_ge(*mid.at(turn, "qr"))
                    nc.scalar.activation(qsb[:, :, :], qsb[:, :, :], ACT.Exp, scale=-1.0).then_inc(*rms_done.did(turn, "eq"))
                if turn.shared:
                    hidden(turn, hids[3:])
                if turn.front:
                    act.wait_ge(*mid.at(turn, "y"))
                    nc.scalar.copy(y_hi[:, :, :], kvsum[:, :, :]).then_inc(*rms_done.did(turn, "yhi"))
                    hidden(turn, hidf)
                if turn.next:
                    act.wait_ge(*scr_full.at(turn, "b"))
                    nc.scalar.copy(feat_hi[:, :, :], scr[:, :, :]).then_inc(*feat_top.did(turn, "b"))
            steps(act, turn_)
            act.wait_ge(*rms_done.at(Turn("tail"), "yhi"))
            act.sem_inc(dense_done, 1)

            nu = KD * 2 * EI
            for e in range(E):
                act.wait_ge(w_in[e % WSTAGES], 32 * (e // WSTAGES + 1))
                nc.scalar.copy(up_hi[:, e * nu:(e + 1) * nu], wst[:, e % WSTAGES, 0:nu]).then_inc(w_hi, 1)
                nc.scalar.copy(dn_hi[:, e * 2 * D:(e + 1) * 2 * D], wst[0:EHP, e % WSTAGES, nu:nu + 2 * D]).then_inc(w_hi, 1)

            def step(s, u):
                if live(s, 0):
                    b = u % 2
                    act.wait_ge(xt_full, num(s, 1))
                    if not isinstance(s, int) or s >= 2:
                        act.wait_ge(up_full, num(s, -1))
                    nc.scalar.copy(xt_hi[:, b, :], ring[:, 0, b, 0:D]).then_inc(xt_hi_done, 1)
                if live(s, 1):
                    b = (u - 1) % 2
                    act.wait_ge(up_full, num(s, 0))
                    if not isinstance(s, int) or s >= 3:
                        act.wait_ge(h_done, num(s, -2))
                    nc.scalar.activation(eg[:, b, :], ring[:, 1, b, 0:EI], ACT.Silu).then_inc(silu_done, 1)
                if live(s, 2):
                    b = (u - 2) % 2
                    act.wait_ge(ht_full, num(s, -1))
                    if not isinstance(s, int) or s >= 4:
                        act.wait_ge(y_full, num(s, -3))
                    nc.scalar.copy(ht_hi[0:EH, b, :], ring[0:EH, 2, b, 0:D]).then_inc(ht_hi_done, 1)
                if live(s, 3):
                    b = (u - 3) % 2
                    act.wait_ge(y_full, num(s, -2))
                    if not isinstance(s, int) or s >= LEAD + UNROLL:
                        act.wait_ge(sent[(u - 3) % UNROLL], (lap(s, u, 3) - 1) * 16)
                    nc.scalar.copy(ysb[:, (u - 3) % UNROLL, :], scr[:, b, 0:D]).then_inc(y_done, 1)
            expert_steps(act, step)
            act.wait_ge(weights, 2)
            nc.scalar.activation(wk[:, 0, :], wk[:, 0, :], ACT.Exp).then_inc(expd, 1)

        @block.vector
        def _(dve):
            V = nc.vector
            V.memset(ones_r[:, :].bitcast(F32), 1.0)
            V.memset(ones_b[:, :], 1.0)
            V.memset(ones_row[:, :], 1.0)
            V.memset(power[:, :], -0.5)
            V.memset(eps_c[:, :], RMS_EPS)
            V.memset(kvend[:, :, :], 0.0)
            V.memset(wend[:, :, :], DEN_EPS).then_inc(vconsts, 1)

            def split_lo(turn, event):
                dve.wait_ge(*feat_top.at(turn, event))
                V.tensor_tensor(feat_lo[:, :, :], scr[:, :, :], feat_hi[:, :, :].bitcast(F32), ALU.subtract
                                ).then_inc(*feat_split.did(turn, event))

            def first_norm(turn, part):
                if part == 0:
                    c = {"pre": 0, "first": 1, "steady": turn.t + 2}[turn.kind]
                    dve.wait_ge(x_in, (c + 1) * 16)
                    for t in range(TT):
                        i = V.bn_stats(st1[:, t, :], xin[:, t, :])
                    i.then_inc(*norm1.did(turn, "stats"))
                    apart(dve, norm1.at(turn, "stats"))
                    for t in range(TT):
                        i = V.bn_aggr(mv1[:, t, :], st1[:, t, :])
                    i.then_inc(*norm1.did(turn, "aggr"))
                    dve.wait_ge(*norm1.at(turn, "aggr"))
                    V.tensor_scalar(sc1[:, 0, :], mv1[:, :, 1], LN_EPS, None, ALU.add).then_inc(*norm1.did(turn, "ve"))
                if part == 1:
                    dve.wait_ge(*pows.at(turn, "n1a"))
                    V.tensor_tensor(sc1[:, 2, :], mv1[:, :, 1], sc1[:, 1, :], ALU.mult).then_inc(*norm1.did(turn, "u0"))
                    dve.wait_ge(*norm1.at(turn, "u0"))
                    V.tensor_tensor(sc1[:, 3, :], sc1[:, 2, :], sc1[:, 1, :], ALU.mult).then_inc(*norm1.did(turn, "u1"))
                    dve.wait_ge(*norm1.at(turn, "u1"))
                    V.tensor_scalar(sc1[:, 4, :], sc1[:, 3, :], RMS_EPS, None, ALU.add).then_inc(*norm1.did(turn, "ue"))
                if part == 2:
                    dve.wait_ge(*pows.at(turn, "n1b"))
                    V.tensor_tensor(sc1[:, 6, :], sc1[:, 1, :], sc1[:, 5, :], ALU.mult).then_inc(*norm1.did(turn, "scale"))
                    dve.wait_ge(*norm1.at(turn, "scale"))
                    for t in range(TT):
                        i = V.tensor_scalar(bnorm[:, t, :], xin[:, t, :], mv1[:, t, 0:1], sc1[:, 6, t:t + 1],
                                            ALU.subtract, ALU.mult)
                    i.then_inc(*norm1.did(turn, "b"))

            def product(turn, event):
                i = silu.events[turn.kind].index(event)
                dve.wait_ge(*silu.at(turn, event))
                if i >= 2:
                    was = silu.events[turn.kind][i - 2]
                    dve.wait_ge(*hid_top.at(turn, was))
                    dve.wait_ge(*(hid_lo_v if was[0] == "G" else hid_lo_p).at(turn, was))
                elif turn.kind in ("steady", "tail", "last"):
                    dve.wait_ge(*hid_lo_p.before(turn, f"S{FT - 2 + i}"))
                V.tensor_tensor(hid[:, i % 2, :], gate[:, i % 2, :], ring[:, slot_of(turn, event), 0, :], ALU.mult
                                ).then_inc(*pair_done.did(turn, event))

            def lower(turn, event):
                f = int(event[1:])
                dve.wait_ge(*hid_top.at(turn, event))
                V.tensor_tensor(hid_lo[:, f, :], hid[:, silu.events[turn.kind].index(event) % 2, :],
                                hid_hi[:, f, :].bitcast(F32), ALU.subtract).then_inc(*hid_lo_v.did(turn, event))

            def bc(ap, n):
                return ap.unsqueeze(2).to_broadcast([P, TT, n])

            def r3(i):
                return rt[:, i, :].rearrange("p (t e) -> p t e", t=TT)

            GT, EQ, CEQ, OK, TIE, SEL, RANK, RSEL, OFF, SLOT, TMP = range(11)

            def link(turn, ins, event):
                ins.then_inc(*routed.did(turn, event))
                dve.wait_ge(*routed.at(turn, event))

            def route_a(turn):
                dve.wait_ge(*scr_full.at(turn, "logit_t"))
                dve.wait_ge(table_clear, 16)
                link(turn, V.tensor_copy(lg[:, :, :], scr[:, 1, 0:TT * RW].rearrange("p (t r) -> p t r", t=TT)), "lg")
                c = {"steady": turn.t, "tail": CHUNKS - 2, "last": CHUNKS - 1}[turn.kind]
                l = lg[:, :, 0:E]
                V.tensor_copy(logits_all[:, bass.ds(c, 1), :, :].rearrange("p c t e -> p (c t) e"), l
                              ).then_inc(*routed.did(turn, "keep"))
                for t in range(TT):
                    i = V.max(top8[:, t, :], lg[:, t, 0:E])
                link(turn, i, "top")
                fourth = top8[:, :, TOPK - 1:TOPK].to_broadcast([P, TT, E])
                V.tensor_tensor(r3(GT), l, fourth, ALU.is_gt).then_inc(*routed.did(turn, "gt"))
                link(turn, V.tensor_tensor(r3(EQ), l, fourth, ALU.is_equal), "eq")
                link(turn, V.tensor_reduce(rsm[:, 0, :], r3(GT), AX_X, ALU.add), "cgt")
                link(turn, V.tensor_scalar(rsm[:, 1, :], rsm[:, 0, :], -1.0, float(TOPK), ALU.mult, ALU.add), "need")
                link(turn, V.tensor_tensor_scan(rt[:, CEQ, :], notfirst[:, :], rt[:, EQ, :], 0.0, ALU.mult, ALU.add), "ceq")
                link(turn, V.tensor_tensor(r3(OK), r3(CEQ), bc(rsm[:, 1, :], E), ALU.is_le), "ok")
                link(turn, V.tensor_tensor(rt[:, TIE, :], rt[:, EQ, :], rt[:, OK, :], ALU.mult), "tie")
                link(turn, V.tensor_tensor(rt[:, SEL, :], rt[:, GT, :], rt[:, TIE, :], ALU.add), "sel")
                V.tensor_copy(selb[:, :], rt[:, SEL, :]).then_inc(*routed.did(turn, "selb"))
                link(turn, V.tensor_tensor_scan(rt[:, RANK, :], notfirst[:, :], rt[:, SEL, :], 0.0, ALU.mult, ALU.add), "rank")
                link(turn, V.tensor_tensor(rt[:, RSEL, :], rt[:, RANK, :], rt[:, SEL, :], ALU.mult), "rsel")
                V.tensor_copy(rank_all[:, bass.ds(c, 1), :, :].rearrange("p c t e -> p (c t e)"), rt[:, RSEL, :]
                              ).then_inc(*routed.did(turn, "rkeep"))

            def route_b(turn):
                dve.wait_ge(*scr_full.at(turn, "count"))
                link(turn, V.tensor_copy(rt[:, OFF, 0:E], filled[:, :]), "off0")
                for t in range(1, TT + 1):
                    to = rt[:, OFF, t * E:(t + 1) * E] if t < TT else filled[:, :]
                    link(turn, V.tensor_tensor(to, rt[:, OFF, (t - 1) * E:t * E], scr[:, 1, 192 + (t - 1) * E:192 + t * E],
                                               ALU.add), f"off{t}")
                link(turn, V.tensor_tensor(rt[:, SLOT, :], rt[:, OFF, :], scr[:, 1, 128:192], ALU.add), "slot")
                for k in range(TOPK):
                    link(turn, V.scalar_tensor_tensor(rt[:, TMP, :], rt[:, RSEL, :], float(k + 1), rt[:, SLOT, :],
                                                      ALU.is_equal, ALU.mult), f"m{k}")
                    link(turn, V.tensor_reduce(slot_f[:, :, k], r3(TMP), AX_X, ALU.add), f"s{k}")
                c = {"steady": turn.t, "tail": CHUNKS - 2, "last": CHUNKS - 1}[turn.kind]
                if turn.kind == "steady":
                    dve.wait_ge(id_out, c * (16 * TT * TOPK))
                else:
                    dve.wait_ge(id_out, c * 16 * TT * TOPK)
                V.tensor_copy(slot_u[:, :], slot_f[:, :, :].rearrange("p t k -> p (t k)")).then_inc(*routed.did(turn, "slotu"))
                V.tensor_scalar(idval[:, :], idval[:, :], float(TOPK * CHUNK), None, ALU.add).then_inc(*routed.did(turn, "id"))

            for n, (a, b) in enumerate(PIECES):
                dve.wait_ge(whi_done, n + 1)
                V.tensor_tensor(wlo[:, a:b], stage[:, n % STAGES, 0:b - a], whi[:, a:b].bitcast(F32), ALU.subtract
                                ).then_inc(wlo_done, 1)
            dve.wait_ge(consts, 1)
            dve.wait_ge(vconsts, 1)

            def turn_(turn):
                if turn.front:
                    if turn.kind != "first":
                        dve.wait_ge(*mid.before(turn, "ylo"))
                    for part, of, to in (("k", kvsum, ksb), ("q", wsum, qsb)):
                        dve.wait_ge(*squares.at(turn, part))
                        V.tensor_copy(to[:, :, :], ring[:, slot_of(turn, part), :, :]).then_inc(*pair_done.did(turn, part))
                        V.tensor_tensor(of[:, 0, :], of[:, 0, :], of[:, 1, :], ALU.add).then_inc(*mid.did(turn, part + "sum"))
                        h = "kq".index(part)
                        dve.wait_ge(*sq_hi.at(turn, part))
                        V.tensor_tensor(y_lo[:, h, :], of[:, 0, :], y_hi[:, h, :].bitcast(F32), ALU.subtract
                                        ).then_inc(*mid.did(turn, part + "lo"))
                    dve.wait_ge(*pair_full.at(turn, "v"))
                    V.tensor_copy(vsb[:, :, :], ring[:, slot_of(turn, "v"), :, :]).then_inc(*pair_done.did(turn, "v"))
                if turn.shared:
                    split_lo(turn, "x")
                    route_a(turn)
                    product(turn, "G0")
                    lower(turn, "G0")
                    product(turn, "G1")
                    lower(turn, "G1")
                    route_b(turn)
                    product(turn, "G2")
                    lower(turn, "G2")
                    dve.wait_ge(*logit_out.at(turn, "tanh"))
                    V.tensor_scalar(sig[:, :], sig[:, :], 0.5, 0.5, ALU.mult, ALU.add).then_inc(*sig_done.did(turn, "half"))
                if turn.front:
                    for h, (part, to) in enumerate((("k", ksb), ("q", qsb))):
                        dve.wait_ge(*rms_done.at(turn, part))
                        V.tensor_tensor(to[:, :, :], to[:, :, :], rms[:, h, :].unsqueeze(1).to_broadcast([P, KD, CHUNK]),
                                        ALU.mult).then_inc(*mid.did(turn, part + "r"))
                if turn.shared:
                    product(turn, "G3")
                    lower(turn, "G3")
                if turn.front:
                    dve.wait_ge(*rms_done.at(turn, "w"))
                    V.tensor_tensor(vsb[:, :, :], vsb[:, :, :], ksb[:, :, :], ALU.mult).then_inc(*mid.did(turn, "wv"))

                    def scans(to, of, end, name):
                        for k in range(KD):
                            for b in range(BATCH):
                                i = V.tensor_tensor_scan(to[:, k, b * RUN:(b + 1) * RUN], ones_row[:, :],
                                                         of[:, k, b * RUN:(b + 1) * RUN], end[:, k, b:b + 1], ALU.mult, ALU.add)
                        i.then_inc(*mid.did(turn, name))
                        dve.wait_ge(*mid.at(turn, name))
                        V.tensor_copy(end[:, :, :], to[:, :, :].rearrange("p k (b r) -> p k b r", b=BATCH)[:, :, :, RUN - 1]
                                      ).then_inc(*mid.did(turn, name[:-3] + "end"))
                    if turn.kind != "first":
                        dve.wait_ge(*mid.before(turn, "kvend"))
                    scans(wsum, ksb, wend, "wsum")
                    dve.wait_ge(*mid.at(turn, "wv"))
                    scans(kvsum, vsb, kvend, "kvsum")
                if turn.shared:
                    product(turn, "G4")
                    lower(turn, "G4")
                if turn.front:
                    dve.wait_ge(*rms_done.at(turn, "eq"))
                    V.scalar_tensor_tensor(qsb[:, :, :], qsb[:, :, :], 1.0, wsum[:, :, :], ALU.add, ALU.mult
                                           ).then_inc(*mid.did(turn, "d"))
                    dve.wait_ge(*mid.at(turn, "d"))
                    V.reciprocal(ksb[:, :, :], qsb[:, :, :]).then_inc(*mid.did(turn, "rec"))
                if turn.shared:
                    product(turn, "G5")
                    lower(turn, "G5")
                if turn.front:
                    dve.wait_ge(*mid.at(turn, "rec"))
                    V.tensor_tensor(kvsum[:, :, :], kvsum[:, :, :], ksb[:, :, :], ALU.mult).then_inc(*mid.did(turn, "y"))
                    dve.wait_ge(*rms_done.at(turn, "yhi"))
                    V.tensor_tensor(y_lo[:, :, :], kvsum[:, :, :], y_hi[:, :, :].bitcast(F32), ALU.subtract
                                    ).then_inc(*mid.did(turn, "ylo"))
                if turn.shared:
                    dve.wait_ge(*sig_done.at(turn, "half"))
                    for d in range(2):
                        dve.wait_ge(*pair_full.at(turn, f"D{d}"))
                        for h in range(2):
                            t = 2 * d + h
                            i = V.scalar_tensor_tensor(x1[:, t, :], ring[:, slot_of(turn, f"D{d}"), h, 0:D], sig[:, t:t + 1],
                                                       x1[:, t, :], ALU.mult, ALU.add)
                        i.then_inc(*pair_done.did(turn, f"D{d}"))
                if turn.front:
                    for f in range(FT):
                        product(turn, f"S{f}")
                        if turn.next and f in (1, 3, 5):
                            first_norm(turn, f // 2)
                elif turn.next:
                    for part in range(3):
                        first_norm(turn, part)
                if turn.next:
                    split_lo(turn, "b")
                if turn.front:
                    if turn.kind != "first":
                        dve.wait_ge(acc_out, (turn.t + 1) * 16 if turn.kind == "steady" else (CHUNKS - 1) * 16)
                    (dve.wait_ge(*resid.before(turn, "res")))
                    for w in range(2):
                        dve.wait_ge(*pair_full.at(turn, f"W{w}"))
                        V.tensor_tensor(x1[:, 2 * w:2 * w + 2, :], res[:, 2 * w:2 * w + 2, :],
                                        ring[:, slot_of(turn, f"W{w}"), :, 0:D], ALU.add).then_inc(*pair_done.did(turn, f"W{w}"))
                    dve.wait_ge(*pair_done.at(turn, "W1"))
                    for t in range(TT):
                        i = V.bn_stats(st2[:, t, :], x1[:, t, :])
                    i.then_inc(*norm2.did(turn, "stats"))
                    apart(dve, norm2.at(turn, "stats"))
                    for t in range(TT):
                        i = V.bn_aggr(mv2[:, t, :], st2[:, t, :])
                    i.then_inc(*norm2.did(turn, "aggr"))
                    dve.wait_ge(*norm2.at(turn, "aggr"))
                    V.tensor_scalar(sc2[:, 0, :], mv2[:, :, 1], LN_EPS, None, ALU.add).then_inc(*norm2.did(turn, "ve"))
                    dve.wait_ge(*pows.at(turn, "n2"))
                    if turn.kind != "first":
                        dve.wait_ge(xn2_out, (turn.t + 1) * 16 if turn.kind == "steady" else (CHUNKS - 1) * 16)
                        dve.wait_ge(*scr_full.at(turn, "x"))
                    for t in range(TT):
                        i = V.tensor_scalar(xn2[:, t, :], x1[:, t, :], mv2[:, t, 0:1], sc2[:, 1, t:t + 1],
                                            ALU.subtract, ALU.mult)
                    i.then_inc(*norm2.did(turn, "xn2"))
            steps(dve, turn_)
            dve.wait_ge(*norm2.at(Turn("tail"), "xn2"))
            dve.wait_ge(*pair_done.at(Turn("last"), "D1"))
            dve.wait_ge(*routed.at(Turn("last"), "id"))
            dve.sem_inc(dense_done, 1)

            done = [0]

            def note(ins):
                done[0] += 1
                ins.then_inc(lists, 1)
                dve.wait_ge(lists, done[0])
            dve.wait_ge(acc_out, 16 * CHUNKS)
            dve.wait_ge(id_out, CHUNKS * 16 * TT * TOPK)
            dve.wait_ge(dense_done, 3)
            NTOK, NLIST, UPTO, BASE = range(4)
            lots = pick[:, :, :].rearrange("p g l -> p (g l)")[:, 0:E * ROWS]
            note(V.tensor_tensor(em[:, NTOK, :], filled[:, :], first_slot[:, :], ALU.subtract))
            note(V.tensor_tensor(lots.rearrange("p (e j) -> p e j", e=E), em[:, NTOK, :].unsqueeze(2).to_broadcast([P, E, ROWS]),
                                 list_start[:, :].unsqueeze(1).to_broadcast([P, E, ROWS]), ALU.is_gt))
            note(V.tensor_reduce(em[:, NLIST, :], lots.rearrange("p (e j) -> p e j", e=E), AX_X, ALU.add))
            note(V.tensor_tensor_scan(em[:, UPTO, :], ones_row[:, 0:E], em[:, NLIST, :], 0.0, ALU.mult, ALU.add))
            note(V.tensor_tensor(em[:, BASE, :], em[:, UPTO, :], em[:, NLIST, :], ALU.subtract))
            mask = quarter[:, :].unsqueeze(1).to_broadcast([P, 4, 4])
            V.tensor_tensor(em[:, 4, :].rearrange("p (g q) -> p g q", g=4), em[:, BASE, :].rearrange("p (g q) -> p g q", g=4), mask, ALU.mult)
            note(V.tensor_tensor(em[:, 5, :].rearrange("p (g q) -> p g q", g=4), em[:, NLIST, :].rearrange("p (g q) -> p g q", g=4), mask, ALU.mult))
            V.tensor_reduce(em[:, 6, 0:4], em[:, 4, :].rearrange("p (g q) -> p g q", g=4), AX_X, ALU.add)
            note(V.tensor_reduce(em[:, 6, 4:8], em[:, 5, :].rearrange("p (g q) -> p g q", g=4), AX_X, ALU.add))
            link2 = [0]

            def small(ins):
                link2[0] += 1
                ins.then_inc(smalls, 1)
                dve.wait_ge(smalls, link2[0])
            V.tensor_scalar(em[:, 7, 0:4], em[:, 6, 0:4], in_quarter[:, 0:1], 1.0, ALU.add, ALU.add)
            small(V.tensor_scalar(em[:, 7, 4:8], em[:, 6, 4:8], in_quarter[:, 0:1], None, ALU.is_gt))
            small(V.tensor_tensor(em[:, 7, 8:12], em[:, 7, 0:4], em[:, 7, 4:8], ALU.mult))
            small(V.tensor_scalar(em[:, 7, 12:16], em[:, 7, 8:12], -1.0, None, ALU.add))
            for g in range(4):
                i = V.tensor_scalar(pick[:, g, :], list_no[:, :], em[:, 7, 12 + g:13 + g], None, ALU.is_equal)
            note(i)
            assert done[0] == 8
            for e in range(E):
                last = small if e < E - 1 else note
                was = ix[0:1, 0, :] if e else None
                if e == 0:
                    last(V.tensor_scalar(ix[0:1, 0, :], list_no[0:1, :], em[0:1, BASE, 0:1], None, ALU.is_ge))
                else:
                    last(V.scalar_tensor_tensor(ix[0:1, 0, :], list_no[0:1, :], em[0:1, BASE, e:e + 1], was, ALU.is_ge, ALU.add))
            note(V.tensor_scalar(whose[:, :], ix[0:1, 0, :], -1.0, None, ALU.add))
            dve.wait_ge(lists_t, 1)
            note(V.tensor_scalar(ix[:, 1, :], scr[:, 0, 0:LISTS], 1.0, 0.0, ALU.subtract, ALU.max))
            V.scalar_tensor_tensor(ix[:, 2, :], scr[:, 0, 0:LISTS], 0.0, spare[:, :], ALU.is_equal, ALU.mult)
            V.memset(take[:, LISTS:LISTS + UNROLL], 0)
            note(V.tensor_copy(take[:, 0:LISTS], ix[:, 1, :]))
            note(V.tensor_scalar(take[:, 0:LISTS], take[:, 0:LISTS], 2, None, ALU.logical_shift_right))
            note(V.scalar_tensor_tensor(put[:, :], scr[:, 0, 0:LISTS], -1.0, ix[:, 2, :], ALU.add, ALU.add))
            assert done[0] == 14
            V.tensor_copy(take_now[:, :], take[:, 0:UNROLL]).then_inc(take_set, UNROLL)
            V.memset(ht_hi[64:EHP, :, :].bitcast(F32), 0.0).then_inc(pad_rows, 1)
            V.memset(ht_lo[64:EHP, :, :].bitcast(F32), 0.0).then_inc(pad_rows, 1)
            dve.wait_ge(pad_rows, 2)

            nu = KD * 2 * EI
            for e in range(E):
                dve.wait_ge(w_hi, 2 * e + 2)
                V.tensor_tensor(up_lo[:, e * nu:(e + 1) * nu], wst[:, e % WSTAGES, 0:nu],
                                up_hi[:, e * nu:(e + 1) * nu].bitcast(F32), ALU.subtract)
                V.tensor_tensor(dn_lo[:, e * 2 * D:(e + 1) * 2 * D], wst[0:EHP, e % WSTAGES, nu:nu + 2 * D],
                                dn_hi[:, e * 2 * D:(e + 1) * 2 * D].bitcast(F32), ALU.subtract).then_inc(w_lo, 1)

            def step(s, u):
                if live(s, 0):
                    b = u % 2
                    dve.wait_ge(xt_hi_done, num(s, 1))
                    V.tensor_tensor(xt_lo[:, b, :], ring[:, 0, b, 0:D], xt_hi[:, b, :].bitcast(F32), ALU.subtract
                                    ).then_inc(xt_lo_done, 1)
                    dve.wait_ge(got[u], lap(s, u) * 16)
                    V.tensor_copy(take_now[:, u:u + 1], take[:, bass.ds(num(s, UNROLL), 1)]).then_inc(take_set, 1)
                if live(s, 1):
                    b = (u - 1) % 2
                    dve.wait_ge(silu_done, num(s, 0))
                    if not isinstance(s, int) or s >= 3:
                        dve.wait_ge(ht_full, num(s, -2))
                    V.tensor_tensor(eh[:, b, :], eg[:, b, :], ring[:, 1, b, EI:2 * EI], ALU.mult).then_inc(h_done, 1)
                if live(s, 2):
                    b = (u - 2) % 2
                    dve.wait_ge(ht_hi_done, num(s, -1))
                    V.tensor_tensor(ht_lo[0:EH, b, :], ring[0:EH, 2, b, 0:D], ht_hi[0:EH, b, :].bitcast(F32), ALU.subtract
                                    ).then_inc(ht_lo_done, 1)
                if live(s, 3):
                    if not isinstance(s, int) or s >= LEAD + UNROLL:
                        dve.wait_ge(sent[(u - 3) % UNROLL], (lap(s, u, 3) - 1) * 16)
                    V.tensor_copy(put_now[:, (u - 3) % UNROLL:(u - 3) % UNROLL + 1], put[:, bass.ds(num(s, -3), 1)]
                                  ).then_inc(put_set, 1)
            expert_steps(dve, step)

            dve.wait_ge(h_done, LISTS)
            dve.wait_ge(ht_lo_done, LISTS)
            for i in range(UNROLL):
                dve.wait_ge(sent[i], 16 * (LISTS // UNROLL))
            done = [0]

            def note3(ins):
                done[0] += 1
                ins.then_inc(weights, 1)
                dve.wait_ge(weights, done[0])
            la = logits_all[:, :, :, :].rearrange("p c t e -> p (c t) e")
            ra = rank_all[:, :, :, :].rearrange("p c t e -> p (c t e)")
            ex = wk[:, 0, :]
            tmp = wk[:, 1, :]
            note3(V.tensor_reduce(wm[:, 0, :], la, AX_X, ALU.max))
            note3(V.tensor_tensor(ex.rearrange("p (i e) -> p i e", e=E), la, wm[:, 0, :].unsqueeze(2).to_broadcast([P, TILES, E]),
                                  ALU.subtract))
            dve.wait_ge(expd, 1)
            for k in range(TOPK):
                note3(V.scalar_tensor_tensor(tmp, ra, float(k + 1), ex, ALU.is_equal, ALU.mult))
                note3(V.tensor_reduce(share[:, :, k], tmp.rearrange("p (i e) -> p i e", e=E), AX_X, ALU.add))
            note3(V.tensor_reduce(wm[:, 1, :], share[:, :, :], AX_X, ALU.add))
            note3(V.reciprocal(wm[:, 2, :], wm[:, 1, :]))
            note3(V.tensor_tensor(share[:, :, :], share[:, :, :], wm[:, 2, :].unsqueeze(2).to_broadcast([P, TILES, TOPK]), ALU.mult))

            def total(i, t, u):
                lap_ = 1 if isinstance(t, int) else t + 2
                dve.wait_ge(z_in[u], 32 * lap_)
                if not isinstance(t, int):
                    dve.wait_ge(o_out[u], 16 * (t + 1))
                for k in range(TOPK):
                    if k:
                        dve.wait_ge(summed, i * TOPK + k)
                    V.scalar_tensor_tensor(sums[:, u, :], zin[:, u, k * D:(k + 1) * D],
                                           share[:, bass.ds(i, 1), k:k + 1].rearrange("p a b -> p (a b)"),
                                           sums[:, u, :] if k else ain[:, u, :], ALU.mult, ALU.add).then_inc(summed, 1)
            for u in range(UNROLL):
                total(u, -1, u)
            with dve.Fori(0, TILES // UNROLL - 1) as t:
                for u in range(UNROLL):
                    total(t * UNROLL + (UNROLL + u), t, u)

        @block.gpsimd
        def _(pool):
            G = nc.gpsimd
            gchain = sem("gchain")
            n = 0

            def link(ins):
                nonlocal n
                n += 1
                ins.then_inc(gchain, 1)
                pool.wait_ge(gchain, n)
            link(G.memset(ident[:, :], 0.0))
            link(G.affine_select(out=ident[:, :], in_=ident[:, :], compare_op=ALU.not_equal, fill=1.0, base=0,
                                 pattern=[[-1, P]], channel_multiplier=1))
            link(G.memset(notfirst[:, :], 1.0))
            nf = notfirst[:, :].rearrange("p (t e) -> p t e", t=TT)
            link(G.memset(nf[:, :, 0:1], 0.0))
            link(G.iota(filled[:, :], pattern=[[TOKENS, E]], base=0, channel_multiplier=0,
                        allow_small_or_imprecise_dtypes=True))
            link(G.iota(idval[:, :], pattern=[[TOPK * P, TT], [1, TOPK]], base=1 - TOPK * CHUNK, channel_multiplier=TOPK,
                        allow_small_or_imprecise_dtypes=True))
            link(G.iota(first_slot[:, :], pattern=[[TOKENS, E]], base=0, channel_multiplier=0, allow_small_or_imprecise_dtypes=True))
            link(G.iota(list_start[:, :], pattern=[[P, ROWS]], base=0, channel_multiplier=0, allow_small_or_imprecise_dtypes=True))
            link(G.iota(list_no[:, :], pattern=[[1, LISTS]], base=0, channel_multiplier=0, allow_small_or_imprecise_dtypes=True))
            link(G.iota(spare[:, :], pattern=[[P, LISTS]], base=PICKED + 1, channel_multiplier=1, allow_small_or_imprecise_dtypes=True))
            link(G.memset(quarter[:, :], 0.0))
            for q in range(4):
                link(G.memset(quarter[32 * q:32 * q + 32, q:q + 1], 1.0))
                link(G.iota(in_quarter[32 * q:32 * q + 32, :], pattern=[[0, 1]], base=0, channel_multiplier=1,
                            allow_small_or_imprecise_dtypes=True))
            link(G.memset(earlier[:, :], 1.0))
            G.affine_select(out=earlier[:, :], in_=earlier[:, :], compare_op=ALU.is_gt, fill=0.0, base=0,
                            pattern=[[1, P]], channel_multiplier=-1).then_inc(consts, 1)
            link(G.memset(rank_all[:, :, :, :], 0.0))
            pool.dma_start(ids.rearrange("(p n) o -> p (n o)", p=P), rank_all[:, :, :, :].rearrange("p c t e -> p (c t e)")
                           ).then_inc(table_clear, 16)
            pool.wait_ge(table_clear, 16)
            pool.wait_ge(vconsts, 1)

            def turn_(turn):
                if turn.kind == "pre":
                    first(turn)
                    residual(turn)
                    return
                if turn.shared:
                    apart(pool, routed.at(turn, "id"))
                    for i in range(TT * TOPK):
                        scatter(i)
                if turn.front:
                    for f in range(FT):
                        pool.wait_ge(*hid_top.at(turn, f"S{f}"))
                        G.tensor_tensor(hid_lo[:, f, :], hid[:, silu.events[turn.kind].index(f"S{f}") % 2, :],
                                        hid_hi[:, f, :].bitcast(F32), ALU.subtract).then_inc(*hid_lo_p.did(turn, f"S{f}"))
                        if turn.next and f == 1:
                            power_a(turn)
                        if turn.next and f == 3:
                            power_b(turn)
                    pool.wait_ge(*norm2.at(turn, "ve"))
                    G.tensor_tensor(sc2[:, 1, :], sc2[:, 0, :], power[:, :], ALU.pow).then_inc(*pows.did(turn, "n2"))
                if turn.next:
                    residual(turn)

            def power_a(turn):
                pool.wait_ge(*norm1.at(turn, "ve"))
                G.tensor_tensor(sc1[:, 1, :], sc1[:, 0, :], power[:, :], ALU.pow).then_inc(*pows.did(turn, "n1a"))

            def power_b(turn):
                pool.wait_ge(*norm1.at(turn, "ue"))
                G.tensor_tensor(sc1[:, 5, :], sc1[:, 4, :], power[:, :], ALU.pow).then_inc(*pows.did(turn, "n1b"))

            def first(turn):
                power_a(turn)
                power_b(turn)

            def residual(turn):
                apart(pool, norm1.at(turn, "b"), *([pair_done.at(turn, "W1")] if turn.front else []))
                G.tensor_scalar(sc1[:, 7, :], sc1[:, 1, :], 1.0, 1.0, ALU.mult, ALU.add).then_inc(*resid.did(turn, "rp"))
                G.tensor_tensor(sc1[:, 2, :], mv1[:, :, 0], sc1[:, 1, :], ALU.mult).then_inc(*resid.did(turn, "nm"))
                apart(pool, resid.at(turn, "nm"))
                for t in range(TT):
                    i = G.tensor_scalar(res[:, t, :], xin[:, t, :], sc1[:, 7, t:t + 1], sc1[:, 2, t:t + 1],
                                        ALU.mult, ALU.subtract)
                i.then_inc(*resid.did(turn, "res"))

            def scatter(i):
                G.indirect_dma_start(out=ids, out_offset=bass.IndirectOffsetOnAxis(ap=slot_u[:, i:i + 1], axis=0),
                                     in_=idval[:, i:i + 1], in_offset=None).then_inc(id_out, 16)
            steps(pool, turn_)
            pool.wait_ge(id_out, CHUNKS * 16 * TT * TOPK)
            pool.wait_ge(*hid_lo_p.at(Turn("tail"), f"S{FT - 1}"))
            pool.sem_inc(dense_done, 1)

            def gather(tile, u):
                G.indirect_dma_start(out=xg[:, u, :], out_offset=None, in_=xn2_rows,
                                     in_offset=bass.IndirectOffsetOnAxis(ap=take_now[:, u:u + 1], axis=0)).then_inc(got[u], 16)

            def send(u):
                G.indirect_dma_start(out=picked, out_offset=bass.IndirectOffsetOnAxis(ap=put_now[:, u:u + 1], axis=0),
                                     in_=ysb[:, u, :], in_offset=None).then_inc(sent[u], 16)

            def next_gather(n, u):
                apart(pool, (take_set, n + (UNROLL + 1)), (xt_full, n + 1))
                gather(None, u)

            def next_send(n, u):
                apart(pool, (put_set, n + 1), (y_done, n + 1))
                send(u)
            pool.wait_ge(xn2_out, 16 * CHUNKS)
            pool.wait_ge(take_set, UNROLL)
            for u in range(UNROLL):
                gather(None, u)
            for u in range(UNROLL):
                next_gather(u, u)
            with pool.Fori(0, LISTS // UNROLL - 2) as t:
                for u in range(UNROLL):
                    next_gather(t * UNROLL + (UNROLL + u), u)
                    next_send(t * UNROLL + u, u)
            for n in range(LISTS - 2 * UNROLL, LISTS):
                next_send(n, n % UNROLL)

        for s in (pair_full, scr_full, pair_done, feat_split, norm1, norm2, mid, routed, sig_done, hid_lo_v, squares, sq_hi,
                  feat_top, logit_out, rms_done, silu, hid_top, pows, resid, hid_lo_p):
            s.check()


def kernel(**inputs):
    import numpy as np
    import concourse.bacc as bacc
    from concourse.bass_utils import run_bass_kernel_spmd

    def by_rows(w):
        k = w.shape[0] // P
        return w.reshape(k, P, -1).transpose(1, 0, 2).reshape(P, -1)

    get = {name: np.asarray(a) for name, a in inputs.items()}
    x = get["L0_attn_x"].reshape(BATCH, CHUNKS, RUN, D).transpose(1, 0, 2, 3).reshape(TOKENS, D)
    router = np.zeros((D, RW), np.float32)
    router[:, 0:E] = get["L0_ffn_gate_w"].T
    router[:, E] = get["L0_ffn_shared_gate_vec"][0]
    s_up = np.zeros((D, 2, SIP), np.float32)
    s_up[:, :, 0:SI] = get["L0_ffn_shared_gate_up"].T.reshape(D, 2, SI)
    s_down = np.zeros((SIP, D), np.float32)
    s_down[0:SI] = get["L0_ffn_shared_down"].T
    w1 = np.concatenate([by_rows(w) for w in (get["L0_attn_w_qkv"].T, router, get["L0_attn_w_swiglu"].T, get["L0_attn_w_out"].T,
                                              s_up.reshape(D, 2 * SIP), s_down)], axis=1)
    w_up = get["L0_ffn_expert_gate_up"].transpose(0, 2, 1).reshape(E, KD, P, 2 * EI).transpose(0, 2, 1, 3).reshape(E, P, KD * 2 * EI)
    w_down = np.zeros((E, EHP, 2, D), np.float32)
    w_down[:, 0:EH] = get["L0_ffn_expert_down"].transpose(0, 2, 1).reshape(E, 2, EH, D).transpose(0, 2, 1, 3)
    arrays = {name: np.ascontiguousarray(a) for name, a in
              {"x": x, "w1": w1, "w_up": w_up, "w_down": w_down.reshape(E, EHP, 2 * D)}.items()}
    nc = bacc.Bacc("TRN2", target_bir_lowering=False, num_devices=1)
    ins = [nc.dram_tensor(name, a.shape, F32, kind="ExternalInput").ap() for name, a in arrays.items()]
    out = nc.dram_tensor("out", (TOKENS, D), F32, kind="ExternalOutput").ap()
    scratch = [nc.dram_tensor(name, shape, F32, kind="Internal").ap() for name, shape in
               (("xn2_rows", (TOKENS, D)), ("acc", (TOKENS, D)), ("ids", (E * TOKENS, 1)), ("picked", (PICKED + LISTS * P, D)))]
    build(nc, *ins, out, *scratch)
    got = run_bass_kernel_spmd(nc, [arrays], core_ids=[0]).results[0]["out"]
    return got.reshape(CHUNKS, BATCH, RUN, D).transpose(1, 0, 2, 3).reshape(BATCH, SEQ, D)
```

```python
from contextlib import ExitStack

import concourse.bass as bass
from concourse import mybir

F32 = mybir.dt.float32
F32R = mybir.dt.float32r
BF16 = mybir.dt.bfloat16
U32 = mybir.dt.uint32
ALU = mybir.AluOpType
ACT = mybir.ActivationFunctionType
AX_X = mybir.AxisListType.X

P = 128
D = 256
KD = D // P
BATCH, SEQ = 2, 2048
TOKENS = BATCH * SEQ
CHUNK = 512
CHUNKS = TOKENS // CHUNK
TT = CHUNK // P
RUN = CHUNK // BATCH
FF = 1024
FT = FF // P
SI = 704
ST = -(-SI // P)
SIP = ST * P
E = 16
TOPK = 4
EI = 176
EH = EI // 2
EHP = 96
RW = 32
LN_EPS = 1e-5
RMS_EPS = 1.1920929e-07
DEN_EPS = 1e-6

QKV0 = 0
RT0 = QKV0 + KD * 3 * D
SW0 = RT0 + KD * RW
WO0 = SW0 + KD * 2 * FF
SG0 = WO0 + FT * D
SD0 = SG0 + KD * 2 * SIP
WCOLS = SD0 + ST * D
PIECES = [(QKV0, SW0), (SW0, SW0 + FF * 2), (SW0 + FF * 2, WO0), (WO0, SG0),
          (SG0, SG0 + SIP * 2), (SG0 + SIP * 2, SD0), (SD0, WCOLS)]
STAGE = 2048
STAGES = 4

ROWS = TOKENS // P
LISTS = TOKENS * TOPK // P + E
PICKED = TOKENS * TOPK
UNROLL = 4
LEAD = 3
WSTAGES = 3
assert LISTS % UNROLL == 0
KINDS = ["pre", "first", "steady", "tail", "last"]
STEADY = CHUNKS - 2


class Turn:

    def __init__(self, kind, t=0):
        self.kind, self.t = kind, t
        self.front = kind in ("first", "steady", "tail")
        self.shared = kind in ("steady", "tail", "last")
        self.next = kind in ("pre", "first", "steady")


class Signal:

    def __init__(self, sem, front=(), shared=(), nxt=(), order=None):
        self.sem = sem
        every = order or [*front, *shared, *nxt]
        self.events = {}
        for kind in KINDS:
            turn = Turn(kind)
            on = [*(front if turn.front else ()), *(shared if turn.shared else ()), *(nxt if turn.next else ())]
            self.events[kind] = [e for e in every if e in on]
        self.raised = {kind: 0 for kind in KINDS}

    def start(self, turn):
        n = {kind: len(self.events[kind]) for kind in KINDS}
        before = KINDS[:KINDS.index(turn.kind)]
        at = sum(n[k] * (STEADY if k == "steady" else 1) for k in before)
        return turn.t * n["steady"] + at if turn.kind == "steady" else at

    def did(self, turn, event):
        assert self.events[turn.kind][self.raised[turn.kind]] == event, (turn.kind, event, self.events[turn.kind])
        self.raised[turn.kind] += 1
        return self.sem, 1

    def at(self, turn, event):
        return self.sem, self.start(turn) + (self.events[turn.kind].index(event) + 1)

    def before(self, turn, event):
        was = {"first": ["pre"], "steady": ["first", "steady"], "tail": ["steady"], "last": ["tail"]}[turn.kind]
        after = {len(self.events[k]) - self.events[k].index(event) - 1 for k in was}
        assert len(after) == 1
        return self.sem, self.start(turn) - after.pop()

    def check(self):
        for kind in KINDS:
            assert self.raised[kind] == len(self.events[kind]), (kind, self.raised, self.events)


SHARED_UP = [f"G{f}" for f in range(ST)]
FRONT_UP = [f"S{f}" for f in range(FT)]
FILLS = ["x", "stat", *SHARED_UP, "D0", "D1", *FRONT_UP, "b", "W0", "W1", "k", "q", "v"]
PAIRS = 3
assert len(FILLS) % PAIRS == 0


def build(nc, x, w1, w_up, w_down, out, xn2_rows, acc, ids, picked):
    ctx = ExitStack()
    with ctx:
        def sb(name, shape, dt, where=ctx):
            return where.enter_context(nc.sbuf_tensor(name, shape, dt))

        def sem(name):
            return ctx.enter_context(nc.semaphore(name))

        ident = sb("ident", [P, P], F32)
        ones_r = sb("ones_r", [P, P], F32R)
        ones_b = sb("ones_b", [P, P], BF16)
        earlier = sb("earlier", [P, P], BF16)
        ones_row = sb("ones_row", [P, RUN], F32)
        notfirst = sb("notfirst", [P, TT * E], F32)
        power = sb("power", [P, TT], F32)
        eps_c = sb("eps_c", [P, 1], F32)
        logits_all = sb("logits_all", [P, CHUNKS, TT, E], F32)
        rank_all = sb("rank_all", [P, CHUNKS, TT, E], F32)
        filled = sb("filled", [P, E], F32)
        first_slot = sb("first_slot", [P, E], F32)
        list_start = sb("list_start", [P, ROWS], F32)
        quarter = sb("quarter", [P, 4], F32)
        in_quarter = sb("in_quarter", [P, 1], F32)
        list_no = sb("list_no", [P, LISTS], F32)
        spare = sb("spare", [P, LISTS], F32)
        share = sb("share", [P, TOKENS // P, TOPK], F32)

        dense = ExitStack()
        whi = sb("whi", [P, WCOLS], F32R, dense)
        wlo = sb("wlo", [P, WCOLS], F32R, dense)
        with ExitStack() as early:
            stage = sb("stage", [P, STAGES, STAGE], F32, early)
        hid_hi = sb("hid_hi", [P, FT, CHUNK], F32R, dense)
        hid_lo = sb("hid_lo", [P, FT, CHUNK], F32R, dense)
        feat_hi = sb("feat_hi", [P, KD, CHUNK], F32R, dense)
        feat_lo = sb("feat_lo", [P, KD, CHUNK], F32R, dense)
        y_hi = sb("y_hi", [P, KD, CHUNK], F32R, dense)
        y_lo = sb("y_lo", [P, KD, CHUNK], F32R, dense)
        xin = sb("xin", [P, TT, D], F32, dense)
        bnorm = sb("bnorm", [P, TT, D], F32, dense)
        rms = bnorm[:, :, :].rearrange("p t d -> p (t d)").rearrange("p (k n) -> p k n", k=KD)
        res = sb("res", [P, TT, D], F32, dense)
        x1 = sb("x1", [P, TT, D], F32, dense)
        xn2 = sb("xn2", [P, TT, D], F32, dense)
        ksb = sb("ksb", [P, KD, CHUNK], F32, dense)
        qsb = sb("qsb", [P, KD, CHUNK], F32, dense)
        vsb = sb("vsb", [P, KD, CHUNK], F32, dense)
        kvsum = sb("kvsum", [P, KD, CHUNK], F32, dense)
        wsum = sb("wsum", [P, KD, CHUNK], F32, dense)
        kvend = sb("kvend", [P, KD, BATCH], F32, dense)
        wend = sb("wend", [P, KD, BATCH], F32, dense)
        gate = sb("gate", [P, 2, CHUNK], F32, dense)
        hid = sb("hid", [P, 2, CHUNK], F32, dense)
        st1 = sb("st1", [P, TT, 6], F32, dense)
        mv1 = sb("mv1", [P, TT, 2], F32, dense)
        sc1 = sb("sc1", [P, 8, TT], F32, dense)
        st2 = sb("st2", [P, TT, 6], F32, dense)
        mv2 = sb("mv2", [P, TT, 2], F32, dense)
        sc2 = sb("sc2", [P, 4, TT], F32, dense)
        lgt = sb("lgt", [RW, CHUNK], F32, dense)
        lg = sb("lg", [P, TT, RW], F32, dense)
        top8 = sb("top8", [P, TT, 8], F32, dense)
        rt = sb("rt", [P, 12, TT * E], F32, dense)
        rsm = sb("rsm", [P, 4, TT], F32, dense)
        selb = sb("selb", [P, TT * E], BF16, dense)
        slot_f = sb("slot_f", [P, TT, TOPK], F32, dense)
        slot_u = sb("slot_u", [P, TT * TOPK], U32, dense)
        idval = sb("idval", [P, TT * TOPK], F32, dense)
        sig = sb("sig", [P, TT], F32, dense)
        dense.close()

        moe = ExitStack()
        up_hi = sb("up_hi", [P, E * KD * 2 * EI], F32R, moe)
        up_lo = sb("up_lo", [P, E * KD * 2 * EI], F32R, moe)
        dn_hi = sb("dn_hi", [EHP, E * 2 * D], F32R, moe)
        dn_lo = sb("dn_lo", [EHP, E * 2 * D], F32R, moe)
        wst = sb("wst", [P, WSTAGES, KD * 2 * EI + 2 * D], F32, moe)
        xg = sb("xg", [P, UNROLL, D], F32, moe)
        xt_hi = sb("xt_hi", [P, 2, D], F32R, moe)
        xt_lo = sb("xt_lo", [P, 2, D], F32R, moe)
        eg = sb("eg", [P, 2, EI], F32, moe)
        eh = sb("eh", [P, 2, EI], F32, moe)
        ht_hi = sb("ht_hi", [EHP, 2, D], F32R, moe)
        ht_lo = sb("ht_lo", [EHP, 2, D], F32R, moe)
        ysb = sb("ysb", [P, UNROLL, D], F32, moe)
        take_now = sb("take_now", [P, UNROLL], U32, moe)
        put_now = sb("put_now", [P, UNROLL], U32, moe)
        take = sb("take", [P, LISTS + UNROLL], U32, moe)
        put = sb("put", [P, LISTS], U32, moe)
        whose = sb("whose", [1, LISTS], mybir.dt.int32, moe)
        tab = sb("tab", [P, E * ROWS // P, P], F32, moe)
        pick = sb("pick", [P, E * ROWS // P, LISTS], F32, moe)
        ix = sb("ix", [P, 4, LISTS], F32, moe)
        em = sb("em", [P, 8, E], F32, moe)
        moe.close()
        TILES = TOKENS // P
        join = ExitStack()
        zin = sb("zin", [P, UNROLL, TOPK * D], F32, join)
        ain = sb("ain", [P, UNROLL, D], F32, join)
        sums = sb("sums", [P, UNROLL, D], F32, join)
        wk = sb("wk", [P, 2, TILES * E], F32, join)
        wm = sb("wm", [P, 3, TILES], F32, join)
        join.close()

        ring = ctx.enter_context(nc.psum_tensor("ring", [P, 3, 2, CHUNK], F32))
        scr = ctx.enter_context(nc.psum_tensor("scr", [P, 2, CHUNK], F32))

        pair_full = Signal(sem("pair_full"), ["stat", *FRONT_UP, "W0", "W1"], ["x", *SHARED_UP, "D0", "D1"],
                           ["b", "k", "q", "v"], order=FILLS)
        scr_full = Signal(sem("scr_full"), (), ["logit", "logit_t", "count"])
        pair_done = Signal(sem("pair_done"), [*FRONT_UP, "W0", "W1"], ["x", *SHARED_UP, "D0", "D1"], ["b"],
                           order=[e for e in FILLS if e not in ("stat", "k", "q", "v")])
        norm1 = Signal(sem("norm1"), (), (), ["stats", "aggr", "ve", "u0", "u1", "ue", "scale", "b"])
        norm2 = Signal(sem("norm2"), ["stats", "aggr", "ve", "xn2"])
        mid = Signal(sem("mid"), ["kr", "qr", "wv", "wsum", "wend", "kvsum", "kvend", "d", "rec0", "rec1", "y", "ylo"],
                     (), ["ksum", "klo", "qsum", "qlo"])
        routed = Signal(sem("routed"), (), ["lg", "keep", "top", "gt", "eq", "cgt", "need", "ceq", "ok", "tie", "sel", "selb",
                                            "rank", "rsel", "rkeep", "off0", "off1", "off2", "off3", "off4", "slot",
                                            *[f"{a}{k}" for k in range(TOPK) for a in ("m", "s")], "slotu", "id"])
        sig_done = Signal(sem("sig_done"), (), ["half"])
        act_done = Signal(sem("act_done"), ["stat"], (), ["k", "q", "v"])
        squares = Signal(sem("squares"), (), (), ["k", "q"])
        sq_hi = Signal(sem("sq_hi"), (), (), ["k", "q"])
        feat_top = Signal(sem("feat_top"), (), ["x"], ["b"])
        logit_out = Signal(sem("logit_out"), (), ["logit", "tanh"])
        rms_done = Signal(sem("rms_done"), ["lnk", "k", "q", "w", "eq", "yhi"])
        silu = Signal(sem("silu"), FRONT_UP, SHARED_UP, order=SHARED_UP + FRONT_UP)
        hid_top = Signal(sem("hid_top"), FRONT_UP, SHARED_UP, order=SHARED_UP + FRONT_UP)
        hid_low = Signal(sem("hid_low"), FRONT_UP, SHARED_UP, order=SHARED_UP + FRONT_UP)
        pows = Signal(sem("pows"), ["n2"], (), ["n1a", "n1b"], order=["n1a", "n1b", "n2"])
        resid = Signal(sem("resid"), (), (), ["rp", "nm", "res"])
        x_in = sem("x_in")
        xn2_out = sem("xn2_out")
        acc_out = sem("acc_out")
        id_out = sem("id_out")
        stage_in = [sem(f"stage_in{i}") for i in range(STAGES)]
        table_clear = sem("table_clear")
        whi_done = sem("whi_done")
        wlo_done = sem("wlo_done")
        consts = sem("consts")
        table_in = sem("table_in")
        lists = sem("lists")
        smalls = sem("smalls")
        lists_t = sem("lists_t")
        w_in = [sem(f"w_in{i}") for i in range(WSTAGES)]
        w_hi = sem("w_hi")
        w_lo = sem("w_lo")
        pad_rows = sem("pad_rows")
        got = [sem(f"got{i}") for i in range(UNROLL)]
        sent = [sem(f"sent{i}") for i in range(UNROLL)]
        take_set = sem("take_set")
        put_set = sem("put_set")
        xt_full = sem("xt_full")
        up_full = sem("up_full")
        ht_full = sem("ht_full")
        y_full = sem("y_full")
        xt_hi_done = sem("xt_hi_done")
        xt_lo_done = sem("xt_lo_done")
        silu_done = sem("silu_done")
        h_done = sem("h_done")
        ht_hi_done = sem("ht_hi_done")
        ht_lo_done = sem("ht_lo_done")
        y_done = sem("y_done")
        z_in = [sem(f"z_in{i}") for i in range(UNROLL)]
        o_out = [sem(f"o_out{i}") for i in range(UNROLL)]
        weights = sem("weights")
        expd = sem("expd")
        summed = sem("summed")
        dense_done = sem("dense_done")
        vconsts = sem("vconsts")

        def whi_c(c0, n):
            return whi[:, c0:c0 + n]

        def wlo_c(c0, n):
            return wlo[:, c0:c0 + n]

        def slot_of(turn, event):
            return (pair_full.start(Turn(turn.kind)) + pair_full.events[turn.kind].index(event)) % PAIRS

        def apart(eng, *waits):
            for _, n in waits:
                if not isinstance(n, int):
                    eng.compute_val(n)
            eng.wait_ge(consts, 1)
            for s, n in waits:
                eng.wait_ge(s, n)

        def expert_steps(eng, fn):
            for s in range(UNROLL):
                fn(s, s)
            with eng.Fori(0, LISTS // UNROLL - 1) as t:
                for u in range(UNROLL):
                    fn((t, u), u)
            for s in range(LISTS, LISTS + LEAD):
                fn(s, s % UNROLL)

        def num(s, c=0):
            return s + c if isinstance(s, int) else s[0] * UNROLL + (UNROLL + s[1] + c)

        def lap(s, u, back=0):
            if isinstance(s, int):
                return (s - back) // UNROLL + 1
            return s[0] + ((UNROLL + s[1] - back) // UNROLL + 1)

        def live(s, back):
            return 0 <= s - back < LISTS if isinstance(s, int) else True

        def steps(eng, fn, pre=True):
            if pre:
                fn(Turn("pre"))
            fn(Turn("first"))
            with eng.Fori(0, STEADY) as t:
                fn(Turn("steady", t))
            fn(Turn("tail"))
            fn(Turn("last"))

        block = ctx.enter_context(nc.Block())

        @block.sync
        def _(sp):
            sp.dma_start(xin[:, :, :], x[0:CHUNK, :].rearrange("(t p) d -> p t d", p=P)).then_inc(x_in, 16)
            for n, (a, b) in enumerate(PIECES):
                if n >= STAGES:
                    sp.wait_ge(whi_done, n - STAGES + 1)
                    sp.wait_ge(wlo_done, n - STAGES + 1)
                sp.dma_start(stage[:, n % STAGES, 0:b - a], w1[:, a:b]).then_inc(stage_in[n % STAGES], 16)

            def turn_(turn):
                c = {"first": 0, "steady": turn.t + 1, "tail": CHUNKS - 1, "last": CHUNKS}.get(turn.kind)
                if turn.front and turn.next:
                    sp.wait_ge(*resid.before(turn, "res"))
                    sp.dma_start(xin[:, :, :], x[bass.ds((c + 1) * CHUNK, CHUNK), :].rearrange("(t p) d -> p t d", p=P)
                                 ).then_inc(x_in, 16)
                if turn.shared:
                    sp.wait_ge(*pair_done.at(turn, "D1"))
                    sp.dma_start(acc[bass.ds((c - 1) * CHUNK, CHUNK), :].rearrange("(t p) d -> p t d", p=P),
                                 x1[:, :, :]).then_inc(acc_out, 16)
                if turn.front:
                    sp.wait_ge(*norm2.at(turn, "xn2"))
                    sp.dma_start(xn2_rows[bass.ds(c * CHUNK, CHUNK), :].rearrange("(t p) d -> p t d", p=P),
                                 xn2[:, :, :]).then_inc(xn2_out, 16)
            steps(sp, turn_)
            sp.wait_ge(acc_out, 16 * CHUNKS)
            sp.wait_ge(xn2_out, 16 * CHUNKS)
            sp.wait_ge(dense_done, 3)
            sp.wait_ge(id_out, CHUNKS * 16 * TT * TOPK)
            sp.dma_start(tab[:, :, :], ids.rearrange("(g p n) o -> p g (n o)", p=P, n=P)).then_inc(table_in, 16)
            nu = KD * 2 * EI
            for e in range(E):
                if e >= WSTAGES:
                    sp.wait_ge(w_lo, e - WSTAGES + 1)
                sp.dma_start(wst[:, e % WSTAGES, 0:nu], w_up[e, :, :]).then_inc(w_in[e % WSTAGES], 16)
                sp.dma_start(wst[0:EHP, e % WSTAGES, nu:nu + 2 * D], w_down[e, :, :]).then_inc(w_in[e % WSTAGES], 16)
            for i in range(UNROLL):
                sp.wait_ge(sent[i], 16 * (LISTS // UNROLL))

            def load(i, u):
                sp.dma_start(zin[:, u, :], picked[bass.ds(i * (P * TOPK), P * TOPK), :].rearrange("(p k) d -> p (k d)", k=TOPK)
                             ).then_inc(z_in[u], 16)
                sp.dma_start(ain[:, u, :], acc[bass.ds(i * P, P), :]).then_inc(z_in[u], 16)

            def store(i, u):
                sp.wait_ge(summed, i * TOPK + TOPK)
                sp.dma_start(out[bass.ds(i * P, P), :], sums[:, u, :]).then_inc(o_out[u], 16)
            for u in range(UNROLL):
                load(u, u)
            with sp.Fori(0, TILES // UNROLL - 1) as t:
                for u in range(UNROLL):
                    store(t * UNROLL + u, u)
                    load(t * UNROLL + (u + UNROLL), u)
            for u in range(UNROLL):
                store(TILES - UNROLL + u, u)
            for u in range(UNROLL):
                sp.wait_ge(o_out[u], 16 * (TILES // UNROLL))

        @block.tensor
        def _(pe):
            def three(out, lhs, rhs, first, last):
                pairs = [(0, 0), (0, 1), (1, 0)]
                for n, (a, b) in enumerate(pairs):
                    mm = pe.matmul(out, lhs[a], rhs[b], start=first and n == 0, stop=last and n == 2)
                return mm

            def bank_pair(turn, event):
                every = pair_full.events[turn.kind]
                n = every.index(event) - PAIRS
                if n >= 0:
                    was = every[n]
                    pe.wait_ge(*(pair_done if was in pair_done.events[turn.kind] else act_done).at(turn, was))
                elif turn.kind != "pre":
                    kind = KINDS[KINDS.index(turn.kind) - 1]
                    was = pair_full.events[kind][n]
                    pe.wait_ge(*(pair_done if was in pair_done.events[kind] else act_done).before(turn, was))
                return slot_of(turn, event)

            def proj(turn, event, cols, width, rhi, rlo):
                s = bank_pair(turn, event)
                for h, c in enumerate(cols):
                    for k in range(KD):
                        mm = three(ring[:, s, h, :], (whi_c(c + k * width, P), wlo_c(c + k * width, P)),
                                   (rhi[:, k, :], rlo[:, k, :]), k == 0, k == KD - 1)
                mm.then_inc(*pair_full.did(turn, event))

            def down(turn, event, tiles, w0, hidden):
                s = bank_pair(turn, event)
                n = len(hidden)
                for h, t in enumerate(tiles):
                    for f in range(n):
                        if t == 0:
                            pe.wait_ge(*hid_low.at(turn, hidden[f]))
                        mm = three(ring[:, s, h, 0:D], (hid_hi[:, f, t * P:(t + 1) * P], hid_lo[:, f, t * P:(t + 1) * P]),
                                   (whi_c(w0 + f * D, D), wlo_c(w0 + f * D, D)), f == 0, f == n - 1)
                mm.then_inc(*pair_full.did(turn, event))

            def turn_columns(turn, event, rows):
                s = bank_pair(turn, event)
                for k in range(KD):
                    for t in range(TT):
                        mm = pe.transpose(ring[:, s, k, t * P:(t + 1) * P], rows[:, t, k * P:(k + 1) * P], ident[:, :])
                mm.then_inc(*pair_full.did(turn, event))

            pe.wait_ge(consts, 1)
            pe.wait_ge(vconsts, 1)

            def turn_(turn):
                def shared_up(*tiles):
                    for f in tiles:
                        proj(turn, f"G{f}", (SG0 + SIP + f * P, SG0 + f * P), 2 * SIP, feat_hi, feat_lo)

                def front_up(*tiles):
                    for f in tiles:
                        proj(turn, f"S{f}", (SW0 + f * P, SW0 + FF + f * P), 2 * FF, y_hi, y_lo)

                def counts():
                    pe.wait_ge(*routed.at(turn, "selb"))
                    pe.matmul(scr[:, 1, 128:192], earlier[:, :], selb[:, :], start=True, stop=True)
                    pe.matmul(scr[:, 1, 192:256], ones_b[:, :], selb[:, :], start=True, stop=True
                              ).then_inc(*scr_full.did(turn, "count"))

                if turn.shared:
                    pe.wait_ge(*norm2.before(turn, "xn2"))
                    turn_columns(turn, "x", xn2)
                if turn.front:
                    s = bank_pair(turn, "stat")
                    pe.wait_ge(*mid.before(turn, "qlo"))
                    for h in range(2):
                        pe.matmul(ring[:, s, h, :], ones_r[:, :], y_hi[:, h, :], start=True, stop=False)
                        mm = pe.matmul(ring[:, s, h, :], ones_r[:, :], y_lo[:, h, :], start=False, stop=True)
                    mm.then_inc(*pair_full.did(turn, "stat"))
                if turn.shared:
                    pe.wait_ge(*pair_done.at(turn, "x"))
                    for k in range(KD):
                        mm = three(scr[0:RW, 0, :], (whi_c(RT0 + k * RW, RW), wlo_c(RT0 + k * RW, RW)),
                                   (feat_hi[:, k, :], feat_lo[:, k, :]), k == 0, k == KD - 1)
                    mm.then_inc(*scr_full.did(turn, "logit"))
                    shared_up(0, 1)
                    apart(pe, logit_out.at(turn, "logit"))
                    for t in range(TT):
                        mm = pe.transpose(scr[:, 1, t * RW:(t + 1) * RW], lgt[:, t * P:(t + 1) * P], ident[0:RW, 0:RW])
                    mm.then_inc(*scr_full.did(turn, "logit_t"))
                    shared_up(2, 3, 4)
                    if not turn.front:
                        counts()
                    shared_up(5)
                    down(turn, "D0", (0, 1), SD0, SHARED_UP)
                    down(turn, "D1", (2, 3), SD0, SHARED_UP)
                if turn.front:
                    if turn.kind == "first":
                        pe.wait_ge(wlo_done, len(PIECES))
                    pe.wait_ge(*mid.at(turn, "ylo"))
                    front_up(0, 1, 2)
                    if turn.shared:
                        counts()
                    front_up(3, 4, 5, 6, 7)
                if turn.next:
                    pe.wait_ge(*norm1.at(turn, "b"))
                    turn_columns(turn, "b", bnorm)
                if turn.front:
                    down(turn, "W0", (0, 1), WO0, FRONT_UP)
                    down(turn, "W1", (2, 3), WO0, FRONT_UP)
                if turn.next:
                    if turn.kind == "pre":
                        pe.wait_ge(wlo_done, 1)
                    pe.wait_ge(*pair_done.at(turn, "b"))
                    for n, part in ((1, "k"), (0, "q"), (2, "v")):
                        proj(turn, part, (QKV0 + n * D, QKV0 + n * D + P), 3 * D, feat_hi, feat_lo)
            steps(pe, turn_)

            pe.wait_ge(table_in, 16)
            pe.wait_ge(lists, 8)
            groups = E * ROWS // P
            for g in range(groups):
                mm = pe.matmul(scr[:, 0, 0:LISTS], tab[:, g, :], pick[:, g, :], start=g == 0, stop=g == groups - 1)
            mm.then_inc(lists_t, 1)
            pe.wait_ge(lists, 14)
            pe.wait_ge(w_lo, E)
            pe.wait_ge(pad_rows, 2)

            def step(s, u):
                if live(s, 0):
                    b = u % 2
                    pe.wait_ge(got[u], lap(s, u) * 16)
                    if not isinstance(s, int) or s >= 2:
                        pe.wait_ge(xt_lo_done, num(s, -1))
                    for k in range(KD):
                        mm = pe.transpose(ring[:, 0, b, k * P:(k + 1) * P], xg[:, u, k * P:(k + 1) * P], ident[:, :])
                    mm.then_inc(xt_full, 1)
                if live(s, 1):
                    b = (u - 1) % 2
                    pe.wait_ge(consts, 1)
                    pe.wait_ge(xt_lo_done, num(s, 0))
                    if not isinstance(s, int) or s >= 3:
                        pe.wait_ge(h_done, num(s, -2))
                    e = pe.value_load(whose[0:1, bass.ds(num(s, -1), 1)], min_val=0, max_val=E - 1)
                    for k in range(KD):
                        lhs = (xt_hi[:, b, k * P:(k + 1) * P], xt_lo[:, b, k * P:(k + 1) * P])
                        at = e * (KD * 2 * EI) + k * 2 * EI
                        mm = three(ring[:, 1, b, 0:2 * EI], lhs, (up_hi[:, bass.ds(at, 2 * EI)], up_lo[:, bass.ds(at, 2 * EI)]),
                                   k == 0, k == KD - 1)
                    mm.then_inc(up_full, 1)
                if live(s, 2):
                    b = (u - 2) % 2
                    pe.wait_ge(h_done, num(s, -1))
                    if not isinstance(s, int) or s >= 4:
                        pe.wait_ge(ht_lo_done, num(s, -3))
                    for k in range(2):
                        mm = pe.transpose(ring[0:EH, 2, b, k * P:(k + 1) * P], eh[:, b, k * EH:(k + 1) * EH], ident[:, :])
                    mm.then_inc(ht_full, 1)
                if live(s, 3):
                    b = (u - 3) % 2
                    pe.wait_ge(consts, 1)
                    pe.wait_ge(ht_lo_done, num(s, -2))
                    if not isinstance(s, int) or s >= 5:
                        pe.wait_ge(y_done, num(s, -4))
                    e = pe.value_load(whose[0:1, bass.ds(num(s, -3), 1)], min_val=0, max_val=E - 1)
                    for k in range(2):
                        lhs = (ht_hi[:, b, k * P:(k + 1) * P], ht_lo[:, b, k * P:(k + 1) * P])
                        at = e * (2 * D) + k * D
                        mm = three(scr[:, b, 0:D], lhs, (dn_hi[:, bass.ds(at, D)], dn_lo[:, bass.ds(at, D)]), k == 0, k == 1)
                    mm.then_inc(y_full, 1)
            expert_steps(pe, step)

        @block.scalar
        def _(act):
            def upper(pieces):
                for n in pieces:
                    a, b = PIECES[n]
                    act.wait_ge(stage_in[n % STAGES], 16 * (n // STAGES + 1))
                    nc.scalar.copy(whi[:, a:b], stage[:, n % STAGES, 0:b - a]).then_inc(whi_done, 1)

            def hidden(turn, events, extra=None):
                every = silu.events[turn.kind]

                def top(event):
                    f = int(event[1:])
                    act.wait_ge(*pair_done.at(turn, event))
                    nc.scalar.copy(hid_hi[:, f, :], hid[:, every.index(event) % 2, :]).then_inc(*hid_top.did(turn, event))
                for n, event in enumerate(events):
                    act.wait_ge(*pair_full.at(turn, event))
                    i = every.index(event)
                    if i >= 2:
                        act.wait_ge(*pair_done.at(turn, every[i - 2]))
                    nc.scalar.activation(gate[:, i % 2, :], ring[:, slot_of(turn, event), 1, :], ACT.Silu
                                         ).then_inc(*silu.did(turn, event))
                    if n:
                        top(events[n - 1])
                    if extra and n == 2:
                        extra()
                top(events[-1])

            def turned(turn, event):
                act.wait_ge(*pair_full.at(turn, event))
                nc.scalar.copy(feat_hi[:, :, :], ring[:, slot_of(turn, event), :, :]).then_inc(*feat_top.did(turn, event))

            upper([0])
            act.wait_ge(vconsts, 1)

            def turn_(turn):
                def half_tanh():
                    act.wait_ge(*scr_full.at(turn, "logit_t"))
                    nc.scalar.activation(sig[:, :], scr[:, 1, 0:TT * RW].rearrange("p (t r) -> p t r", t=TT)[:, :, E],
                                         ACT.Tanh, scale=0.5).then_inc(*logit_out.did(turn, "tanh"))

                if turn.shared:
                    turned(turn, "x")
                if turn.front:
                    act.wait_ge(*pair_full.at(turn, "stat"))
                    s = slot_of(turn, "stat")
                    nc.scalar.activation(rms[:, 0, :], ring[:, s, 0, :], ACT.Ln, bias=eps_c[:, 0:1], scale=1.0 / D
                                         ).then_inc(*rms_done.did(turn, "lnk"))
                    nc.scalar.activation(rms[:, 1, :], ring[:, s, 1, :], ACT.Ln, bias=eps_c[:, 0:1], scale=1.0 / D
                                         ).then_inc(*act_done.did(turn, "stat"))
                    act.wait_ge(*rms_done.at(turn, "lnk"))
                    nc.scalar.activation(rms[:, 0, :], rms[:, 0, :], ACT.Exp, scale=-0.5).then_inc(*rms_done.did(turn, "k"))
                    act.wait_ge(*act_done.at(turn, "stat"))
                    nc.scalar.activation(rms[:, 1, :], rms[:, 1, :], ACT.Exp, scale=-0.5).then_inc(*rms_done.did(turn, "q"))
                if turn.shared:
                    act.wait_ge(*scr_full.at(turn, "logit"))
                    nc.scalar.copy(lgt[:, :], scr[0:RW, 0, :]).then_inc(*logit_out.did(turn, "logit"))
                if turn.front:
                    act.wait_ge(*mid.at(turn, "kr"))
                    nc.scalar.activation(ksb[:, :, :], ksb[:, :, :], ACT.Exp).then_inc(*rms_done.did(turn, "w"))
                    act.wait_ge(*mid.at(turn, "qr"))
                    nc.scalar.activation(qsb[:, :, :], qsb[:, :, :], ACT.Exp, scale=-1.0).then_inc(*rms_done.did(turn, "eq"))
                if turn.shared:
                    hidden(turn, SHARED_UP, half_tanh)
                if turn.front:
                    act.wait_ge(*mid.at(turn, "y"))
                    nc.scalar.copy(y_hi[:, :, :], kvsum[:, :, :]).then_inc(*rms_done.did(turn, "yhi"))
                    hidden(turn, FRONT_UP)
                if turn.next:
                    turned(turn, "b")

                    def take(part, to):
                        nc.scalar.copy(to[:, :, :], ring[:, slot_of(turn, part), :, :]).then_inc(*act_done.did(turn, part))

                    def square(part, to):
                        act.wait_ge(*pair_full.at(turn, part))
                        nc.scalar.activation(to[:, :, :], ring[:, slot_of(turn, part), :, :], ACT.Square
                                             ).then_inc(*squares.did(turn, part))

                    def upper_sum(part, of):
                        act.wait_ge(*mid.at(turn, part + "sum"))
                        nc.scalar.copy(y_hi[:, "kq".index(part), :], of[:, 0, :]).then_inc(*sq_hi.did(turn, part))
                    square("k", kvsum)
                    take("k", ksb)
                    square("q", wsum)
                    upper_sum("k", kvsum)
                    upper_sum("q", wsum)
                    take("q", qsb)
                    act.wait_ge(*pair_full.at(turn, "v"))
                    take("v", vsb)
                if turn.kind == "pre":
                    upper(range(1, len(PIECES)))
            steps(act, turn_)
            act.wait_ge(*rms_done.at(Turn("tail"), "yhi"))
            act.sem_inc(dense_done, 1)

            nu = KD * 2 * EI
            for e in range(E):
                act.wait_ge(w_in[e % WSTAGES], 32 * (e // WSTAGES + 1))
                nc.scalar.copy(up_hi[:, e * nu:(e + 1) * nu], wst[:, e % WSTAGES, 0:nu]).then_inc(w_hi, 1)
                nc.scalar.copy(dn_hi[:, e * 2 * D:(e + 1) * 2 * D], wst[0:EHP, e % WSTAGES, nu:nu + 2 * D]).then_inc(w_hi, 1)

            def step(s, u):
                if live(s, 0):
                    b = u % 2
                    act.wait_ge(xt_full, num(s, 1))
                    if not isinstance(s, int) or s >= 2:
                        act.wait_ge(up_full, num(s, -1))
                    nc.scalar.copy(xt_hi[:, b, :], ring[:, 0, b, 0:D]).then_inc(xt_hi_done, 1)
                if live(s, 1):
                    b = (u - 1) % 2
                    act.wait_ge(up_full, num(s, 0))
                    if not isinstance(s, int) or s >= 3:
                        act.wait_ge(h_done, num(s, -2))
                    nc.scalar.activation(eg[:, b, :], ring[:, 1, b, 0:EI], ACT.Silu).then_inc(silu_done, 1)
                if live(s, 2):
                    b = (u - 2) % 2
                    act.wait_ge(ht_full, num(s, -1))
                    if not isinstance(s, int) or s >= 4:
                        act.wait_ge(y_full, num(s, -3))
                    nc.scalar.copy(ht_hi[0:EH, b, :], ring[0:EH, 2, b, 0:D]).then_inc(ht_hi_done, 1)
                if live(s, 3):
                    b = (u - 3) % 2
                    act.wait_ge(y_full, num(s, -2))
                    if not isinstance(s, int) or s >= LEAD + UNROLL:
                        act.wait_ge(sent[(u - 3) % UNROLL], (lap(s, u, 3) - 1) * 16)
                    nc.scalar.copy(ysb[:, (u - 3) % UNROLL, :], scr[:, b, 0:D]).then_inc(y_done, 1)
            expert_steps(act, step)
            act.wait_ge(weights, 2)
            nc.scalar.activation(wk[:, 0, :], wk[:, 0, :], ACT.Exp).then_inc(expd, 1)

        @block.vector
        def _(dve):
            V = nc.vector
            V.memset(ones_r[:, :].bitcast(F32), 1.0)
            V.memset(ones_b[:, :], 1.0)
            V.memset(ones_row[:, :], 1.0)
            V.memset(power[:, :], -0.5)
            V.memset(eps_c[:, :], RMS_EPS)
            V.memset(kvend[:, :, :], 0.0)
            V.memset(wend[:, :, :], DEN_EPS).then_inc(vconsts, 1)

            def split_lo(turn, event):
                dve.wait_ge(*feat_top.at(turn, event))
                V.tensor_tensor(feat_lo[:, :, :], ring[:, slot_of(turn, event), :, :], feat_hi[:, :, :].bitcast(F32), ALU.subtract
                                ).then_inc(*pair_done.did(turn, event))

            def first_norm(turn, part):
                if part == 0:
                    c = {"pre": 0, "first": 1, "steady": turn.t + 2}[turn.kind]
                    dve.wait_ge(x_in, (c + 1) * 16)
                    for t in range(TT):
                        i = V.bn_stats(st1[:, t, :], xin[:, t, :])
                    i.then_inc(*norm1.did(turn, "stats"))
                    apart(dve, norm1.at(turn, "stats"))
                    for t in range(TT):
                        i = V.bn_aggr(mv1[:, t, :], st1[:, t, :])
                    i.then_inc(*norm1.did(turn, "aggr"))
                    dve.wait_ge(*norm1.at(turn, "aggr"))
                    V.tensor_scalar(sc1[:, 0, :], mv1[:, :, 1], LN_EPS, None, ALU.add).then_inc(*norm1.did(turn, "ve"))
                if part == 1:
                    dve.wait_ge(*pows.at(turn, "n1a"))
                    V.tensor_tensor(sc1[:, 2, :], mv1[:, :, 1], sc1[:, 1, :], ALU.mult).then_inc(*norm1.did(turn, "u0"))
                    dve.wait_ge(*norm1.at(turn, "u0"))
                    V.tensor_tensor(sc1[:, 3, :], sc1[:, 2, :], sc1[:, 1, :], ALU.mult).then_inc(*norm1.did(turn, "u1"))
                    dve.wait_ge(*norm1.at(turn, "u1"))
                    V.tensor_scalar(sc1[:, 4, :], sc1[:, 3, :], RMS_EPS, None, ALU.add).then_inc(*norm1.did(turn, "ue"))
                if part == 2:
                    dve.wait_ge(*pows.at(turn, "n1b"))
                    V.tensor_tensor(sc1[:, 6, :], sc1[:, 1, :], sc1[:, 5, :], ALU.mult).then_inc(*norm1.did(turn, "scale"))
                    dve.wait_ge(*norm1.at(turn, "scale"))
                    for t in range(TT):
                        i = V.tensor_scalar(bnorm[:, t, :], xin[:, t, :], mv1[:, t, 0:1], sc1[:, 6, t:t + 1],
                                            ALU.subtract, ALU.mult)
                    i.then_inc(*norm1.did(turn, "b"))

            def product(turn, event):
                i = silu.events[turn.kind].index(event)
                dve.wait_ge(*silu.at(turn, event))
                if i >= 2:
                    was = silu.events[turn.kind][i - 2]
                    dve.wait_ge(*hid_top.at(turn, was))
                    dve.wait_ge(*hid_low.at(turn, was))
                elif turn.kind != "first":
                    dve.wait_ge(*hid_low.before(turn, f"S{FT - 2 + i}"))
                V.tensor_tensor(hid[:, i % 2, :], gate[:, i % 2, :], ring[:, slot_of(turn, event), 0, :], ALU.mult
                                ).then_inc(*pair_done.did(turn, event))

            def bc(ap, n):
                return ap.unsqueeze(2).to_broadcast([P, TT, n])

            def r3(i):
                return rt[:, i, :].rearrange("p (t e) -> p t e", t=TT)

            GT, EQ, CEQ, OK, TIE, SEL, RANK, RSEL, OFF, SLOT, TMP = range(11)

            def link(turn, ins, event):
                ins.then_inc(*routed.did(turn, event))
                dve.wait_ge(*routed.at(turn, event))

            def route_a(turn):
                dve.wait_ge(*logit_out.at(turn, "tanh"))
                dve.wait_ge(table_clear, 16)
                link(turn, V.tensor_copy(lg[:, :, :], scr[:, 1, 0:TT * RW].rearrange("p (t r) -> p t r", t=TT)), "lg")
                c = {"steady": turn.t, "tail": CHUNKS - 2, "last": CHUNKS - 1}[turn.kind]
                l = lg[:, :, 0:E]
                V.tensor_copy(logits_all[:, bass.ds(c, 1), :, :].rearrange("p c t e -> p (c t) e"), l
                              ).then_inc(*routed.did(turn, "keep"))
                for t in range(TT):
                    i = V.max(top8[:, t, :], lg[:, t, 0:E])
                link(turn, i, "top")
                fourth = top8[:, :, TOPK - 1:TOPK].to_broadcast([P, TT, E])
                V.tensor_tensor(r3(GT), l, fourth, ALU.is_gt).then_inc(*routed.did(turn, "gt"))
                link(turn, V.tensor_tensor(r3(EQ), l, fourth, ALU.is_equal), "eq")
                link(turn, V.tensor_reduce(rsm[:, 0, :], r3(GT), AX_X, ALU.add), "cgt")
                link(turn, V.tensor_scalar(rsm[:, 1, :], rsm[:, 0, :], -1.0, float(TOPK), ALU.mult, ALU.add), "need")
                link(turn, V.tensor_tensor_scan(rt[:, CEQ, :], notfirst[:, :], rt[:, EQ, :], 0.0, ALU.mult, ALU.add), "ceq")
                link(turn, V.tensor_tensor(r3(OK), r3(CEQ), bc(rsm[:, 1, :], E), ALU.is_le), "ok")
                link(turn, V.tensor_tensor(rt[:, TIE, :], rt[:, EQ, :], rt[:, OK, :], ALU.mult), "tie")
                link(turn, V.tensor_tensor(rt[:, SEL, :], rt[:, GT, :], rt[:, TIE, :], ALU.add), "sel")
                V.tensor_copy(selb[:, :], rt[:, SEL, :]).then_inc(*routed.did(turn, "selb"))
                link(turn, V.tensor_tensor_scan(rt[:, RANK, :], notfirst[:, :], rt[:, SEL, :], 0.0, ALU.mult, ALU.add), "rank")
                link(turn, V.tensor_tensor(rt[:, RSEL, :], rt[:, RANK, :], rt[:, SEL, :], ALU.mult), "rsel")
                V.tensor_copy(rank_all[:, bass.ds(c, 1), :, :].rearrange("p c t e -> p (c t e)"), rt[:, RSEL, :]
                              ).then_inc(*routed.did(turn, "rkeep"))

            def route_b(turn):
                dve.wait_ge(*scr_full.at(turn, "count"))
                link(turn, V.tensor_copy(rt[:, OFF, 0:E], filled[:, :]), "off0")
                for t in range(1, TT + 1):
                    to = rt[:, OFF, t * E:(t + 1) * E] if t < TT else filled[:, :]
                    link(turn, V.tensor_tensor(to, rt[:, OFF, (t - 1) * E:t * E], scr[:, 1, 192 + (t - 1) * E:192 + t * E],
                                               ALU.add), f"off{t}")
                link(turn, V.tensor_tensor(rt[:, SLOT, :], rt[:, OFF, :], scr[:, 1, 128:192], ALU.add), "slot")
                for k in range(TOPK):
                    link(turn, V.scalar_tensor_tensor(rt[:, TMP, :], rt[:, RSEL, :], float(k + 1), rt[:, SLOT, :],
                                                      ALU.is_equal, ALU.mult), f"m{k}")
                    link(turn, V.tensor_reduce(slot_f[:, :, k], r3(TMP), AX_X, ALU.add), f"s{k}")
                c = {"steady": turn.t, "tail": CHUNKS - 2, "last": CHUNKS - 1}[turn.kind]
                if turn.kind == "steady":
                    dve.wait_ge(id_out, c * (16 * TT * TOPK))
                else:
                    dve.wait_ge(id_out, c * 16 * TT * TOPK)
                V.tensor_copy(slot_u[:, :], slot_f[:, :, :].rearrange("p t k -> p (t k)")).then_inc(*routed.did(turn, "slotu"))
                V.tensor_scalar(idval[:, :], idval[:, :], float(TOPK * CHUNK), None, ALU.add).then_inc(*routed.did(turn, "id"))

            def lower_weights(pieces):
                for n in pieces:
                    a, b = PIECES[n]
                    dve.wait_ge(whi_done, n + 1)
                    V.tensor_tensor(wlo[:, a:b], stage[:, n % STAGES, 0:b - a], whi[:, a:b].bitcast(F32), ALU.subtract
                                    ).then_inc(wlo_done, 1)
            lower_weights([0])
            dve.wait_ge(consts, 1)
            dve.wait_ge(vconsts, 1)

            def turn_(turn):
                def shared_products(*tiles):
                    if turn.shared:
                        for f in tiles:
                            product(turn, f"G{f}")

                if turn.shared:
                    split_lo(turn, "x")
                if turn.shared and not turn.front:
                    shared_products(0, 1, 2)
                    route_a(turn)
                    shared_products(3, 4)
                    route_b(turn)
                    shared_products(5)
                if turn.front:
                    for h, (part, to) in enumerate((("k", ksb), ("q", qsb))):
                        dve.wait_ge(*rms_done.at(turn, part))
                        if turn.kind == "first" and not h:
                            dve.wait_ge(*act_done.before(turn, "v"))
                        V.tensor_tensor(to[:, :, :], to[:, :, :], rms[:, h, :].unsqueeze(1).to_broadcast([P, KD, CHUNK]),
                                        ALU.mult).then_inc(*mid.did(turn, part + "r"))
                    dve.wait_ge(*rms_done.at(turn, "w"))
                    V.tensor_tensor(vsb[:, :, :], vsb[:, :, :], ksb[:, :, :], ALU.mult).then_inc(*mid.did(turn, "wv"))

                    def scans(to, of, end, name):
                        for k in range(KD):
                            for b in range(BATCH):
                                i = V.tensor_tensor_scan(to[:, k, b * RUN:(b + 1) * RUN], ones_row[:, :],
                                                         of[:, k, b * RUN:(b + 1) * RUN], end[:, k, b:b + 1], ALU.mult, ALU.add)
                        i.then_inc(*mid.did(turn, name))
                        dve.wait_ge(*mid.at(turn, name))
                        V.tensor_copy(end[:, :, :], to[:, :, :].rearrange("p k (b r) -> p k b r", b=BATCH)[:, :, :, RUN - 1]
                                      ).then_inc(*mid.did(turn, name[:-3] + "end"))
                    if turn.kind != "first":
                        dve.wait_ge(*mid.before(turn, "kvend"))
                    scans(wsum, ksb, wend, "wsum")
                    dve.wait_ge(*mid.at(turn, "wv"))
                    scans(kvsum, vsb, kvend, "kvsum")
                    shared_products(0)
                    dve.wait_ge(*rms_done.at(turn, "eq"))
                    V.scalar_tensor_tensor(qsb[:, :, :], qsb[:, :, :], 1.0, wsum[:, :, :], ALU.add, ALU.mult
                                           ).then_inc(*mid.did(turn, "d"))
                    shared_products(1)
                    dve.wait_ge(*mid.at(turn, "d"))
                    V.reciprocal(ksb[:, 0, :], qsb[:, 0, :]).then_inc(*mid.did(turn, "rec0"))
                    shared_products(2)
                    V.reciprocal(ksb[:, 1, :], qsb[:, 1, :]).then_inc(*mid.did(turn, "rec1"))
                    shared_products(3)
                    dve.wait_ge(*mid.at(turn, "rec1"))
                    V.tensor_tensor(kvsum[:, :, :], kvsum[:, :, :], ksb[:, :, :], ALU.mult).then_inc(*mid.did(turn, "y"))
                    shared_products(4, 5)
                    dve.wait_ge(*rms_done.at(turn, "yhi"))
                    V.tensor_tensor(y_lo[:, :, :], kvsum[:, :, :], y_hi[:, :, :].bitcast(F32), ALU.subtract
                                    ).then_inc(*mid.did(turn, "ylo"))
                if turn.shared:
                    dve.wait_ge(*logit_out.at(turn, "tanh"))
                    V.tensor_scalar(sig[:, :], sig[:, :], 0.5, 0.5, ALU.mult, ALU.add).then_inc(*sig_done.did(turn, "half"))
                    dve.wait_ge(*sig_done.at(turn, "half"))
                    for d in range(2):
                        dve.wait_ge(*pair_full.at(turn, f"D{d}"))
                        for h in range(2):
                            t = 2 * d + h
                            i = V.scalar_tensor_tensor(x1[:, t, :], ring[:, slot_of(turn, f"D{d}"), h, 0:D], sig[:, t:t + 1],
                                                       x1[:, t, :], ALU.mult, ALU.add)
                        i.then_inc(*pair_done.did(turn, f"D{d}"))
                if turn.front:
                    for f in range(FT):
                        product(turn, f"S{f}")
                        if turn.shared and f == 0:
                            route_a(turn)
                        if turn.shared and f == 3:
                            route_b(turn)
                        if turn.next and f in (4, 5, 6):
                            first_norm(turn, f - 4)
                elif turn.next:
                    for part in range(3):
                        first_norm(turn, part)
                if turn.next:
                    split_lo(turn, "b")
                if turn.front:
                    if turn.kind != "first":
                        dve.wait_ge(acc_out, (turn.t + 1) * 16 if turn.kind == "steady" else (CHUNKS - 1) * 16)
                    dve.wait_ge(*resid.before(turn, "res"))
                    for w in range(2):
                        dve.wait_ge(*pair_full.at(turn, f"W{w}"))
                        V.tensor_tensor(x1[:, 2 * w:2 * w + 2, :], res[:, 2 * w:2 * w + 2, :],
                                        ring[:, slot_of(turn, f"W{w}"), :, 0:D], ALU.add).then_inc(*pair_done.did(turn, f"W{w}"))
                        dve.wait_ge(*pair_done.at(turn, f"W{w}"))
                        for t in range(2 * w, 2 * w + 2):
                            i = V.bn_stats(st2[:, t, :], x1[:, t, :])
                    i.then_inc(*norm2.did(turn, "stats"))
                    apart(dve, norm2.at(turn, "stats"))
                    for t in range(TT):
                        i = V.bn_aggr(mv2[:, t, :], st2[:, t, :])
                    i.then_inc(*norm2.did(turn, "aggr"))
                    dve.wait_ge(*norm2.at(turn, "aggr"))
                    V.tensor_scalar(sc2[:, 0, :], mv2[:, :, 1], LN_EPS, None, ALU.add).then_inc(*norm2.did(turn, "ve"))
                    dve.wait_ge(*pows.at(turn, "n2"))
                    if turn.kind != "first":
                        dve.wait_ge(xn2_out, (turn.t + 1) * 16 if turn.kind == "steady" else (CHUNKS - 1) * 16)
                        dve.wait_ge(*pair_full.at(turn, "x"))
                    for t in range(TT):
                        i = V.tensor_scalar(xn2[:, t, :], x1[:, t, :], mv2[:, t, 0:1], sc2[:, 1, t:t + 1],
                                            ALU.subtract, ALU.mult)
                    i.then_inc(*norm2.did(turn, "xn2"))
                if turn.next:
                    def square_sum(part, of):
                        dve.wait_ge(*squares.at(turn, part))
                        V.tensor_tensor(of[:, 0, :], of[:, 0, :], of[:, 1, :], ALU.add).then_inc(*mid.did(turn, part + "sum"))

                    def lower_sum(part, of):
                        h = "kq".index(part)
                        dve.wait_ge(*sq_hi.at(turn, part))
                        V.tensor_tensor(y_lo[:, h, :], of[:, 0, :], y_hi[:, h, :].bitcast(F32), ALU.subtract
                                        ).then_inc(*mid.did(turn, part + "lo"))
                    square_sum("k", kvsum)
                    lower_sum("k", kvsum)
                    square_sum("q", wsum)
                    lower_sum("q", wsum)
                if turn.kind == "pre":
                    lower_weights(range(1, len(PIECES)))
            steps(dve, turn_)
            dve.wait_ge(*norm2.at(Turn("tail"), "xn2"))
            dve.wait_ge(*pair_done.at(Turn("last"), "D1"))
            dve.wait_ge(*routed.at(Turn("last"), "id"))
            dve.sem_inc(dense_done, 1)

            done = [0]

            def note(ins):
                done[0] += 1
                ins.then_inc(lists, 1)
                dve.wait_ge(lists, done[0])
            dve.wait_ge(acc_out, 16 * CHUNKS)
            dve.wait_ge(id_out, CHUNKS * 16 * TT * TOPK)
            dve.wait_ge(dense_done, 3)
            NTOK, NLIST, UPTO, BASE = range(4)
            lots = pick[:, :, :].rearrange("p g l -> p (g l)")[:, 0:E * ROWS]
            note(V.tensor_tensor(em[:, NTOK, :], filled[:, :], first_slot[:, :], ALU.subtract))
            note(V.tensor_tensor(lots.rearrange("p (e j) -> p e j", e=E), em[:, NTOK, :].unsqueeze(2).to_broadcast([P, E, ROWS]),
                                 list_start[:, :].unsqueeze(1).to_broadcast([P, E, ROWS]), ALU.is_gt))
            note(V.tensor_reduce(em[:, NLIST, :], lots.rearrange("p (e j) -> p e j", e=E), AX_X, ALU.add))
            note(V.tensor_tensor_scan(em[:, UPTO, :], ones_row[:, 0:E], em[:, NLIST, :], 0.0, ALU.mult, ALU.add))
            note(V.tensor_tensor(em[:, BASE, :], em[:, UPTO, :], em[:, NLIST, :], ALU.subtract))
            mask = quarter[:, :].unsqueeze(1).to_broadcast([P, 4, 4])
            V.tensor_tensor(em[:, 4, :].rearrange("p (g q) -> p g q", g=4), em[:, BASE, :].rearrange("p (g q) -> p g q", g=4), mask, ALU.mult)
            note(V.tensor_tensor(em[:, 5, :].rearrange("p (g q) -> p g q", g=4), em[:, NLIST, :].rearrange("p (g q) -> p g q", g=4), mask, ALU.mult))
            V.tensor_reduce(em[:, 6, 0:4], em[:, 4, :].rearrange("p (g q) -> p g q", g=4), AX_X, ALU.add)
            note(V.tensor_reduce(em[:, 6, 4:8], em[:, 5, :].rearrange("p (g q) -> p g q", g=4), AX_X, ALU.add))
            link2 = [0]

            def small(ins):
                link2[0] += 1
                ins.then_inc(smalls, 1)
                dve.wait_ge(smalls, link2[0])
            V.tensor_scalar(em[:, 7, 0:4], em[:, 6, 0:4], in_quarter[:, 0:1], 1.0, ALU.add, ALU.add)
            small(V.tensor_scalar(em[:, 7, 4:8], em[:, 6, 4:8], in_quarter[:, 0:1], None, ALU.is_gt))
            small(V.tensor_tensor(em[:, 7, 8:12], em[:, 7, 0:4], em[:, 7, 4:8], ALU.mult))
            small(V.tensor_scalar(em[:, 7, 12:16], em[:, 7, 8:12], -1.0, None, ALU.add))
            for g in range(4):
                i = V.tensor_scalar(pick[:, g, :], list_no[:, :], em[:, 7, 12 + g:13 + g], None, ALU.is_equal)
            note(i)
            assert done[0] == 8
            for e in range(E):
                last = small if e < E - 1 else note
                was = ix[0:1, 0, :] if e else None
                if e == 0:
                    last(V.tensor_scalar(ix[0:1, 0, :], list_no[0:1, :], em[0:1, BASE, 0:1], None, ALU.is_ge))
                else:
                    last(V.scalar_tensor_tensor(ix[0:1, 0, :], list_no[0:1, :], em[0:1, BASE, e:e + 1], was, ALU.is_ge, ALU.add))
            note(V.tensor_scalar(whose[:, :], ix[0:1, 0, :], -1.0, None, ALU.add))
            dve.wait_ge(lists_t, 1)
            note(V.tensor_scalar(ix[:, 1, :], scr[:, 0, 0:LISTS], 1.0, 0.0, ALU.subtract, ALU.max))
            V.scalar_tensor_tensor(ix[:, 2, :], scr[:, 0, 0:LISTS], 0.0, spare[:, :], ALU.is_equal, ALU.mult)
            V.memset(take[:, LISTS:LISTS + UNROLL], 0)
            note(V.tensor_copy(take[:, 0:LISTS], ix[:, 1, :]))
            note(V.tensor_scalar(take[:, 0:LISTS], take[:, 0:LISTS], 2, None, ALU.logical_shift_right))
            note(V.scalar_tensor_tensor(put[:, :], scr[:, 0, 0:LISTS], -1.0, ix[:, 2, :], ALU.add, ALU.add))
            assert done[0] == 14
            V.tensor_copy(take_now[:, :], take[:, 0:UNROLL]).then_inc(take_set, UNROLL)
            V.memset(ht_hi[64:EHP, :, :].bitcast(F32), 0.0).then_inc(pad_rows, 1)
            V.memset(ht_lo[64:EHP, :, :].bitcast(F32), 0.0).then_inc(pad_rows, 1)
            dve.wait_ge(pad_rows, 2)

            nu = KD * 2 * EI
            for e in range(E):
                dve.wait_ge(w_hi, 2 * e + 2)
                V.tensor_tensor(up_lo[:, e * nu:(e + 1) * nu], wst[:, e % WSTAGES, 0:nu],
                                up_hi[:, e * nu:(e + 1) * nu].bitcast(F32), ALU.subtract)
                V.tensor_tensor(dn_lo[:, e * 2 * D:(e + 1) * 2 * D], wst[0:EHP, e % WSTAGES, nu:nu + 2 * D],
                                dn_hi[:, e * 2 * D:(e + 1) * 2 * D].bitcast(F32), ALU.subtract).then_inc(w_lo, 1)

            def step(s, u):
                if live(s, 0):
                    b = u % 2
                    dve.wait_ge(xt_hi_done, num(s, 1))
                    V.tensor_tensor(xt_lo[:, b, :], ring[:, 0, b, 0:D], xt_hi[:, b, :].bitcast(F32), ALU.subtract
                                    ).then_inc(xt_lo_done, 1)
                    dve.wait_ge(got[u], lap(s, u) * 16)
                    V.tensor_copy(take_now[:, u:u + 1], take[:, bass.ds(num(s, UNROLL), 1)]).then_inc(take_set, 1)
                if live(s, 1):
                    b = (u - 1) % 2
                    dve.wait_ge(silu_done, num(s, 0))
                    if not isinstance(s, int) or s >= 3:
                        dve.wait_ge(ht_full, num(s, -2))
                    V.tensor_tensor(eh[:, b, :], eg[:, b, :], ring[:, 1, b, EI:2 * EI], ALU.mult).then_inc(h_done, 1)
                if live(s, 2):
                    b = (u - 2) % 2
                    dve.wait_ge(ht_hi_done, num(s, -1))
                    V.tensor_tensor(ht_lo[0:EH, b, :], ring[0:EH, 2, b, 0:D], ht_hi[0:EH, b, :].bitcast(F32), ALU.subtract
                                    ).then_inc(ht_lo_done, 1)
                if live(s, 3):
                    if not isinstance(s, int) or s >= LEAD + UNROLL:
                        dve.wait_ge(sent[(u - 3) % UNROLL], (lap(s, u, 3) - 1) * 16)
                    V.tensor_copy(put_now[:, (u - 3) % UNROLL:(u - 3) % UNROLL + 1], put[:, bass.ds(num(s, -3), 1)]
                                  ).then_inc(put_set, 1)
            expert_steps(dve, step)

            dve.wait_ge(h_done, LISTS)
            dve.wait_ge(ht_lo_done, LISTS)
            for i in range(UNROLL):
                dve.wait_ge(sent[i], 16 * (LISTS // UNROLL))
            done = [0]

            def note3(ins):
                done[0] += 1
                ins.then_inc(weights, 1)
                dve.wait_ge(weights, done[0])
            la = logits_all[:, :, :, :].rearrange("p c t e -> p (c t) e")
            ra = rank_all[:, :, :, :].rearrange("p c t e -> p (c t e)")
            ex = wk[:, 0, :]
            tmp = wk[:, 1, :]
            note3(V.tensor_reduce(wm[:, 0, :], la, AX_X, ALU.max))
            note3(V.tensor_tensor(ex.rearrange("p (i e) -> p i e", e=E), la, wm[:, 0, :].unsqueeze(2).to_broadcast([P, TILES, E]),
                                  ALU.subtract))
            dve.wait_ge(expd, 1)
            for k in range(TOPK):
                note3(V.scalar_tensor_tensor(tmp, ra, float(k + 1), ex, ALU.is_equal, ALU.mult))
                note3(V.tensor_reduce(share[:, :, k], tmp.rearrange("p (i e) -> p i e", e=E), AX_X, ALU.add))
            note3(V.tensor_reduce(wm[:, 1, :], share[:, :, :], AX_X, ALU.add))
            note3(V.reciprocal(wm[:, 2, :], wm[:, 1, :]))
            note3(V.tensor_tensor(share[:, :, :], share[:, :, :], wm[:, 2, :].unsqueeze(2).to_broadcast([P, TILES, TOPK]), ALU.mult))

            def total(i, t, u):
                lap_ = 1 if isinstance(t, int) else t + 2
                dve.wait_ge(z_in[u], 32 * lap_)
                if not isinstance(t, int):
                    dve.wait_ge(o_out[u], 16 * (t + 1))
                for k in range(TOPK):
                    if k:
                        dve.wait_ge(summed, i * TOPK + k)
                    V.scalar_tensor_tensor(sums[:, u, :], zin[:, u, k * D:(k + 1) * D],
                                           share[:, bass.ds(i, 1), k:k + 1].rearrange("p a b -> p (a b)"),
                                           sums[:, u, :] if k else ain[:, u, :], ALU.mult, ALU.add).then_inc(summed, 1)
            for u in range(UNROLL):
                total(u, -1, u)
            with dve.Fori(0, TILES // UNROLL - 1) as t:
                for u in range(UNROLL):
                    total(t * UNROLL + (UNROLL + u), t, u)

        @block.gpsimd
        def _(pool):
            G = nc.gpsimd
            gchain = sem("gchain")
            n = 0

            def link(ins):
                nonlocal n
                n += 1
                ins.then_inc(gchain, 1)
                pool.wait_ge(gchain, n)
            link(G.memset(ident[:, :], 0.0))
            link(G.affine_select(out=ident[:, :], in_=ident[:, :], compare_op=ALU.not_equal, fill=1.0, base=0,
                                 pattern=[[-1, P]], channel_multiplier=1))
            link(G.memset(notfirst[:, :], 1.0))
            nf = notfirst[:, :].rearrange("p (t e) -> p t e", t=TT)
            link(G.memset(nf[:, :, 0:1], 0.0))
            link(G.iota(filled[:, :], pattern=[[TOKENS, E]], base=0, channel_multiplier=0,
                        allow_small_or_imprecise_dtypes=True))
            link(G.iota(idval[:, :], pattern=[[TOPK * P, TT], [1, TOPK]], base=1 - TOPK * CHUNK, channel_multiplier=TOPK,
                        allow_small_or_imprecise_dtypes=True))
            link(G.iota(first_slot[:, :], pattern=[[TOKENS, E]], base=0, channel_multiplier=0, allow_small_or_imprecise_dtypes=True))
            link(G.iota(list_start[:, :], pattern=[[P, ROWS]], base=0, channel_multiplier=0, allow_small_or_imprecise_dtypes=True))
            link(G.iota(list_no[:, :], pattern=[[1, LISTS]], base=0, channel_multiplier=0, allow_small_or_imprecise_dtypes=True))
            link(G.iota(spare[:, :], pattern=[[P, LISTS]], base=PICKED + 1, channel_multiplier=1, allow_small_or_imprecise_dtypes=True))
            link(G.memset(quarter[:, :], 0.0))
            for q in range(4):
                link(G.memset(quarter[32 * q:32 * q + 32, q:q + 1], 1.0))
                link(G.iota(in_quarter[32 * q:32 * q + 32, :], pattern=[[0, 1]], base=0, channel_multiplier=1,
                            allow_small_or_imprecise_dtypes=True))
            link(G.memset(earlier[:, :], 1.0))
            G.affine_select(out=earlier[:, :], in_=earlier[:, :], compare_op=ALU.is_gt, fill=0.0, base=0,
                            pattern=[[1, P]], channel_multiplier=-1).then_inc(consts, 1)
            link(G.memset(rank_all[:, :, :, :], 0.0))
            pool.dma_start(ids.rearrange("(p n) o -> p (n o)", p=P), rank_all[:, :, :, :].rearrange("p c t e -> p (c t e)")
                           ).then_inc(table_clear, 16)
            pool.wait_ge(table_clear, 16)
            pool.wait_ge(vconsts, 1)

            def turn_(turn):
                def lower(event):
                    f = int(event[1:])
                    pool.wait_ge(*hid_top.at(turn, event))
                    G.tensor_tensor(hid_lo[:, f, :], hid[:, silu.events[turn.kind].index(event) % 2, :],
                                    hid_hi[:, f, :].bitcast(F32), ALU.subtract).then_inc(*hid_low.did(turn, event))
                if turn.kind == "pre":
                    power_a(turn)
                    power_b(turn)
                if turn.shared:
                    for f in range(ST):
                        lower(f"G{f}")
                if turn.front:
                    for f in range(FT):
                        lower(f"S{f}")
                        if turn.next and f == 4:
                            power_a(turn)
                        if turn.next and f == 5:
                            power_b(turn)
                        if turn.shared and f == 6:
                            apart(pool, routed.at(turn, "id"))
                            scatter(0, 1)
                    if turn.shared:
                        scatter(1, 9)
                    pool.wait_ge(*norm2.at(turn, "ve"))
                    G.tensor_tensor(sc2[:, 1, :], sc2[:, 0, :], power[:, :], ALU.pow).then_inc(*pows.did(turn, "n2"))
                    if turn.shared:
                        scatter(9, TT * TOPK)
                elif turn.shared:
                    apart(pool, routed.at(turn, "id"))
                    scatter(0, TT * TOPK)
                if turn.next:
                    residual(turn)

            def power_a(turn):
                pool.wait_ge(*norm1.at(turn, "ve"))
                G.tensor_tensor(sc1[:, 1, :], sc1[:, 0, :], power[:, :], ALU.pow).then_inc(*pows.did(turn, "n1a"))

            def power_b(turn):
                pool.wait_ge(*norm1.at(turn, "ue"))
                G.tensor_tensor(sc1[:, 5, :], sc1[:, 4, :], power[:, :], ALU.pow).then_inc(*pows.did(turn, "n1b"))

            def residual(turn):
                apart(pool, norm1.at(turn, "b"), *([pair_done.at(turn, "W1")] if turn.front else []))
                G.tensor_scalar(sc1[:, 7, :], sc1[:, 1, :], 1.0, 1.0, ALU.mult, ALU.add).then_inc(*resid.did(turn, "rp"))
                G.tensor_tensor(sc1[:, 2, :], mv1[:, :, 0], sc1[:, 1, :], ALU.mult).then_inc(*resid.did(turn, "nm"))
                apart(pool, resid.at(turn, "nm"))
                for t in range(TT):
                    i = G.tensor_scalar(res[:, t, :], xin[:, t, :], sc1[:, 7, t:t + 1], sc1[:, 2, t:t + 1],
                                        ALU.mult, ALU.subtract)
                i.then_inc(*resid.did(turn, "res"))

            def scatter(a, b):
                for i in range(a, b):
                    G.indirect_dma_start(out=ids, out_offset=bass.IndirectOffsetOnAxis(ap=slot_u[:, i:i + 1], axis=0),
                                         in_=idval[:, i:i + 1], in_offset=None).then_inc(id_out, 16)
            steps(pool, turn_)
            pool.wait_ge(id_out, CHUNKS * 16 * TT * TOPK)
            pool.sem_inc(dense_done, 1)

            def gather(tile, u):
                G.indirect_dma_start(out=xg[:, u, :], out_offset=None, in_=xn2_rows,
                                     in_offset=bass.IndirectOffsetOnAxis(ap=take_now[:, u:u + 1], axis=0)).then_inc(got[u], 16)

            def send(u):
                G.indirect_dma_start(out=picked, out_offset=bass.IndirectOffsetOnAxis(ap=put_now[:, u:u + 1], axis=0),
                                     in_=ysb[:, u, :], in_offset=None).then_inc(sent[u], 16)

            def next_gather(n, u):
                apart(pool, (take_set, n + (UNROLL + 1)), (xt_full, n + 1))
                gather(None, u)

            def next_send(n, u):
                apart(pool, (put_set, n + 1), (y_done, n + 1))
                send(u)
            pool.wait_ge(xn2_out, 16 * CHUNKS)
            pool.wait_ge(take_set, UNROLL)
            for u in range(UNROLL):
                gather(None, u)
            for u in range(UNROLL):
                next_gather(u, u)
            with pool.Fori(0, LISTS // UNROLL - 2) as t:
                for u in range(UNROLL):
                    next_gather(t * UNROLL + (UNROLL + u), u)
                    next_send(t * UNROLL + u, u)
            for n in range(LISTS - 2 * UNROLL, LISTS):
                next_send(n, n % UNROLL)

        for s in (pair_full, scr_full, pair_done, act_done, norm1, norm2, mid, routed, sig_done, squares, sq_hi,
                  feat_top, logit_out, rms_done, silu, hid_top, hid_low, pows, resid):
            s.check()


def kernel(**inputs):
    import numpy as np
    import concourse.bacc as bacc
    from concourse.bass_utils import run_bass_kernel_spmd

    def by_rows(w):
        k = w.shape[0] // P
        return w.reshape(k, P, -1).transpose(1, 0, 2).reshape(P, -1)

    get = {name: np.asarray(a) for name, a in inputs.items()}
    x = get["L0_attn_x"].reshape(BATCH, CHUNKS, RUN, D).transpose(1, 0, 2, 3).reshape(TOKENS, D)
    router = np.zeros((D, RW), np.float32)
    router[:, 0:E] = get["L0_ffn_gate_w"].T
    router[:, E] = get["L0_ffn_shared_gate_vec"][0]
    s_up = np.zeros((D, 2, SIP), np.float32)
    s_up[:, :, 0:SI] = get["L0_ffn_shared_gate_up"].T.reshape(D, 2, SI)
    s_down = np.zeros((SIP, D), np.float32)
    s_down[0:SI] = get["L0_ffn_shared_down"].T
    w1 = np.concatenate([by_rows(w) for w in (get["L0_attn_w_qkv"].T, router, get["L0_attn_w_swiglu"].T, get["L0_attn_w_out"].T,
                                              s_up.reshape(D, 2 * SIP), s_down)], axis=1)
    w_up = get["L0_ffn_expert_gate_up"].transpose(0, 2, 1).reshape(E, KD, P, 2 * EI).transpose(0, 2, 1, 3).reshape(E, P, KD * 2 * EI)
    w_down = np.zeros((E, EHP, 2, D), np.float32)
    w_down[:, 0:EH] = get["L0_ffn_expert_down"].transpose(0, 2, 1).reshape(E, 2, EH, D).transpose(0, 2, 1, 3)
    arrays = {name: np.ascontiguousarray(a) for name, a in
              {"x": x, "w1": w1, "w_up": w_up, "w_down": w_down.reshape(E, EHP, 2 * D)}.items()}
    nc = bacc.Bacc("TRN2", target_bir_lowering=False, num_devices=1)
    ins = [nc.dram_tensor(name, a.shape, F32, kind="ExternalInput").ap() for name, a in arrays.items()]
    out = nc.dram_tensor("out", (TOKENS, D), F32, kind="ExternalOutput").ap()
    scratch = [nc.dram_tensor(name, shape, F32, kind="Internal").ap() for name, shape in
               (("xn2_rows", (TOKENS, D)), ("acc", (TOKENS, D)), ("ids", (E * TOKENS, 1)), ("picked", (PICKED + LISTS * P, D)))]
    build(nc, *ins, out, *scratch)
    got = run_bass_kernel_spmd(nc, [arrays], core_ids=[0]).results[0]["out"]
    return got.reshape(CHUNKS, BATCH, RUN, D).transpose(1, 0, 2, 3).reshape(BATCH, SEQ, D)
```

```python
from contextlib import ExitStack

import concourse.bass as bass
from concourse import mybir

F32 = mybir.dt.float32
F32R = mybir.dt.float32r
BF16 = mybir.dt.bfloat16
U32 = mybir.dt.uint32
ALU = mybir.AluOpType
ACT = mybir.ActivationFunctionType
AX_X = mybir.AxisListType.X

P = 128
D = 256
KD = D // P
BATCH, SEQ = 2, 2048
TOKENS = BATCH * SEQ
CHUNK = 512
CHUNKS = TOKENS // CHUNK
TT = CHUNK // P
RUN = CHUNK // BATCH
FF = 1024
FT = FF // P
SI = 704
ST = -(-SI // P)
SIP = ST * P
E = 16
TOPK = 4
EI = 176
EH = EI // 2
EHP = 96
RW = 32
LN_EPS = 1e-5
RMS_EPS = 1.1920929e-07
DEN_EPS = 1e-6

QKV0 = 0
SW0 = QKV0 + KD * 3 * D
WO0 = SW0 + KD * 2 * FF
RT0 = WO0 + FT * D
SG0 = RT0 + KD * RW
SD0 = SG0 + KD * 2 * SIP
WCOLS = SD0 + ST * D
PIECES = [(QKV0, SW0), (SW0, SW0 + FF * 2), (SW0 + FF * 2, WO0), (WO0, RT0), (RT0, SD0), (SD0, WCOLS)]

JOINS = 16
ROWS = TOKENS // P
LISTS = TOKENS * TOPK // P + E
PICKED = TOKENS * TOPK
GROUP = 4
GROUPS = LISTS // GROUP
EU = KD * 2 * EI
EW = EU + 2 * D
EARLY, EARLIER = SD0 // EW, RT0 // EW
RUNS, PEEL = 8, 2
AHEAD = 11
SPLIT_FIRST = 12
PICKS_SET, LISTS_SET = 11, 20
assert (GROUPS - 2 * PEEL) % RUNS == 0
assert LISTS % GROUP == 0
KINDS = ["pre", "first", "steady", "tail", "last"]
STEADY = CHUNKS - 2
ROUTE = 11
LATE_GAP = 396


class Turn:

    def __init__(self, kind, t=0):
        self.kind, self.t = kind, t
        self.front = kind in ("first", "steady", "tail")
        self.shared = kind in ("steady", "tail", "last")
        self.next = kind in ("pre", "first", "steady")


class Signal:

    def __init__(self, sem, front=(), shared=(), nxt=(), order=None):
        self.sem = sem
        every = order or [*front, *shared, *nxt]
        self.events = {}
        for kind in KINDS:
            turn = Turn(kind)
            on = [*(front if turn.front else ()), *(shared if turn.shared else ()), *(nxt if turn.next else ())]
            self.events[kind] = [e for e in every if e in on]
        self.raised = {kind: 0 for kind in KINDS}

    def start(self, turn):
        n = {kind: len(self.events[kind]) for kind in KINDS}
        before = KINDS[:KINDS.index(turn.kind)]
        at = sum(n[k] * (STEADY if k == "steady" else 1) for k in before)
        return turn.t * n["steady"] + at if turn.kind == "steady" else at

    def did(self, turn, event):
        assert self.events[turn.kind][self.raised[turn.kind]] == event, (turn.kind, event, self.events[turn.kind])
        self.raised[turn.kind] += 1
        return self.sem, 1

    def at(self, turn, event):
        return self.sem, self.start(turn) + (self.events[turn.kind].index(event) + 1)

    def before(self, turn, event):
        was = {"first": ["pre"], "steady": ["first", "steady"], "tail": ["steady"], "last": ["tail"]}[turn.kind]
        after = {len(self.events[k]) - self.events[k].index(event) - 1 for k in was}
        assert len(after) == 1
        return self.sem, self.start(turn) - after.pop()

    def check(self):
        for kind in KINDS:
            assert self.raised[kind] == len(self.events[kind]), (kind, self.raised, self.events)


SHARED_UP = [f"G{f}" for f in range(ST)]
FRONT_UP = [f"S{f}" for f in range(FT)]
FILLS = ["x", "stat", *SHARED_UP, "D0", "D1", *FRONT_UP, "b", "W0", "W1", "k", "q", "v"]
PAIRS = 3
assert len(FILLS) % PAIRS == 0


def build(nc, x, w1, w_up, w_down, out, xn2_rows, acc, ids, picked):
    ctx = ExitStack()
    with ctx:
        def sb(name, shape, dt, where=ctx):
            return where.enter_context(nc.sbuf_tensor(name, shape, dt))

        def sem(name):
            return ctx.enter_context(nc.semaphore(name))

        ident = sb("ident", [P, P], F32)
        ones_r = sb("ones_r", [P, P], F32R)
        ones_b = sb("ones_b", [P, P], BF16)
        earlier = sb("earlier", [P, P], BF16)
        ones_row = sb("ones_row", [P, RUN], F32)
        notfirst = sb("notfirst", [P, TT * E], F32)
        power = sb("power", [P, TT], F32)
        eps_c = sb("eps_c", [P, 1], F32)
        filled = sb("filled", [P, E], F32)
        first_slot = sb("first_slot", [P, E], F32)
        list_start = sb("list_start", [P, ROWS], F32)
        quarter = sb("quarter", [P, 4], F32)
        row_expert = sb("row_expert", [P, 4], F32)
        in_quarter = sb("in_quarter", [P, 1], F32)
        list_no = sb("list_no", [P, LISTS], F32)
        spare = sb("spare", [P, LISTS], F32)
        share = sb("share", [P, TOKENS // P, TOPK], F32)

        dense = ExitStack()
        whi = sb("whi", [P, WCOLS], F32R, dense)
        ksb = sb("ksb", [P, KD, CHUNK], F32, dense)
        qsb = sb("qsb", [P, KD, CHUNK], F32, dense)
        vsb = sb("vsb", [P, KD, CHUNK], F32, dense)
        kvsum = sb("kvsum", [P, KD, CHUNK], F32, dense)
        wsum = sb("wsum", [P, KD, CHUNK], F32, dense)
        y_hi = sb("y_hi", [P, KD, CHUNK], F32R, dense)
        y_lo = sb("y_lo", [P, KD, CHUNK], F32R, dense)
        with ExitStack() as early:
            wraw = sb("wraw", [P, WCOLS], F32, early)
        wlo = sb("wlo", [P, WCOLS], F32R, dense)
        hid_hi = sb("hid_hi", [P, FT, CHUNK], F32R, dense)
        hid_lo = sb("hid_lo", [P, FT, CHUNK], F32R, dense)
        xin = sb("xin", [P, TT, D], F32, dense)
        bnorm = sb("bnorm", [P, TT, D], F32, dense)
        rms = bnorm[:, :, :].rearrange("p t d -> p (t d)").rearrange("p (k n) -> p k n", k=KD)
        res = sb("res", [P, TT, D], F32, dense)
        feat_hi = sb("feat_hi", [P, KD, CHUNK], F32R, dense)
        feat_lo = sb("feat_lo", [P, KD, CHUNK], F32R, dense)
        x1 = sb("x1", [P, TT, D], F32, dense)
        xn2 = sb("xn2", [P, TT, D], F32, dense)
        kvend = sb("kvend", [P, KD, BATCH], F32, dense)
        wend = sb("wend", [P, KD, BATCH], F32, dense)
        gate = sb("gate", [P, 2, CHUNK], F32, dense)
        hid = sb("hid", [P, 2, CHUNK], F32, dense)
        st1 = sb("st1", [P, TT, 6], F32, dense)
        mv1 = sb("mv1", [P, TT, 2], F32, dense)
        sc1 = sb("sc1", [P, 8, TT], F32, dense)
        st2 = sb("st2", [P, TT, 6], F32, dense)
        mv2 = sb("mv2", [P, TT, 2], F32, dense)
        sc2 = sb("sc2", [P, 4, TT], F32, dense)
        lgt = sb("lgt", [RW, CHUNK], F32, dense)
        lg = sb("lg", [P, TT, RW], F32, dense)
        top8 = sb("top8", [P, TT, 8], F32, dense)
        rsm = sb("rsm", [P, 4, TT], F32, dense)
        selb = sb("selb", [P, TT * E], BF16, dense)
        slot_f = sb("slot_f", [P, TT, TOPK], F32, dense)
        slot_u = sb("slot_u", [P, TT * TOPK], U32, dense)
        idval = sb("idval", [P, TT * TOPK], F32, dense)
        sig = sb("sig", [P, TT], F32, dense)
        sb("gap_0", [P, LATE_GAP], F32, dense)
        rt = sb("rt", [P, ROUTE, TT * E], F32, dense)
        odds = sb("odds", [P, TT * E], F32, dense)
        rsh = sb("rsh", [P, TT, TOPK], F32, dense)
        total = sb("total", [P, 2, TT], F32, dense)
        dense.close()

        moe = ExitStack()
        ew_hi = sb("ew_hi", [P, E * EW], F32R, moe)
        gap = WCOLS + (5 + 2) * KD * CHUNK - E * EW
        assert gap >= 0
        sb("gap_1", [P, gap], F32, moe)
        with ExitStack() as early:
            eraw = [sb(f"eraw_{e}", [P, EW], F32, early) for e in range(E)]
        ew_lo = sb("ew_lo", [P, E * EW], F32R, moe)
        xg = sb("xg", [P, GROUP, D], F32, moe)
        gap = WCOLS + 2 * FT * CHUNK - E * EW - GROUP * D
        assert gap >= 0
        sb("gap_2", [P, gap], F32, moe)
        pick = sb("pick", [P, E * ROWS // P, LISTS], F32, moe)
        ix = sb("ix", [P, 4, LISTS], F32, moe)
        em = sb("em", [P, 8, E], F32, moe)
        whose = sb("whose", [1, GROUPS], mybir.dt.int32, moe)
        take = sb("take", [P, LISTS + GROUP], U32, moe)
        put = sb("put", [P, LISTS], U32, moe)
        take_now = sb("take_now", [P, GROUP], U32, moe)
        put_now = sb("put_now", [P, GROUP], U32, moe)
        tab = sb("tab", [P, E * ROWS // P, P], F32, moe)
        xt_hi = sb("xt_hi", [P, GROUP, D], F32R, moe)
        xt_lo = sb("xt_lo", [P, GROUP, D], F32R, moe)
        eg = sb("eg", [P, 2, EI], F32, moe)
        eh = sb("eh", [P, 2, EI], F32, moe)
        ht_hi = sb("ht_hi", [EHP, 2, D], F32R, moe)
        ht_lo = sb("ht_lo", [EHP, 2, D], F32R, moe)
        ysb = sb("ysb", [P, GROUP, D], F32, moe)
        ain = sb("ain", [P, JOINS, D], F32, moe)
        moe.close()
        TILES = TOKENS // P
        join = ExitStack()
        zin = sb("zin", [P, JOINS, TOPK * D], F32, join)
        sums = sb("sums", [P, JOINS, D], F32, join)
        join.close()

        ring = ctx.enter_context(nc.psum_tensor("ring", [P, PAIRS, 2, CHUNK], F32))
        scr = ctx.enter_context(nc.psum_tensor("scr", [P, 2, CHUNK], F32))

        pair_full = Signal(sem("pair_full"), ["stat", *FRONT_UP, "W0", "W1"], ["x", *SHARED_UP, "D0", "D1"],
                           ["b", "k", "q", "v"], order=FILLS)
        scr_full = Signal(sem("scr_full"), (), ["logit", "logit_t", "count"])
        pair_done = Signal(sem("pair_done"), [*FRONT_UP, "W0", "W1"], ["x", *SHARED_UP, "D0", "D1"], ["b"],
                           order=[e for e in FILLS if e not in ("stat", "k", "q", "v")])
        norm1 = Signal(sem("norm1"), (), (), ["stats", "aggr", "ve", "u0", "u1", "ue", "scale", "b"])
        norm2 = Signal(sem("norm2"), ["stats", "aggr", "ve", "xn2"])
        mid = Signal(sem("mid"), ["kr", "qr", "wv", "wsum", "wend", "kvsum", "kvend", "d", "rec0", "y0", "rec1", "y1",
                                  "ylo0", "ylo1"],
                     (), ["ksum", "qsum", "klo", "qlo"])
        routed = Signal(sem("routed"), (), ["lg", "top", "gt", "eq", "cgt", "need", "ceq", "ok", "tie", "sel", "selb",
                                            "rank", "rsel", "off0", "off1", "off2", "off3", "off4", "slot",
                                            *[f"{a}{k}" for k in range(TOPK) for a in ("m", "s")], "slotu", "id", "less"])
        shares = Signal(sem("shares"), (), [*[f"{a}{k}" for k in range(TOPK) for a in ("m", "s")], "sum", "inv", "share"])
        sig_done = Signal(sem("sig_done"), (), ["half"])
        x_top = Signal(sem("x_top"), (), ["hi0", "lo0", "hi1"])
        act_done = Signal(sem("act_done"), ["stat"], (), ["k", "q", "v"])
        squares = Signal(sem("squares"), (), (), ["k", "q"])
        sq_hi = Signal(sem("sq_hi"), (), (), ["k", "q"])
        feat_top = Signal(sem("feat_top"), (), (), ["b"])
        logit_out = Signal(sem("logit_out"), (), ["logit", "tanh", "exp"])
        rms_done = Signal(sem("rms_done"), ["lnk", "k", "q", "w", "eq", "yhi0", "yhi1"])
        silu = Signal(sem("silu"), FRONT_UP, SHARED_UP, order=SHARED_UP + FRONT_UP)
        hid_top = Signal(sem("hid_top"), FRONT_UP, SHARED_UP, order=SHARED_UP + FRONT_UP)
        hid_low = Signal(sem("hid_low"), FRONT_UP, SHARED_UP, order=SHARED_UP + FRONT_UP)
        pows = Signal(sem("pows"), ["n2"], (), ["n1a", "n1b"], order=["n1a", "n1b", "n2"])
        resid = Signal(sem("resid"), (), (), ["rp", "nm", "res"])
        x_in = sem("x_in")
        xn2_out = sem("xn2_out")
        acc_out = sem("acc_out")
        id_out = sem("id_out")
        piece_in = [sem(f"piece_in{i}") for i in range(len(PIECES))]
        whi_done = sem("whi_done")
        wlo_done = sem("wlo_done")
        consts = sem("consts")
        table_in = sem("table_in")
        lists = sem("lists")
        lists_t = sem("lists_t")
        w_in = [sem(f"w_in{i}") for i in range(E)]
        w_hi = sem("w_hi")
        w_lo = sem("w_lo")
        pad_rows = sem("pad_rows")
        got = [sem(f"got{i}") for i in range(GROUP)]
        sent = [sem(f"sent{i}") for i in range(GROUP)]
        take_set = [sem(f"take_set{j}") for j in range(GROUP)]
        put_set = [sem(f"put_set{j}") for j in range(GROUP)]
        xt_full = [sem(f"xt_full{j}") for j in range(GROUP)]
        up_full = [sem(f"up_full{j}") for j in range(GROUP)]
        ht_full = [sem(f"ht_full{j}") for j in range(GROUP)]
        y_full = [sem(f"y_full{j}") for j in range(GROUP)]
        xt_hi_done = [sem(f"xt_hi_done{j}") for j in range(GROUP)]
        xt_lo_done = [sem(f"xt_lo_done{j}") for j in range(GROUP)]
        silu_done = [sem(f"silu_done{j}") for j in range(GROUP)]
        h_done = [sem(f"h_done{j}") for j in range(GROUP)]
        ht_hi_done = [sem(f"ht_hi_done{j}") for j in range(GROUP)]
        ht_lo_done = [sem(f"ht_lo_done{j}") for j in range(GROUP)]
        y_done = [sem(f"y_done{j}") for j in range(GROUP)]
        z_in = [sem(f"z_in{i}") for i in range(JOINS)]
        o_out = [sem(f"o_out{i}") for i in range(JOINS)]
        summed = sem("summed")
        vconsts = sem("vconsts")

        def whi_c(c0, n):
            return whi[:, c0:c0 + n]

        def wlo_c(c0, n):
            return wlo[:, c0:c0 + n]

        def scattered(chunks):
            return chunks * (16 * TT * TOPK) + 16

        def slot_of(turn, event):
            return (pair_full.start(Turn(turn.kind)) + pair_full.events[turn.kind].index(event)) % PAIRS

        def apart(eng, *waits):
            for _, n in waits:
                if not isinstance(n, int):
                    eng.compute_val(n)
            eng.wait_ge(consts, 1)
            for s, n in waits:
                eng.wait_ge(s, n)

        def groups(eng, fn):
            fn(0)
            with eng.Fori(0, GROUPS - 2) as t:
                fn(t + 1)
            fn(GROUPS - 1)

        def tile_done(sems, g, j, back=0):
            g, j = (g, j - back) if j >= back else (g - 1, j - back + GROUP)
            return (sems[j], g + 1) if not isinstance(g, int) or g >= 0 else None

        def live_next(g):
            return not isinstance(g, int) or g < GROUPS - 1

        ORDER = [("up", 0), ("rows", 0), ("up", 1), ("hidden", 0), ("rows", 1), ("up", 2), ("hidden", 1), ("down", 0),
                 ("up", 3), ("rows", 2), ("hidden", 2), ("down", 1), ("hidden", 3), ("rows", 3), ("down", 2), ("down", 3)]

        def steps(eng, fn):
            fn(Turn("pre"))
            fn(Turn("first"))
            with eng.Fori(0, STEADY) as t:
                fn(Turn("steady", t))
            fn(Turn("tail"))
            fn(Turn("last"))

        block = ctx.enter_context(nc.Block())

        @block.sync
        def _(sp):
            sp.dma_start(xin[:, :, :], x[0:CHUNK, :].rearrange("(t p) d -> p t d", p=P)).then_inc(x_in, 16)
            for n, (a, b) in enumerate(PIECES):
                sp.dma_start(wraw[:, a:b], w1[:, a:b]).then_inc(piece_in[n], 16)

            def expert_weights(experts):
                for e in experts:
                    sp.dma_start(eraw[e][:, 0:EU], w_up[e, :, :]).then_inc(w_in[e], 16)
                    sp.dma_start(eraw[e][0:EHP, EU:EW], w_down[e, :, :]).then_inc(w_in[e], 16)

            def turn_(turn):
                c = {"first": 0, "steady": turn.t + 1, "tail": CHUNKS - 1, "last": CHUNKS}.get(turn.kind)
                if turn.front and turn.next:
                    sp.wait_ge(*resid.before(turn, "res"))
                    sp.dma_start(xin[:, :, :], x[bass.ds((c + 1) * CHUNK, CHUNK), :].rearrange("(t p) d -> p t d", p=P)
                                 ).then_inc(x_in, 16)

                def store_acc():
                    sp.wait_ge(*pair_done.at(turn, "D1"))
                    sp.dma_start(acc[bass.ds((c - 1) * CHUNK, CHUNK), :].rearrange("(t p) d -> p t d", p=P),
                                 x1[:, :, :]).then_inc(acc_out, 16)
                if turn.kind == "last":
                    sp.wait_ge(*pair_done.before(turn, "W1"))
                    expert_weights(range(EARLIER))
                    sp.wait_ge(*pair_full.at(turn, SHARED_UP[-1]))
                    expert_weights(range(EARLIER, EARLY))
                    sp.wait_ge(*pair_full.at(turn, "D1"))
                    expert_weights(range(EARLY, EARLY + 3))
                    store_acc()
                    sp.wait_ge(id_out, scattered(CHUNKS))
                    sp.dma_start(tab[:, :, :], ids.rearrange("(g p n) o -> p g (n o)", p=P, n=P)).then_inc(table_in, 16)
                    expert_weights(range(EARLY + 3, E))
                elif turn.shared:
                    store_acc()
                if turn.front:
                    sp.wait_ge(*norm2.at(turn, "xn2"))
                    sp.dma_start(xn2_rows[bass.ds(c * CHUNK, CHUNK), :].rearrange("(t p) d -> p t d", p=P),
                                 xn2[:, :, :]).then_inc(xn2_out, 16)
            steps(sp, turn_)
            sp.wait_ge(acc_out, 16 * CHUNKS)

            def load_sum(i, u):
                sp.dma_start(ain[:, u, :], acc[bass.ds(i * P, P), :]).then_inc(z_in[u], 16)

            def load_picked(i, u):
                sp.dma_start(zin[:, u, :], picked[bass.ds(i * (P * TOPK), P * TOPK), :].rearrange("(p k) d -> p (k d)", k=TOPK)
                             ).then_inc(z_in[u], 16)
            for u in range(JOINS):
                load_sum(u, u)
            for i in range(GROUP):
                sp.wait_ge(sent[i], 16 * GROUPS)
            for u in range(JOINS):
                load_picked(u, u)
            for i in range(JOINS, TILES):
                if i % 2 == 0:
                    sp.wait_ge(summed, ((i - JOINS) // 2 + 1) * TOPK)
                load_picked(i, i % JOINS)
                load_sum(i, i % JOINS)
            for u in range(JOINS):
                sp.wait_ge(o_out[u], 16 * (TILES // JOINS))

        @block.tensor
        def _(pe):
            def three(out, lhs, rhs, first, last):
                pairs = [(0, 0), (0, 1), (1, 0)]
                for n, (a, b) in enumerate(pairs):
                    mm = pe.matmul(out, lhs[a], rhs[b], start=first and n == 0, stop=last and n == 2)
                return mm

            def bank_pair(turn, event):
                every = pair_full.events[turn.kind]
                n = every.index(event) - PAIRS
                if n >= 0:
                    was = every[n]
                    pe.wait_ge(*(pair_done if was in pair_done.events[turn.kind] else act_done).at(turn, was))
                elif turn.kind != "pre":
                    kind = KINDS[KINDS.index(turn.kind) - 1]
                    was = pair_full.events[kind][n]
                    pe.wait_ge(*(pair_done if was in pair_done.events[kind] else act_done).before(turn, was))
                return slot_of(turn, event)

            def proj(turn, event, cols, width, rhi, rlo):
                s = bank_pair(turn, event)
                for h, c in enumerate(cols):
                    for k in range(KD):
                        mm = three(ring[:, s, h, :], (whi_c(c + k * width, P), wlo_c(c + k * width, P)),
                                   (rhi[:, k, :], rlo[:, k, :]), k == 0, k == KD - 1)
                mm.then_inc(*pair_full.did(turn, event))

            def down(turn, events, w0, hidden, late):
                n, pair = len(hidden), {}
                for fs in (range(n - late), range(n - late, n)):
                    for event, first in events:
                        if fs[0] == 0:
                            pair[event] = bank_pair(turn, event)
                        for h, t in enumerate((first, first + 1)):
                            for f in fs:
                                if t == 0:
                                    pe.wait_ge(*hid_low.at(turn, hidden[f]))
                                mm = three(ring[:, pair[event], h, 0:D],
                                           (hid_hi[:, f, t * P:(t + 1) * P], hid_lo[:, f, t * P:(t + 1) * P]),
                                           (whi_c(w0 + f * D, D), wlo_c(w0 + f * D, D)), f == 0, f == n - 1)
                        if fs[-1] == n - 1:
                            mm.then_inc(*pair_full.did(turn, event))

            def turn_columns(turn, event, rows):
                s = bank_pair(turn, event)
                for k in range(KD):
                    for t in range(TT):
                        mm = pe.transpose(ring[:, s, k, t * P:(t + 1) * P], rows[:, t, k * P:(k + 1) * P], ident[:, :])
                mm.then_inc(*pair_full.did(turn, event))

            pe.wait_ge(consts, 1)
            pe.wait_ge(vconsts, 1)

            def turn_(turn):
                def shared_up(*tiles):
                    for f in tiles:
                        proj(turn, f"G{f}", (SG0 + SIP + f * P, SG0 + f * P), 2 * SIP, feat_hi, feat_lo)

                def front_up(*tiles):
                    for f in tiles:
                        proj(turn, f"S{f}", (SW0 + f * P, SW0 + FF + f * P), 2 * FF, y_hi, y_lo)

                def counts():
                    pe.wait_ge(*routed.at(turn, "selb"))
                    pe.matmul(scr[:, 1, 128:192], earlier[:, :], selb[:, :], start=True, stop=True)
                    pe.matmul(scr[:, 1, 192:256], ones_b[:, :], selb[:, :], start=True, stop=True
                              ).then_inc(*scr_full.did(turn, "count"))

                if turn.shared:
                    pe.wait_ge(*norm2.before(turn, "xn2"))
                    turn_columns(turn, "x", xn2)
                if turn.front:
                    s = bank_pair(turn, "stat")
                    for h in range(2):
                        pe.wait_ge(*mid.before(turn, ("klo", "qlo")[h]))
                        pe.matmul(ring[:, s, h, :], ones_r[:, :], y_hi[:, h, :], start=True, stop=False)
                        mm = pe.matmul(ring[:, s, h, :], ones_r[:, :], y_lo[:, h, :], start=False, stop=True)
                    mm.then_inc(*pair_full.did(turn, "stat"))
                if turn.shared:
                    for k in range(KD):
                        pe.wait_ge(*(pair_done.at(turn, "x") if k else x_top.at(turn, "lo0")))
                        mm = three(scr[0:RW, 0, :], (whi_c(RT0 + k * RW, RW), wlo_c(RT0 + k * RW, RW)),
                                   (feat_hi[:, k, :], feat_lo[:, k, :]), k == 0, k == KD - 1)
                    mm.then_inc(*scr_full.did(turn, "logit"))
                    if turn.front:
                        shared_up(0, 1)
                    apart(pe, logit_out.at(turn, "logit"))
                    for t in range(TT):
                        mm = pe.transpose(scr[:, 1, t * RW:(t + 1) * RW], lgt[:, t * P:(t + 1) * P], ident[0:RW, 0:RW])
                    mm.then_inc(*scr_full.did(turn, "logit_t"))
                    if turn.front:
                        shared_up(2, 3, 4, 5)
                    else:
                        shared_up(0)
                        counts()
                        shared_up(1, 2, 3, 4, 5)
                    down(turn, (("D0", 0), ("D1", 2)), SD0, SHARED_UP, late=2)
                if turn.front:
                    if turn.kind == "first":
                        pe.wait_ge(wlo_done, 3)
                    pe.wait_ge(*mid.at(turn, "ylo1"))
                    front_up(0, 1, 2)
                    if turn.shared:
                        counts()
                    front_up(3, 4, 5, 6, 7)
                if turn.next:
                    pe.wait_ge(*norm1.at(turn, "b"))
                    turn_columns(turn, "b", bnorm)
                if turn.front:
                    if turn.kind == "first":
                        pe.wait_ge(wlo_done, len(PIECES))
                    down(turn, (("W0", 0),), WO0, FRONT_UP, late=1)
                    down(turn, (("W1", 2),), WO0, FRONT_UP, late=1)
                if turn.next:
                    if turn.kind == "pre":
                        pe.wait_ge(wlo_done, 1)
                    pe.wait_ge(*pair_done.at(turn, "b"))
                    for n, part in ((1, "k"), (0, "q"), (2, "v")):
                        proj(turn, part, (QKV0 + n * D, QKV0 + n * D + P), 3 * D, feat_hi, feat_lo)
            steps(pe, turn_)

            pe.wait_ge(table_in, 16)
            pe.wait_ge(lists, PICKS_SET)
            parts = E * ROWS // P
            for g in range(parts):
                mm = pe.matmul(scr[:, 0, 0:LISTS], tab[:, g, :], pick[:, g, :], start=g == 0, stop=g == parts - 1)
            for g in range(parts):
                mm = pe.matmul(scr[0:1, 1, 0:LISTS], row_expert[:, g:g + 1], pick[:, g, :], start=g == 0, stop=g == parts - 1)
            mm.then_inc(lists_t, 1)
            pe.wait_ge(lists, LISTS_SET)

            def turn_rows(g, j):
                b = j % 2
                pe.wait_ge(got[j], 16 * (g + 1))
                if j >= 2:
                    pe.wait_ge(*tile_done(xt_lo_done, g, j, 2))
                for k in range(KD):
                    mm = pe.transpose(ring[:, 0, b, k * P:(k + 1) * P], xg[:, j, k * P:(k + 1) * P], ident[:, :])
                mm.then_inc(xt_full[j], 1)

            def up(g, j, at):
                b = j % 2
                if j == 0:
                    pe.wait_ge(*tile_done(xt_lo_done, g, GROUP - 1))
                for k in range(KD):
                    lhs = (xt_hi[:, j, k * P:(k + 1) * P], xt_lo[:, j, k * P:(k + 1) * P])
                    to = bass.ds(at + k * 2 * EI, 2 * EI)
                    mm = three(ring[:, 1, b, 0:2 * EI], lhs, (ew_hi[:, to], ew_lo[:, to]), k == 0, k == KD - 1)
                mm.then_inc(up_full[j], 1)

            def turn_hidden(g, j):
                b = j % 2
                pe.wait_ge(*tile_done(h_done, g, j))
                for k in range(2):
                    mm = pe.transpose(ring[0:EH, 2, b, k * P:(k + 1) * P], eh[:, b, k * EH:(k + 1) * EH], ident[:, :])
                mm.then_inc(ht_full[j], 1)

            def down_rows(g, j, at):
                b = j % 2
                pe.wait_ge(*tile_done(ht_lo_done, g, j))
                free = tile_done(y_done, g, j, 2)
                if free:
                    pe.wait_ge(*free)
                for k in range(2):
                    lhs = (ht_hi[:, b, k * P:(k + 1) * P], ht_lo[:, b, k * P:(k + 1) * P])
                    to = bass.ds(at + EU + k * D, D)
                    mm = three(scr[:, b, 0:D], lhs, (ew_hi[0:EHP, to], ew_lo[0:EHP, to]), k == 0, k == 1)
                mm.then_inc(y_full[j], 1)

            for j in range(GROUP):
                turn_rows(0, j)
            pe.wait_ge(w_lo, E)
            pe.wait_ge(pad_rows, 2)

            def experts_of(g):
                return pe.value_load(whose[0:1, bass.ds(g, 1)], min_val=0, max_val=E ** GROUP - 1)

            def group(g, experts, ahead=None):
                at, follow = {}, None
                for n, (what, j) in enumerate(ORDER):
                    if n == ahead:
                        follow = experts_of(g + 1)
                    if what == "up":
                        at[j] = (experts // E ** j) % E * EW
                        up(g, j, at[j])
                    elif what == "rows" and live_next(g):
                        turn_rows(g + 1, j)
                    elif what == "hidden":
                        turn_hidden(g, j)
                    elif what == "down":
                        down_rows(g, j, at[j])
                return follow
            def run(g, n):
                experts = experts_of(g)
                for i in range(n):
                    experts = group(g + i, experts, AHEAD if i < n - 1 else None)
            run(0, PEEL)
            with pe.Fori(0, (GROUPS - 2 * PEEL) // RUNS) as t:
                run(t * RUNS + PEEL, RUNS)
            run(GROUPS - PEEL, PEEL)

        @block.scalar
        def _(act):
            def upper(pieces):
                for n in pieces:
                    a, b = PIECES[n]
                    act.wait_ge(piece_in[n], 16)
                    nc.scalar.copy(whi[:, a:b], wraw[:, a:b]).then_inc(whi_done, 1)

            def upper_expert(e):
                act.wait_ge(w_in[e], 32)
                for parts, a, b in ((P, e * EW, e * EW + EU), (EHP, e * EW + EU, (e + 1) * EW)):
                    i = nc.scalar.copy(ew_hi[0:parts, a:b], eraw[e][0:parts, a - e * EW:b - e * EW])
                i.then_inc(w_hi, 1)

            def hidden(turn, events, extra=None):
                every = silu.events[turn.kind]

                def top(event):
                    f = int(event[1:])
                    act.wait_ge(*pair_done.at(turn, event))
                    nc.scalar.copy(hid_hi[:, f, :], hid[:, every.index(event) % 2, :]).then_inc(*hid_top.did(turn, event))
                for n, event in enumerate(events):
                    act.wait_ge(*pair_full.at(turn, event))
                    i = every.index(event)
                    if i >= 2:
                        act.wait_ge(*pair_done.at(turn, every[i - 2]))
                    nc.scalar.activation(gate[:, i % 2, :], ring[:, slot_of(turn, event), 1, :], ACT.Silu
                                         ).then_inc(*silu.did(turn, event))
                    if n:
                        top(events[n - 1])
                    if extra:
                        extra(n)
                top(events[-1])

            def turned(turn, event):
                act.wait_ge(*pair_full.at(turn, event))
                nc.scalar.copy(feat_hi[:, :, :], ring[:, slot_of(turn, event), :, :]).then_inc(*feat_top.did(turn, event))

            upper([0, 1, 2])
            act.wait_ge(vconsts, 1)

            def turn_(turn):
                def between(n):
                    if turn.kind == "first":
                        if n + 3 < len(PIECES):
                            upper([n + 3])
                    if turn.kind == "last":
                        upper_expert(n)

                def half_tanh():
                    act.wait_ge(*scr_full.at(turn, "logit_t"))
                    nc.scalar.activation(sig[:, :], scr[:, 1, 0:TT * RW].rearrange("p (t r) -> p t r", t=TT)[:, :, E],
                                         ACT.Tanh, scale=0.5).then_inc(*logit_out.did(turn, "tanh"))

                if turn.front:
                    act.wait_ge(*pair_full.at(turn, "stat"))
                    s = slot_of(turn, "stat")
                    nc.scalar.activation(rms[:, 0, :], ring[:, s, 0, :], ACT.Ln, bias=eps_c[:, 0:1], scale=1.0 / D
                                         ).then_inc(*rms_done.did(turn, "lnk"))
                    nc.scalar.activation(rms[:, 1, :], ring[:, s, 1, :], ACT.Ln, bias=eps_c[:, 0:1], scale=1.0 / D
                                         ).then_inc(*act_done.did(turn, "stat"))
                    act.wait_ge(*rms_done.at(turn, "lnk"))
                    nc.scalar.activation(rms[:, 0, :], rms[:, 0, :], ACT.Exp, scale=-0.5).then_inc(*rms_done.did(turn, "k"))
                    act.wait_ge(*act_done.at(turn, "stat"))
                    nc.scalar.activation(rms[:, 1, :], rms[:, 1, :], ACT.Exp, scale=-0.5).then_inc(*rms_done.did(turn, "q"))
                if turn.shared:
                    act.wait_ge(*scr_full.at(turn, "logit"))
                    nc.scalar.copy(lgt[:, :], scr[0:RW, 0, :]).then_inc(*logit_out.did(turn, "logit"))
                    if not turn.front:
                        half_tanh()
                if turn.front:
                    act.wait_ge(*mid.at(turn, "kr"))
                    nc.scalar.activation(ksb[:, :, :], ksb[:, :, :], ACT.Exp).then_inc(*rms_done.did(turn, "w"))
                    act.wait_ge(*mid.at(turn, "qr"))
                    nc.scalar.activation(qsb[:, :, :], qsb[:, :, :], ACT.Exp, scale=-1.0).then_inc(*rms_done.did(turn, "eq"))
                if turn.shared:
                    hidden(turn, SHARED_UP, (lambda n: half_tanh() if n == 2 else None) if turn.front else between)
                if turn.front:
                    for k in range(KD):
                        act.wait_ge(*mid.at(turn, f"y{k}"))
                        nc.scalar.copy(y_hi[:, k, :], kvsum[:, k, :]).then_inc(*rms_done.did(turn, f"yhi{k}"))
                    hidden(turn, FRONT_UP, between)
                if turn.next:
                    turned(turn, "b")
                if turn.shared:
                    act.wait_ge(*routed.at(turn, "less"))
                    nc.scalar.activation(odds[:, :], odds[:, :], ACT.Exp).then_inc(*logit_out.did(turn, "exp"))
                if turn.next:

                    def take(part, to):
                        nc.scalar.copy(to[:, :, :], ring[:, slot_of(turn, part), :, :]).then_inc(*act_done.did(turn, part))

                    def square(part, to):
                        act.wait_ge(*pair_full.at(turn, part))
                        nc.scalar.activation(to[:, :, :], ring[:, slot_of(turn, part), :, :], ACT.Square
                                             ).then_inc(*squares.did(turn, part))

                    def upper_sum(part, of):
                        act.wait_ge(*mid.at(turn, part + "sum"))
                        nc.scalar.copy(y_hi[:, "kq".index(part), :], of[:, 0, :]).then_inc(*sq_hi.did(turn, part))
                    square("k", kvsum)
                    take("k", ksb)
                    square("q", wsum)
                    upper_sum("k", kvsum)
                    upper_sum("q", wsum)
                    take("q", qsb)
                    act.wait_ge(*pair_full.at(turn, "v"))
                    take("v", vsb)
            steps(act, turn_)
            for e in range(ST, E):
                upper_expert(e)

            def upper_rows(g, j):
                act.wait_ge(*tile_done(xt_full, g, j))
                if not isinstance(g, int) or g:
                    act.wait_ge(*tile_done(up_full, g, j, GROUP))
                nc.scalar.copy(xt_hi[:, j, :], ring[:, 0, j % 2, 0:D]).then_inc(xt_hi_done[j], 1)

            for j in range(GROUP):
                upper_rows(0, j)

            def group(g):
                for what, j in ORDER:
                    b = j % 2
                    if what == "up":
                        act.wait_ge(*tile_done(up_full, g, j))
                        free = tile_done(h_done, g, j, 2)
                        if free:
                            act.wait_ge(*free)
                        nc.scalar.activation(eg[:, b, :], ring[:, 1, b, 0:EI], ACT.Silu).then_inc(silu_done[j], 1)
                    elif what == "rows" and live_next(g):
                        upper_rows(g + 1, j)
                    elif what == "hidden":
                        act.wait_ge(*tile_done(ht_full, g, j))
                        free = tile_done(y_full, g, j, 2)
                        if free:
                            act.wait_ge(*free)
                        nc.scalar.copy(ht_hi[0:EH, b, :], ring[0:EH, 2, b, 0:D]).then_inc(ht_hi_done[j], 1)
                    elif what == "down":
                        act.wait_ge(*tile_done(y_full, g, j))
                        if not isinstance(g, int) or g:
                            act.wait_ge(sent[j], 16 * g)
                        nc.scalar.copy(ysb[:, j, :], scr[:, b, 0:D]).then_inc(y_done[j], 1)
            groups(act, group)

            def store(pair, i, u):
                act.wait_ge(summed, pair)
                act.dma_start(out[bass.ds(i * P, P), :], sums[:, u, :]).then_inc(o_out[u], 16)
            with act.Fori(0, TILES // JOINS) as t:
                for u in range(JOINS):
                    store(t * (JOINS // 2 * TOPK) + (u // 2 + 1) * TOPK, t * JOINS + u, u)

        @block.vector
        def _(dve):
            V = nc.vector
            V.memset(ones_r[:, :].bitcast(F32), 1.0)
            V.memset(ones_b[:, :], 1.0)
            V.memset(ones_row[:, :], 1.0)
            V.memset(power[:, :], -0.5)
            V.memset(eps_c[:, :], RMS_EPS)
            V.memset(kvend[:, :, :], 0.0)
            V.memset(wend[:, :, :], DEN_EPS).then_inc(vconsts, 1)

            def split_lo(turn, event):
                if event == "x":
                    dve.wait_ge(*pair_full.at(turn, "x"))
                    for k in range(KD):
                        V.tensor_copy(feat_hi[:, k, :], ring[:, slot_of(turn, "x"), k, :]).then_inc(*x_top.did(turn, f"hi{k}"))
                        dve.wait_ge(*x_top.at(turn, f"hi{k}"))
                        V.tensor_tensor(feat_lo[:, k, :], ring[:, slot_of(turn, "x"), k, :], feat_hi[:, k, :].bitcast(F32),
                                        ALU.subtract).then_inc(*(pair_done.did(turn, "x") if k else x_top.did(turn, "lo0")))
                else:
                    dve.wait_ge(*feat_top.at(turn, event))
                    V.tensor_tensor(feat_lo[:, :, :], ring[:, slot_of(turn, event), :, :], feat_hi[:, :, :].bitcast(F32),
                                    ALU.subtract).then_inc(*pair_done.did(turn, event))

            def first_norm(turn, part):
                if part == 0:
                    c = {"pre": 0, "first": 1, "steady": turn.t + 2}[turn.kind]
                    dve.wait_ge(x_in, (c + 1) * 16)
                    for t in range(TT):
                        i = V.bn_stats(st1[:, t, :], xin[:, t, :])
                    i.then_inc(*norm1.did(turn, "stats"))
                    apart(dve, norm1.at(turn, "stats"))
                    for t in range(TT):
                        i = V.bn_aggr(mv1[:, t, :], st1[:, t, :])
                    i.then_inc(*norm1.did(turn, "aggr"))
                    dve.wait_ge(*norm1.at(turn, "aggr"))
                    V.tensor_scalar(sc1[:, 0, :], mv1[:, :, 1], LN_EPS, None, ALU.add).then_inc(*norm1.did(turn, "ve"))
                if part == 1:
                    dve.wait_ge(*pows.at(turn, "n1a"))
                    V.tensor_tensor(sc1[:, 2, :], mv1[:, :, 1], sc1[:, 1, :], ALU.mult).then_inc(*norm1.did(turn, "u0"))
                    dve.wait_ge(*norm1.at(turn, "u0"))
                    V.tensor_tensor(sc1[:, 3, :], sc1[:, 2, :], sc1[:, 1, :], ALU.mult).then_inc(*norm1.did(turn, "u1"))
                    dve.wait_ge(*norm1.at(turn, "u1"))
                    V.tensor_scalar(sc1[:, 4, :], sc1[:, 3, :], RMS_EPS, None, ALU.add).then_inc(*norm1.did(turn, "ue"))
                if part == 2:
                    dve.wait_ge(*pows.at(turn, "n1b"))
                    V.tensor_tensor(sc1[:, 6, :], sc1[:, 1, :], sc1[:, 5, :], ALU.mult).then_inc(*norm1.did(turn, "scale"))
                    dve.wait_ge(*norm1.at(turn, "scale"))
                    for t in range(TT):
                        i = V.tensor_scalar(bnorm[:, t, :], xin[:, t, :], mv1[:, t, 0:1], sc1[:, 6, t:t + 1],
                                            ALU.subtract, ALU.mult)
                    i.then_inc(*norm1.did(turn, "b"))

            def product(turn, event):
                i = silu.events[turn.kind].index(event)
                dve.wait_ge(*silu.at(turn, event))
                if turn.kind == "first" and not i:
                    dve.wait_ge(id_out, scattered(0))
                if i >= 2:
                    was = silu.events[turn.kind][i - 2]
                    dve.wait_ge(*hid_top.at(turn, was))
                    dve.wait_ge(*hid_low.at(turn, was))
                elif turn.kind != "first":
                    dve.wait_ge(*hid_low.before(turn, f"S{FT - 2 + i}"))
                V.tensor_tensor(hid[:, i % 2, :], gate[:, i % 2, :], ring[:, slot_of(turn, event), 0, :], ALU.mult
                                ).then_inc(*pair_done.did(turn, event))

            def bc(ap, n):
                return ap.unsqueeze(2).to_broadcast([P, TT, n])

            def r3(i):
                return rt[:, i, :].rearrange("p (t e) -> p t e", t=TT)

            GT, EQ, CEQ, OK, TIE, SEL, RANK, OFF, SLOT, RSEL, TMP = range(ROUTE)

            def link(turn, ins, event):
                ins.then_inc(*routed.did(turn, event))
                dve.wait_ge(*routed.at(turn, event))

            def route_a(turn):
                dve.wait_ge(*logit_out.at(turn, "tanh"))
                V.tensor_copy(lg[:, :, :], scr[:, 1, 0:TT * RW].rearrange("p (t r) -> p t r", t=TT)
                              ).then_inc(*routed.did(turn, "lg"))
                apart(dve, routed.at(turn, "lg"))
                l = lg[:, :, 0:E]
                for t in range(TT):
                    i = V.max(top8[:, t, :], lg[:, t, 0:E])
                link(turn, i, "top")
                fourth = top8[:, :, TOPK - 1:TOPK].to_broadcast([P, TT, E])
                V.tensor_tensor(r3(GT), l, fourth, ALU.is_gt).then_inc(*routed.did(turn, "gt"))
                link(turn, V.tensor_tensor(r3(EQ), l, fourth, ALU.is_equal), "eq")
                link(turn, V.tensor_reduce(rsm[:, 0, :], r3(GT), AX_X, ALU.add), "cgt")
                link(turn, V.tensor_scalar(rsm[:, 1, :], rsm[:, 0, :], -1.0, float(TOPK), ALU.mult, ALU.add), "need")
                link(turn, V.tensor_tensor_scan(rt[:, CEQ, :], notfirst[:, :], rt[:, EQ, :], 0.0, ALU.mult, ALU.add), "ceq")
                link(turn, V.tensor_tensor(r3(OK), r3(CEQ), bc(rsm[:, 1, :], E), ALU.is_le), "ok")
                link(turn, V.tensor_tensor(rt[:, TIE, :], rt[:, EQ, :], rt[:, OK, :], ALU.mult), "tie")
                link(turn, V.tensor_tensor(rt[:, SEL, :], rt[:, GT, :], rt[:, TIE, :], ALU.add), "sel")
                V.tensor_copy(selb[:, :], rt[:, SEL, :]).then_inc(*routed.did(turn, "selb"))
                link(turn, V.tensor_tensor_scan(rt[:, RANK, :], notfirst[:, :], rt[:, SEL, :], 0.0, ALU.mult, ALU.add), "rank")
                link(turn, V.tensor_tensor(rt[:, RSEL, :], rt[:, RANK, :], rt[:, SEL, :], ALU.mult), "rsel")

            def route_b(turn):
                dve.wait_ge(*scr_full.at(turn, "count"))
                link(turn, V.tensor_copy(rt[:, OFF, 0:E], filled[:, :]), "off0")
                for t in range(1, TT + 1):
                    to = rt[:, OFF, t * E:(t + 1) * E] if t < TT else filled[:, :]
                    link(turn, V.tensor_tensor(to, rt[:, OFF, (t - 1) * E:t * E], scr[:, 1, 192 + (t - 1) * E:192 + t * E],
                                               ALU.add), f"off{t}")
                link(turn, V.tensor_tensor(rt[:, SLOT, :], rt[:, OFF, :], scr[:, 1, 128:192], ALU.add), "slot")
                for k in range(TOPK):
                    link(turn, V.scalar_tensor_tensor(rt[:, TMP, :], rt[:, RSEL, :], float(k + 1), rt[:, SLOT, :],
                                                      ALU.is_equal, ALU.mult), f"m{k}")
                    link(turn, V.tensor_reduce(slot_f[:, :, k], r3(TMP), AX_X, ALU.add), f"s{k}")
                dve.wait_ge(id_out, scattered({"steady": turn.t, "tail": CHUNKS - 2, "last": CHUNKS - 1}[turn.kind]))
                V.tensor_copy(slot_u[:, :], slot_f[:, :, :].rearrange("p t k -> p (t k)")).then_inc(*routed.did(turn, "slotu"))
                V.tensor_scalar(idval[:, :], idval[:, :], float(TOPK * CHUNK), None, ALU.add).then_inc(*routed.did(turn, "id"))
                V.tensor_tensor(odds[:, :].rearrange("p (t e) -> p t e", t=TT), lg[:, :, 0:E],
                                top8[:, :, 0:1].to_broadcast([P, TT, E]), ALU.subtract).then_inc(*routed.did(turn, "less"))

            def weigh(turn):
                def link(ins, event):
                    ins.then_inc(*shares.did(turn, event))
                    dve.wait_ge(*shares.at(turn, event))
                dve.wait_ge(*logit_out.at(turn, "exp"))
                c = {"steady": turn.t, "tail": CHUNKS - 2, "last": CHUNKS - 1}[turn.kind]
                mine = share[:, bass.ds(c * TT, TT), :]
                for k in range(TOPK):
                    link(V.scalar_tensor_tensor(rt[:, TMP, :], rt[:, RSEL, :], float(k + 1), odds[:, :],
                                                ALU.is_equal, ALU.mult), f"m{k}")
                    link(V.tensor_reduce(rsh[:, :, k], r3(TMP), AX_X, ALU.add), f"s{k}")
                link(V.tensor_reduce(total[:, 0, :], rsh[:, :, :], AX_X, ALU.add), "sum")
                link(V.reciprocal(total[:, 1, :], total[:, 0, :]), "inv")
                link(V.tensor_tensor(mine, rsh[:, :, :], bc(total[:, 1, :], TOPK), ALU.mult), "share")

            def lower_weights(pieces):
                for n in pieces:
                    a, b = PIECES[n]
                    dve.wait_ge(whi_done, n + 1)
                    V.tensor_tensor(wlo[:, a:b], wraw[:, a:b], whi[:, a:b].bitcast(F32), ALU.subtract
                                    ).then_inc(wlo_done, 1)

            def lower_expert(e):
                dve.wait_ge(w_hi, e + 1)
                for parts, a, b in ((P, e * EW, e * EW + EU), (EHP, e * EW + EU, (e + 1) * EW)):
                    i = V.tensor_tensor(ew_lo[0:parts, a:b], eraw[e][0:parts, a - e * EW:b - e * EW],
                                        ew_hi[0:parts, a:b].bitcast(F32), ALU.subtract)
                i.then_inc(w_lo, 1)
            dve.wait_ge(consts, 1)
            dve.wait_ge(vconsts, 1)

            list_steps = 0

            def note(ins):
                nonlocal list_steps
                list_steps += 1
                ins.then_inc(lists, 1)
                dve.wait_ge(lists, list_steps)

            def lists_in_use():
                NTOK, NLIST, UPTO, BASE = range(4)

                def by_group(row):
                    return em[:, row, :].rearrange("p (g q) -> p g q", g=4)
                lots = pick[:, :, :].rearrange("p g l -> p (g l)")[:, 0:E * ROWS]
                note(V.tensor_tensor(em[:, NTOK, :], filled[:, :], first_slot[:, :], ALU.subtract))
                note(V.tensor_tensor(lots.rearrange("p (e j) -> p e j", e=E),
                                     em[:, NTOK, :].unsqueeze(2).to_broadcast([P, E, ROWS]),
                                     list_start[:, :].unsqueeze(1).to_broadcast([P, E, ROWS]), ALU.is_gt))
                note(V.tensor_reduce(em[:, NLIST, :], lots.rearrange("p (e j) -> p e j", e=E), AX_X, ALU.add))
                note(V.tensor_tensor_scan(em[:, UPTO, :], ones_row[:, 0:E], em[:, NLIST, :], 0.0, ALU.mult, ALU.add))
                note(V.tensor_tensor(em[:, BASE, :], em[:, UPTO, :], em[:, NLIST, :], ALU.subtract))
                mask = quarter[:, :].unsqueeze(1).to_broadcast([P, 4, 4])
                V.tensor_tensor(by_group(4), by_group(BASE), mask, ALU.mult)
                note(V.tensor_tensor(by_group(5), by_group(NLIST), mask, ALU.mult))
                V.tensor_reduce(em[:, 6, 0:4], by_group(4), AX_X, ALU.add)
                note(V.tensor_reduce(em[:, 6, 4:8], by_group(5), AX_X, ALU.add))
                V.tensor_scalar(em[:, 7, 0:4], em[:, 6, 0:4], in_quarter[:, 0:1], 1.0, ALU.add, ALU.add)
                note(V.tensor_scalar(em[:, 7, 4:8], em[:, 6, 4:8], in_quarter[:, 0:1], None, ALU.is_gt))
                note(V.tensor_tensor(em[:, 7, 8:12], em[:, 7, 0:4], em[:, 7, 4:8], ALU.mult))
                note(V.tensor_scalar(em[:, 7, 12:16], em[:, 7, 8:12], -1.0, None, ALU.add))
                for g in range(4):
                    i = V.tensor_scalar(pick[:, g, :], list_no[:, :], em[:, 7, 12 + g:13 + g], None, ALU.is_equal)
                note(i)
                assert list_steps == PICKS_SET

            def lists_experts():
                of4 = scr[0:1, 1, 0:LISTS].rearrange("p (g j) -> p g j", j=GROUP)
                packed = ix[0:1, 3, 0:GROUPS]
                note(V.tensor_scalar(packed, of4[:, :, 3], float(E), None, ALU.mult))
                note(V.tensor_tensor(packed, packed, of4[:, :, 2], ALU.add))
                note(V.scalar_tensor_tensor(packed, packed, float(E), of4[:, :, 1], ALU.mult, ALU.add))
                note(V.scalar_tensor_tensor(packed, packed, float(E), of4[:, :, 0], ALU.mult, ALU.add))
                note(V.tensor_copy(whose[:, :], packed))

            def turn_(turn):
                def shared_products(*tiles):
                    if turn.shared:
                        for f in tiles:
                            product(turn, f"G{f}")

                if turn.shared:
                    split_lo(turn, "x")
                if turn.shared and not turn.front:
                    route_a(turn)
                    for f in range(ST):
                        shared_products(f)
                        if f == 0:
                            route_b(turn)
                        else:
                            lower_expert(f - 1)
                    lists_in_use()
                if turn.front:
                    for h, (part, to) in enumerate((("k", ksb), ("q", qsb))):
                        dve.wait_ge(*rms_done.at(turn, part))
                        if turn.kind == "first" and not h:
                            dve.wait_ge(*act_done.before(turn, "v"))
                        V.tensor_tensor(to[:, :, :], to[:, :, :], rms[:, h, :].unsqueeze(1).to_broadcast([P, KD, CHUNK]),
                                        ALU.mult).then_inc(*mid.did(turn, part + "r"))
                    dve.wait_ge(*rms_done.at(turn, "w"))
                    V.tensor_tensor(vsb[:, :, :], vsb[:, :, :], ksb[:, :, :], ALU.mult).then_inc(*mid.did(turn, "wv"))

                    def scans(to, of, end, name):
                        for k in range(KD):
                            for b in range(BATCH):
                                i = V.tensor_tensor_scan(to[:, k, b * RUN:(b + 1) * RUN], ones_row[:, :],
                                                         of[:, k, b * RUN:(b + 1) * RUN], end[:, k, b:b + 1], ALU.mult, ALU.add)
                        i.then_inc(*mid.did(turn, name))
                        dve.wait_ge(*mid.at(turn, name))
                        V.tensor_copy(end[:, :, :], to[:, :, :].rearrange("p k (b r) -> p k b r", b=BATCH)[:, :, :, RUN - 1]
                                      ).then_inc(*mid.did(turn, name[:-3] + "end"))
                    if turn.kind != "first":
                        dve.wait_ge(*mid.before(turn, "kvend"))
                    scans(wsum, ksb, wend, "wsum")
                    dve.wait_ge(*mid.at(turn, "wv"))
                    shared_products(0)
                    scans(kvsum, vsb, kvend, "kvsum")
                    shared_products(1, 2)
                    dve.wait_ge(*rms_done.at(turn, "eq"))
                    V.scalar_tensor_tensor(qsb[:, :, :], qsb[:, :, :], 1.0, wsum[:, :, :], ALU.add, ALU.mult
                                           ).then_inc(*mid.did(turn, "d"))
                    shared_products(3)
                    dve.wait_ge(*mid.at(turn, "d"))
                    V.reciprocal(ksb[:, 0, :], qsb[:, 0, :]).then_inc(*mid.did(turn, "rec0"))
                    shared_products(4, 5)
                    for k in range(KD):
                        if k:
                            V.reciprocal(ksb[:, k, :], qsb[:, k, :]).then_inc(*mid.did(turn, f"rec{k}"))
                        dve.wait_ge(*mid.at(turn, f"rec{k}"))
                        V.tensor_tensor(kvsum[:, k, :], kvsum[:, k, :], ksb[:, k, :], ALU.mult).then_inc(*mid.did(turn, f"y{k}"))
                    for k in range(KD):
                        dve.wait_ge(*rms_done.at(turn, f"yhi{k}"))
                        V.tensor_tensor(y_lo[:, k, :], kvsum[:, k, :], y_hi[:, k, :].bitcast(F32), ALU.subtract
                                        ).then_inc(*mid.did(turn, f"ylo{k}"))
                if turn.shared:
                    dve.wait_ge(*logit_out.at(turn, "tanh"))
                    V.tensor_scalar(sig[:, :], sig[:, :], 0.5, 0.5, ALU.mult, ALU.add).then_inc(*sig_done.did(turn, "half"))
                    dve.wait_ge(*sig_done.at(turn, "half"))
                    for d in range(2):
                        dve.wait_ge(*pair_full.at(turn, f"D{d}"))
                        for h in range(2):
                            t = 2 * d + h
                            i = V.scalar_tensor_tensor(x1[:, t, :], ring[:, slot_of(turn, f"D{d}"), h, 0:D], sig[:, t:t + 1],
                                                       x1[:, t, :], ALU.mult, ALU.add)
                        i.then_inc(*pair_done.did(turn, f"D{d}"))
                if turn.front and turn.next:
                    first_norm(turn, 0)
                if turn.front:
                    for f in range(FT):
                        product(turn, f"S{f}")
                        if turn.shared and f == 0:
                            route_a(turn)
                        if turn.shared and f == 3:
                            route_b(turn)
                        if turn.kind == "first" and f + 3 < len(PIECES):
                            lower_weights([f + 3])
                        if turn.next and f in (1, 2):
                            first_norm(turn, f)
                elif turn.next:
                    for part in range(3):
                        first_norm(turn, part)
                        lower_weights([part])
                if turn.next:
                    split_lo(turn, "b")
                if turn.front and turn.shared:
                    weigh(turn)
                if turn.front:
                    if turn.kind != "first":
                        dve.wait_ge(acc_out, (turn.t + 1) * 16 if turn.kind == "steady" else (CHUNKS - 1) * 16)
                    dve.wait_ge(*resid.before(turn, "res"))
                    for w in range(2):
                        dve.wait_ge(*pair_full.at(turn, f"W{w}"))
                        V.tensor_tensor(x1[:, 2 * w:2 * w + 2, :], res[:, 2 * w:2 * w + 2, :],
                                        ring[:, slot_of(turn, f"W{w}"), :, 0:D], ALU.add).then_inc(*pair_done.did(turn, f"W{w}"))
                        dve.wait_ge(*pair_done.at(turn, f"W{w}"))
                        for t in range(2 * w, 2 * w + 2):
                            i = V.bn_stats(st2[:, t, :], x1[:, t, :])
                    i.then_inc(*norm2.did(turn, "stats"))
                    apart(dve, norm2.at(turn, "stats"))
                    for t in range(TT):
                        i = V.bn_aggr(mv2[:, t, :], st2[:, t, :])
                    i.then_inc(*norm2.did(turn, "aggr"))
                    dve.wait_ge(*norm2.at(turn, "aggr"))
                    V.tensor_scalar(sc2[:, 0, :], mv2[:, :, 1], LN_EPS, None, ALU.add).then_inc(*norm2.did(turn, "ve"))
                    dve.wait_ge(*pows.at(turn, "n2"))
                    if turn.kind != "first":
                        dve.wait_ge(xn2_out, (turn.t + 1) * 16 if turn.kind == "steady" else (CHUNKS - 1) * 16)
                        dve.wait_ge(*pair_full.at(turn, "x"))
                    for t in range(TT):
                        i = V.tensor_scalar(xn2[:, t, :], x1[:, t, :], mv2[:, t, 0:1], sc2[:, 1, t:t + 1],
                                            ALU.subtract, ALU.mult)
                    i.then_inc(*norm2.did(turn, "xn2"))
                if turn.next:
                    def square_sum(part, of):
                        dve.wait_ge(*squares.at(turn, part))
                        V.tensor_tensor(of[:, 0, :], of[:, 0, :], of[:, 1, :], ALU.add).then_inc(*mid.did(turn, part + "sum"))

                    def lower_sum(part, of):
                        h = "kq".index(part)
                        dve.wait_ge(*sq_hi.at(turn, part))
                        V.tensor_tensor(y_lo[:, h, :], of[:, 0, :], y_hi[:, h, :].bitcast(F32), ALU.subtract
                                        ).then_inc(*mid.did(turn, part + "lo"))
                    square_sum("k", kvsum)
                    square_sum("q", wsum)
                    lower_sum("k", kvsum)
                    lower_sum("q", wsum)
            steps(dve, turn_)
            for e in range(ST - 1, SPLIT_FIRST):
                lower_expert(e)
            dve.wait_ge(lists_t, 1)
            note(V.tensor_scalar(ix[:, 1, :], scr[:, 0, 0:LISTS], 1.0, 0.0, ALU.subtract, ALU.max))
            V.scalar_tensor_tensor(ix[:, 2, :], scr[:, 0, 0:LISTS], 0.0, spare[:, :], ALU.is_equal, ALU.mult)
            V.memset(take[:, LISTS:LISTS + GROUP], 0)
            note(V.tensor_copy(take[:, 0:LISTS], ix[:, 1, :]))
            note(V.tensor_scalar(take[:, 0:LISTS], take[:, 0:LISTS], 2, None, ALU.logical_shift_right))
            note(V.scalar_tensor_tensor(put[:, :], scr[:, 0, 0:LISTS], -1.0, ix[:, 2, :], ALU.add, ALU.add))
            dve.wait_ge(acc_out, 16 * CHUNKS)
            for j in range(GROUP):
                V.tensor_copy(take_now[:, j:j + 1], take[:, j:j + 1]).then_inc(take_set[j], 1)
            lists_experts()
            assert list_steps == LISTS_SET
            for e in range(SPLIT_FIRST, E):
                lower_expert(e)

            def lower_rows(g, j):
                dve.wait_ge(*tile_done(xt_hi_done, g, j))
                V.tensor_tensor(xt_lo[:, j, :], ring[:, 0, j % 2, 0:D], xt_hi[:, j, :].bitcast(F32), ALU.subtract
                                ).then_inc(xt_lo_done[j], 1)
                dve.wait_ge(got[j], 16 * (g + 1))
                V.tensor_copy(take_now[:, j:j + 1], take[:, bass.ds((g + 1) * GROUP + j, 1)]).then_inc(take_set[j], 1)

            for j in range(GROUP):
                lower_rows(0, j)

            def group(g):
                for what, j in ORDER:
                    b = j % 2
                    if what == "up":
                        dve.wait_ge(*tile_done(silu_done, g, j))
                        free = tile_done(ht_full, g, j, 2)
                        if free:
                            dve.wait_ge(*free)
                        V.tensor_tensor(eh[:, b, :], eg[:, b, :], ring[:, 1, b, EI:2 * EI], ALU.mult).then_inc(h_done[j], 1)
                    elif what == "rows" and live_next(g):
                        lower_rows(g + 1, j)
                    elif what == "hidden":
                        dve.wait_ge(*tile_done(ht_hi_done, g, j))
                        V.tensor_tensor(ht_lo[0:EH, b, :], ring[0:EH, 2, b, 0:D], ht_hi[0:EH, b, :].bitcast(F32), ALU.subtract
                                        ).then_inc(ht_lo_done[j], 1)
                    elif what == "down":
                        if not isinstance(g, int) or g:
                            dve.wait_ge(sent[j], 16 * g)
                        V.tensor_copy(put_now[:, j:j + 1], put[:, bass.ds(g * GROUP + j, 1)]).then_inc(put_set[j], 1)
            groups(dve, group)

            weigh(Turn("last"))

            for j in range(GROUP):
                dve.wait_ge(h_done[j], GROUPS)
                dve.wait_ge(ht_lo_done[j], GROUPS)
                dve.wait_ge(sent[j], 16 * GROUPS)

            def sum_pair(t, q):
                before = t * (JOINS // 2 * TOPK) + q * TOPK
                for u in (2 * q, 2 * q + 1):
                    dve.wait_ge(z_in[u], t * 32 + 32)
                    if t:
                        dve.wait_ge(o_out[u], t * 16)
                for k in range(TOPK):
                    if k:
                        dve.wait_ge(summed, before + k)
                    for u in (2 * q, 2 * q + 1):
                        i = V.scalar_tensor_tensor(sums[:, u, :], zin[:, u, k * D:(k + 1) * D],
                                                   share[:, t * JOINS + u, k:k + 1],
                                                   sums[:, u, :] if k else ain[:, u, :], ALU.mult, ALU.add)
                    i.then_inc(summed, 1)
            for t in range(TILES // JOINS):
                for q in range(JOINS // 2):
                    sum_pair(t, q)

        @block.gpsimd
        def _(pool):
            G = nc.gpsimd
            gchain = sem("gchain")
            n = 0

            def link(ins):
                nonlocal n
                n += 1
                ins.then_inc(gchain, 1)
                pool.wait_ge(gchain, n)
            link(G.memset(ident[:, :], 0.0))
            link(G.affine_select(out=ident[:, :], in_=ident[:, :], compare_op=ALU.not_equal, fill=1.0, base=0,
                                 pattern=[[-1, P]], channel_multiplier=1))
            link(G.memset(notfirst[:, :], 1.0))
            nf = notfirst[:, :].rearrange("p (t e) -> p t e", t=TT)
            link(G.memset(nf[:, :, 0:1], 0.0))
            link(G.iota(filled[:, :], pattern=[[TOKENS, E]], base=0, channel_multiplier=0,
                        allow_small_or_imprecise_dtypes=True))
            link(G.iota(idval[:, :], pattern=[[TOPK * P, TT], [1, TOPK]], base=1 - TOPK * CHUNK, channel_multiplier=TOPK,
                        allow_small_or_imprecise_dtypes=True))
            link(G.iota(first_slot[:, :], pattern=[[TOKENS, E]], base=0, channel_multiplier=0,
                        allow_small_or_imprecise_dtypes=True))
            link(G.iota(list_start[:, :], pattern=[[P, ROWS]], base=0, channel_multiplier=0, allow_small_or_imprecise_dtypes=True))
            link(G.iota(list_no[:, :], pattern=[[1, LISTS]], base=0, channel_multiplier=0, allow_small_or_imprecise_dtypes=True))
            link(G.iota(spare[:, :], pattern=[[P, LISTS]], base=PICKED + 1, channel_multiplier=1,
                        allow_small_or_imprecise_dtypes=True))
            link(G.memset(quarter[:, :], 0.0))
            for q in range(4):
                link(G.memset(quarter[32 * q:32 * q + 32, q:q + 1], 1.0))
                link(G.iota(row_expert[32 * q:32 * q + 32, :], pattern=[[4, 4]], base=q, channel_multiplier=0,
                            allow_small_or_imprecise_dtypes=True))
                link(G.iota(in_quarter[32 * q:32 * q + 32, :], pattern=[[0, 1]], base=0, channel_multiplier=1,
                            allow_small_or_imprecise_dtypes=True))
            link(G.memset(earlier[:, :], 1.0))
            G.affine_select(out=earlier[:, :], in_=earlier[:, :], compare_op=ALU.is_gt, fill=0.0, base=0,
                            pattern=[[1, P]], channel_multiplier=-1).then_inc(consts, 1)
            link(G.memset(hid[:, 0, :], 0.0))
            pool.dma_start(ids.rearrange("(p n) o -> p (n o)", p=P), hid[:, 0, :]).then_inc(id_out, 16)
            pool.wait_ge(vconsts, 1)

            def turn_(turn):
                def lower(event):
                    f = int(event[1:])
                    pool.wait_ge(*hid_top.at(turn, event))
                    G.tensor_tensor(hid_lo[:, f, :], hid[:, silu.events[turn.kind].index(event) % 2, :],
                                    hid_hi[:, f, :].bitcast(F32), ALU.subtract).then_inc(*hid_low.did(turn, event))
                if turn.kind == "pre":
                    power_a(turn)
                    power_b(turn)
                if turn.shared:
                    for f in range(ST):
                        lower(f"G{f}")
                        if not turn.front and f >= 1:
                            if f == 1:
                                apart(pool, routed.at(turn, "id"))
                            scatter(f - 1, f)
                if turn.front:
                    if turn.next:
                        power_a(turn)
                    for f in range(FT):
                        lower(f"S{f}")
                        if turn.next and f == 1:
                            power_b(turn)
                        if turn.shared and f == 6:
                            apart(pool, routed.at(turn, "id"))
                            scatter(0, 1)
                    if turn.shared:
                        scatter(1, 9)
                    pool.wait_ge(*norm2.at(turn, "ve"))
                    G.tensor_tensor(sc2[:, 1, :], sc2[:, 0, :], power[:, :], ALU.pow).then_inc(*pows.did(turn, "n2"))
                    if turn.shared:
                        scatter(9, TT * TOPK)
                elif turn.shared:
                    scatter(ST - 1, TT * TOPK)
                if turn.next:
                    residual(turn)

            def power_a(turn):
                pool.wait_ge(*norm1.at(turn, "ve"))
                G.tensor_tensor(sc1[:, 1, :], sc1[:, 0, :], power[:, :], ALU.pow).then_inc(*pows.did(turn, "n1a"))

            def power_b(turn):
                pool.wait_ge(*norm1.at(turn, "ue"))
                G.tensor_tensor(sc1[:, 5, :], sc1[:, 4, :], power[:, :], ALU.pow).then_inc(*pows.did(turn, "n1b"))

            def residual(turn):
                apart(pool, norm1.at(turn, "b"), *([pair_done.at(turn, "W1")] if turn.front else []))
                G.tensor_scalar(sc1[:, 7, :], sc1[:, 1, :], 1.0, 1.0, ALU.mult, ALU.add).then_inc(*resid.did(turn, "rp"))
                G.tensor_tensor(sc1[:, 2, :], mv1[:, :, 0], sc1[:, 1, :], ALU.mult).then_inc(*resid.did(turn, "nm"))
                apart(pool, resid.at(turn, "nm"))
                for t in range(TT):
                    i = G.tensor_scalar(res[:, t, :], xin[:, t, :], sc1[:, 7, t:t + 1], sc1[:, 2, t:t + 1],
                                        ALU.mult, ALU.subtract)
                i.then_inc(*resid.did(turn, "res"))

            def scatter(a, b):
                for i in range(a, b):
                    G.indirect_dma_start(out=ids, out_offset=bass.IndirectOffsetOnAxis(ap=slot_u[:, i:i + 1], axis=0),
                                         in_=idval[:, i:i + 1], in_offset=None).then_inc(id_out, 16)
            steps(pool, turn_)

            def gather(g, j):
                if isinstance(g, int) and g == 0:
                    pool.wait_ge(take_set[j], 1)
                else:
                    apart(pool, (take_set[j], g + 1), (xt_full[j], g))
                G.indirect_dma_start(out=xg[:, j, :], out_offset=None, in_=xn2_rows,
                                     in_offset=bass.IndirectOffsetOnAxis(ap=take_now[:, j:j + 1], axis=0)).then_inc(got[j], 16)

            def send(g, j):
                apart(pool, tile_done(put_set, g, j), tile_done(y_done, g, j))
                G.indirect_dma_start(out=picked, out_offset=bass.IndirectOffsetOnAxis(ap=put_now[:, j:j + 1], axis=0),
                                     in_=ysb[:, j, :], in_offset=None).then_inc(sent[j], 16)

            def group(g):
                for what, j in ORDER:
                    if what == "rows" and (not isinstance(g, int) or g < GROUPS - 2):
                        gather(g + 2, j)
                    elif what == "down":
                        send(g, j)
            pool.wait_ge(xn2_out, 16 * CHUNKS)
            for j in range(GROUP):
                gather(0, j)
            pool.wait_ge(acc_out, 16 * CHUNKS)
            G.memset(ht_hi[64:EHP, :, :].bitcast(F32), 0.0).then_inc(pad_rows, 1)
            G.memset(ht_lo[64:EHP, :, :].bitcast(F32), 0.0).then_inc(pad_rows, 1)
            for j in range(GROUP):
                gather(1, j)
            group(0)
            with pool.Fori(0, GROUPS - 3) as t:
                group(t + 1)
            group(GROUPS - 2)
            group(GROUPS - 1)

        for s in (pair_full, scr_full, pair_done, act_done, norm1, norm2, mid, routed, sig_done, squares, sq_hi, shares, x_top,
                  feat_top, logit_out, rms_done, silu, hid_top, hid_low, pows, resid):
            s.check()


def kernel(**inputs):
    import numpy as np
    import concourse.bacc as bacc
    from concourse.bass_utils import run_bass_kernel_spmd

    def by_rows(w):
        k = w.shape[0] // P
        return w.reshape(k, P, -1).transpose(1, 0, 2).reshape(P, -1)

    get = {name: np.asarray(a) for name, a in inputs.items()}
    x = get["L0_attn_x"].reshape(BATCH, CHUNKS, RUN, D).transpose(1, 0, 2, 3).reshape(TOKENS, D)
    router = np.zeros((D, RW), np.float32)
    router[:, 0:E] = get["L0_ffn_gate_w"].T
    router[:, E] = get["L0_ffn_shared_gate_vec"][0]
    s_up = np.zeros((D, 2, SIP), np.float32)
    s_up[:, :, 0:SI] = get["L0_ffn_shared_gate_up"].T.reshape(D, 2, SI)
    s_down = np.zeros((SIP, D), np.float32)
    s_down[0:SI] = get["L0_ffn_shared_down"].T
    w1 = np.concatenate([by_rows(w) for w in (get["L0_attn_w_qkv"].T, get["L0_attn_w_swiglu"].T, get["L0_attn_w_out"].T, router,
                                              s_up.reshape(D, 2 * SIP), s_down)], axis=1)
    w_up = get["L0_ffn_expert_gate_up"].transpose(0, 2, 1).reshape(E, KD, P, 2 * EI).transpose(0, 2, 1, 3).reshape(E, P, EU)
    w_down = np.zeros((E, EHP, 2, D), np.float32)
    w_down[:, 0:EH] = get["L0_ffn_expert_down"].transpose(0, 2, 1).reshape(E, 2, EH, D).transpose(0, 2, 1, 3)
    arrays = {name: np.ascontiguousarray(a) for name, a in
              {"x": x, "w1": w1, "w_up": w_up, "w_down": w_down.reshape(E, EHP, 2 * D)}.items()}
    nc = bacc.Bacc("TRN2", target_bir_lowering=False, num_devices=1)
    ins = [nc.dram_tensor(name, a.shape, F32, kind="ExternalInput").ap() for name, a in arrays.items()]
    out = nc.dram_tensor("out", (TOKENS, D), F32, kind="ExternalOutput").ap()
    scratch = [nc.dram_tensor(name, shape, F32, kind="Internal").ap() for name, shape in
               (("xn2_rows", (TOKENS, D)), ("acc", (TOKENS, D)), ("ids", (E * TOKENS, 1)), ("picked", (PICKED + LISTS * P, D)))]
    build(nc, *ins, out, *scratch)
    got = run_bass_kernel_spmd(nc, [arrays], core_ids=[0]).results[0]["out"]
    return got.reshape(CHUNKS, BATCH, RUN, D).transpose(1, 0, 2, 3).reshape(BATCH, SEQ, D)
```
